# Optimizing a Trainium2 kernel written in Bass

```python
import numpy as np
import jax
import jax.numpy as jnp

def _softmax(x, axis=-1):
    return jax.nn.softmax(x, axis=axis)

def _gelu(x):
    return jax.nn.gelu(x, approximate=True)

def _silu(x):
    return jax.nn.silu(x)

def _sigmoid(x):
    return jax.nn.sigmoid(x)

def _layernorm(x, axis=-1, eps=1e-05):
    m = jnp.mean(x, axis=axis, keepdims=True)
    v = jnp.var(x, axis=axis, keepdims=True)
    return (x - m) / jnp.sqrt(v + eps)

def _scatter_add(tgt, idx, src, axis=0):
    return tgt.at[idx].add(src)

def _segment_sum(src, seg, n):
    return jax.ops.segment_sum(src, seg, n)
kernel_name = 'mk_decoder_preln_d4_seqx_r8_54ed21'

def setup_inputs(seed: int=0):
    np.random.seed(seed)
    _w = jnp.asarray

    def _rec_inputs():
        import jax
        import jax.numpy as jnp
        _rk = jax.random.key(seed)
        x = 7.22e-05 + 1 * jax.random.normal(jax.random.fold_in(_rk, 1), (4, 256, 256), jnp.float32)
        _lenS = 256 - jax.random.randint(jax.random.fold_in(_rk, 7), (4,), 0, max(1, 256 // 4) + 1, jnp.int32)
        _lenS2 = 256 - jax.random.randint(jax.random.fold_in(_rk, 8), (4,), 0, max(1, 256 // 4) + 1, jnp.int32)
        _ctx_2048P = jax.random.normal(jax.random.fold_in(_rk, 11), (4, 16, 256), jnp.float32)
        _ctx_2048c = jax.random.dirichlet(jax.random.fold_in(_rk, 511), 0.3 * jnp.ones((16,), jnp.float32), (4, 256))
        _ctx_2048t = jnp.einsum('bsk,bkd->bsd', _ctx_2048c, _ctx_2048P)
        _ctx_2048t = _ctx_2048t * jax.lax.rsqrt(jnp.mean(jnp.square(_ctx_2048t)) + 1e-12) * 0.953939
        ctx_2048 = 4.13588e-05 + 0.999923 * (_ctx_2048t + 0.3 * jax.random.normal(jax.random.fold_in(_rk, 611), (4, 256, 256), jnp.float32))
        return (x, ctx_2048)
    x, ctx_2048 = _rec_inputs()

    def _L0_attn_setup():
        import jax, jax.numpy as jnp
        import numpy as np
        B, T, C = (2, 256, 256)
        NH, NKV, HD = (16, 8, 32)
        SOFTCAP = 50.0
        ROPE_BASE = 10000.0

        def _rotate_half(x):
            x1, x2 = (x[..., :x.shape[-1] // 2], x[..., x.shape[-1] // 2:])
            return jnp.concatenate((-x2, x1), axis=-1)

        def _rope_cos_sin(t, head_dim, dtype):
            inv_freq = 1.0 / ROPE_BASE ** (jnp.arange(0, head_dim, 2, dtype=jnp.int32).astype(jnp.float32) / head_dim)
            pos = jnp.arange(t, dtype=jnp.float32)
            freqs = pos[:, None] * inv_freq[None, :]
            emb = jnp.concatenate((freqs, freqs), axis=-1)
            return (jnp.cos(emb).astype(dtype)[None, None], jnp.sin(emb).astype(dtype)[None, None])
        key = jax.random.key(seed)
        ks = jax.random.split(key, 5)
        s = 0.02
        return {'X': jax.random.normal(ks[0], (B, T, C), dtype=jnp.float32), 'Wq': jax.random.normal(ks[1], (C, NH * HD), dtype=jnp.float32) * s, 'Wk': jax.random.normal(ks[2], (C, NKV * HD), dtype=jnp.float32) * s, 'Wv': jax.random.normal(ks[3], (C, NKV * HD), dtype=jnp.float32) * s, 'Wo': jax.random.normal(ks[4], (NH * HD, C), dtype=jnp.float32) * s}
    _L0_attn_all = _L0_attn_setup()
    _L0_attn_in = {k: v for k, v in _L0_attn_all.items() if k in ('Wq', 'Wk', 'Wv', 'Wo')}
    del _L0_attn_all

    def _L0_xattn_setup():
        import jax, jax.numpy as jnp
        import numpy as np
        N_HEAD = 8
        key = jax.random.key(seed)
        k1, k2, k3 = jax.random.split(key, 3)
        b, d, m = (4, 128, 256)
        c, n = (128, 256)
        q = jax.random.normal(k1, (b, d, m), dtype=jnp.float32)
        k = jax.random.normal(k2, (d // d * b, d, n), dtype=jnp.float32).reshape(b, d, n)
        v = jax.random.normal(k3, (b, c, n), dtype=jnp.float32)
        return {'q': q, 'k': k, 'v': v}
    _L0_xattn_all = _L0_xattn_setup()
    _L0_xattn_in = {k: v for k, v in _L0_xattn_all.items() if k in ()}
    del _L0_xattn_all

    def _L0_ffn_setup():
        import jax, jax.numpy as jnp
        import numpy as np
        BLOCK_SIZE = 32
        FP4_GRID = jnp.array([0.0, 0.5, 1.0, 1.5, 2.0, 3.0, 4.0, 6.0], dtype=jnp.float32)
        FP4_MIDS = jnp.array([0.25, 0.75, 1.25, 1.75, 2.5, 3.5, 5.0], dtype=jnp.float32)

        def quantize_to_mxfp4(w, block_size=BLOCK_SIZE):
            K, N = w.shape
            wb = w.reshape(K // block_size, block_size, N)
            amax = jnp.max(jnp.abs(wb), axis=1, keepdims=True)
            exp = jnp.floor(jnp.log2(jnp.maximum(amax, 1e-30))) - 2.0
            scales = jnp.exp2(exp)
            x = wb / scales
            idx = jnp.digitize(jnp.abs(x), FP4_MIDS)
            q = jnp.sign(x) * FP4_GRID[idx]
            return (q, scales)

        def mxfp4_matmul(inputs, q, scales, block_size=BLOCK_SIZE):
            K = inputs.shape[-1]
            N = q.shape[-1]
            w = (q * scales).reshape(K, N)
            return inputs @ w
        key = jax.random.key(seed)
        ks = jax.random.split(key, 3)
        B, S, D, F = (4, 256, 256, 1024)
        inputs = jax.random.normal(ks[0], (B, S, D), dtype=jnp.float32)
        up_kernel = jax.random.normal(ks[1], (D, F), dtype=jnp.float32) * (1.0 / np.sqrt(D))
        down_kernel = jax.random.normal(ks[2], (F, D), dtype=jnp.float32) * (1.0 / np.sqrt(F))
        up_bias = jnp.zeros((F,), dtype=jnp.float32)
        down_bias = jnp.zeros((D,), dtype=jnp.float32)
        return {'inputs': inputs, 'up_kernel': up_kernel, 'up_bias': up_bias, 'down_kernel': down_kernel, 'down_bias': down_bias}
    _L0_ffn_all = _L0_ffn_setup()
    _L0_ffn_in = {k: v for k, v in _L0_ffn_all.items() if k in ('up_kernel', 'up_bias', 'down_kernel', 'down_bias')}
    del _L0_ffn_all

    def _L1_attn_setup():
        import jax, jax.numpy as jnp
        import numpy as np
        DIM = 256
        B, T = (8, 256)

        def _layernorm(x, g, b, eps=1e-05):
            m = jnp.mean(x, axis=-1, keepdims=True)
            v = jnp.mean(jnp.square(x - m), axis=-1, keepdims=True)
            return (x - m) / jnp.sqrt(v + eps) * g + b

        def _shift(x):
            return jnp.pad(x[:, :-1, :], ((0, 0), (1, 0), (0, 0)))
        key = jax.random.key(seed)
        ks = jax.random.split(key, 16)
        d = DIM
        s = 0.02
        inp = {'x': jax.random.normal(ks[0], (B, T, d), dtype=jnp.float32), 'ln1_g': jnp.ones((d,), jnp.float32), 'ln1_b': jnp.zeros((d,), jnp.float32), 'ln2_g': jnp.ones((d,), jnp.float32), 'ln2_b': jnp.zeros((d,), jnp.float32), 'tm_w': jnp.zeros((d,), jnp.float32), 'tm_u': jnp.zeros((d,), jnp.float32), 'tm_mu_r': jax.random.uniform(ks[1], (d,), jnp.float32), 'tm_mu_k': jax.random.uniform(ks[2], (d,), jnp.float32), 'tm_mu_v': jax.random.uniform(ks[3], (d,), jnp.float32), 'tm_Wr': jax.random.normal(ks[4], (d, d), jnp.float32) * s, 'tm_Wk': jax.random.normal(ks[5], (d, d), jnp.float32) * s, 'tm_Wv': jax.random.normal(ks[6], (d, d), jnp.float32) * s, 'tm_Wout': jax.random.normal(ks[7], (d, d), jnp.float32) * s, 'cm_mu_r': jax.random.uniform(ks[8], (d,), jnp.float32), 'cm_mu_k': jax.random.uniform(ks[9], (d,), jnp.float32), 'cm_Wr': jax.random.normal(ks[10], (d, d), jnp.float32) * s, 'cm_Wk': jax.random.normal(ks[11], (d, d), jnp.float32) * s, 'cm_Wv': jax.random.normal(ks[12], (d, d), jnp.float32) * s}
        return inp
    _L1_attn_all = _L1_attn_setup()
    _L1_attn_in = {k: v for k, v in _L1_attn_all.items() if k in ('ln1_g', 'ln1_b', 'ln2_g', 'ln2_b', 'tm_w', 'tm_u', 'tm_mu_r', 'tm_mu_k', 'tm_mu_v', 'tm_Wr', 'tm_Wk', 'tm_Wv', 'tm_Wout', 'cm_mu_r', 'cm_mu_k', 'cm_Wr', 'cm_Wk', 'cm_Wv')}
    del _L1_attn_all

    def _L1_xattn_setup():
        import jax, jax.numpy as jnp
        import numpy as np
        N_HEAD = 8
        key = jax.random.key(seed)
        k1, k2, k3 = jax.random.split(key, 3)
        B, D, L = (4, 128, 256)
        q = jax.random.normal(k1, (B, D, L), dtype=jnp.float32)
        k = jax.random.normal(k2, (B, D, L), dtype=jnp.float32)
        v = jax.random.normal(k3, (B, D, L), dtype=jnp.float32)
        gamma = jnp.ones((), dtype=jnp.float32)
        return {'q': q, 'k': k, 'v': v, 'gamma': gamma}
    _L1_xattn_all = _L1_xattn_setup()
    _L1_xattn_in = {k: v for k, v in _L1_xattn_all.items() if k in ('gamma',)}
    del _L1_xattn_all

    def _L1_ffn_setup():
        import jax, jax.numpy as jnp
        import numpy as np
        COST_LAMBDA = 1e-07
        HID = [128, 256, 384, 512, 128, 256, 384, 512]
        TOP_K = 2

        def _gelu(v):
            return jax.nn.gelu(v, approximate=False)

        def _forward(x, down_w, down_b, up_w, up_b, router_w, router_b, shared_w1, shared_b1, shared_w2, shared_b2, core_w, core_b, expert_params):
            E = len(expert_params)
            h = x @ down_w + down_b
            cost = jnp.array([w1.shape[0] * w1.shape[1] + w2.shape[0] * w2.shape[1] for w1, _, w2, _ in expert_params], jnp.float32)
            logits = x @ router_w + router_b - COST_LAMBDA * cost
            probs = jax.nn.softmax(logits, axis=-1)
            topv, topi = jax.lax.top_k(probs, TOP_K)
            gate = jax.nn.softmax(topv, axis=-1)
            out = jnp.zeros_like(h)
            for k in range(TOP_K):
                mask = jax.nn.one_hot(topi[..., k], E, dtype=h.dtype)
                acc = jnp.zeros_like(h)
                for e, (w1, b1, w2, b2) in enumerate(expert_params):
                    hm = h * mask[..., e:e + 1]
                    acc = acc + (_gelu(_gelu(hm) @ w1 + b1) @ w2 + b2)
                out = out + acc * gate[..., k:k + 1]
            out = out + 0.1 * (_gelu(_gelu(h) @ shared_w1 + shared_b1) @ shared_w2 + shared_b2)
            out = out @ up_w + up_b
            out = out + (_gelu(x) @ core_w + core_b)
            return out
        key = jax.random.key(seed)
        ks = iter(jax.random.split(key, 80))

        def W(shape):
            return jax.random.normal(next(ks), shape, jnp.float32) * 0.02
        B, T, D, L = (4, 256, 256, 128)
        inp = {'x': jax.random.normal(next(ks), (B, T, D), jnp.float32)}
        inp['down_w'] = W((D, L))
        inp['down_b'] = jnp.zeros((L,), jnp.float32)
        inp['up_w'] = W((L, D))
        inp['up_b'] = jnp.zeros((D,), jnp.float32)
        inp['router_w'] = W((D, len(HID)))
        inp['router_b'] = jnp.zeros((len(HID),), jnp.float32)
        inp['shared_w1'] = W((L, L))
        inp['shared_b1'] = jnp.zeros((L,), jnp.float32)
        inp['shared_w2'] = W((L, L))
        inp['shared_b2'] = jnp.zeros((L,), jnp.float32)
        inp['core_w'] = W((D, D))
        inp['core_b'] = jnp.zeros((D,), jnp.float32)
        for e, h in enumerate(HID):
            inp[f'e{e}_w1'] = W((L, h))
            inp[f'e{e}_b1'] = jnp.zeros((h,), jnp.float32)
            inp[f'e{e}_w2'] = W((h, L))
            inp[f'e{e}_b2'] = jnp.zeros((L,), jnp.float32)
        return inp
    _L1_ffn_all = _L1_ffn_setup()
    _L1_ffn_in = {k: v for k, v in _L1_ffn_all.items() if k in ('down_w', 'down_b', 'up_w', 'up_b', 'router_w', 'router_b', 'shared_w1', 'shared_b1', 'shared_w2', 'shared_b2', 'core_w', 'core_b', 'e0_w1', 'e0_b1', 'e0_w2', 'e0_b2', 'e1_w1', 'e1_b1', 'e1_w2', 'e1_b2', 'e2_w1', 'e2_b1', 'e2_w2', 'e2_b2', 'e3_w1', 'e3_b1', 'e3_w2', 'e3_b2', 'e4_w1', 'e4_b1', 'e4_w2', 'e4_b2', 'e5_w1', 'e5_b1', 'e5_w2', 'e5_b2', 'e6_w1', 'e6_b1', 'e6_w2', 'e6_b2', 'e7_w1', 'e7_b1', 'e7_w2', 'e7_b2')}
    del _L1_ffn_all

    def _L2_attn_setup():
        import jax, jax.numpy as jnp
        import numpy as np
        DIM = 256
        N_HEADS = 32
        N_KV_HEADS = 8
        HEAD_DIM = DIM // N_HEADS
        ROPE_BASE = 10000.0
        BATCH = 2
        SEQ = 256

        def _rope_cos_sin(seq_len, dtype=jnp.float32):
            inv_freq = 1.0 / ROPE_BASE ** (jnp.arange(0, HEAD_DIM, 2, dtype=jnp.float32) / HEAD_DIM)
            pos = jnp.arange(seq_len, dtype=jnp.float32)
            freqs = pos[:, None] * inv_freq[None, :]
            return (jnp.cos(freqs).astype(dtype), jnp.sin(freqs).astype(dtype))

        def _apply_rope(x, cos, sin):
            cos = cos[None, None, :, :]
            sin = sin[None, None, :, :]
            x_even = x[..., ::2]
            x_odd = x[..., 1::2]
            rot_even = x_even * cos - x_odd * sin
            rot_odd = x_even * sin + x_odd * cos
            out = jnp.stack((rot_even, rot_odd), axis=-1)
            return out.reshape(x.shape)
        key = jax.random.key(seed)
        ks = jax.random.split(key, 5)
        s = 0.02
        return {'x': jax.random.normal(ks[0], (BATCH, SEQ, DIM), dtype=jnp.float32), 'wq': jax.random.normal(ks[1], (DIM, N_HEADS * HEAD_DIM), dtype=jnp.float32) * s, 'wk': jax.random.normal(ks[2], (DIM, N_KV_HEADS * HEAD_DIM), dtype=jnp.float32) * s, 'wv': jax.random.normal(ks[3], (DIM, N_KV_HEADS * HEAD_DIM), dtype=jnp.float32) * s, 'wo': jax.random.normal(ks[4], (DIM, DIM), dtype=jnp.float32) * s}
    _L2_attn_all = _L2_attn_setup()
    _L2_attn_in = {k: v for k, v in _L2_attn_all.items() if k in ('wq', 'wk', 'wv', 'wo')}
    del _L2_attn_all

    def _L2_xattn_setup():
        import math
        import jax, jax.numpy as jnp
        import numpy as np
        N_HEADS = 16
        key = jax.random.key(seed)
        k1, k2 = jax.random.split(key)
        qkv = jax.random.normal(k1, (2, 128, 256), dtype=jnp.float32)
        y = jax.random.normal(k2, (2, 128, 256), dtype=jnp.float32)
        return {'qkv': qkv, 'y': y}
    _L2_xattn_all = _L2_xattn_setup()
    _L2_xattn_in = {k: v for k, v in _L2_xattn_all.items() if k in ()}
    del _L2_xattn_all

    def _L2_ffn_setup():
        import jax, jax.numpy as jnp
        import numpy as np
        B, S, H = (2, 256, 256)
        E, K = (16, 4)
        I_MOE, I_SH = (176, 704)
        key = jax.random.key(seed)
        ks = jax.random.split(key, 9)

        def w(k, shape, fan_in):
            return jax.random.normal(k, shape, jnp.float32) * fan_in ** (-0.5)
        return {'hidden_states': jax.random.normal(ks[0], (B, S, H), jnp.float32), 'router_w': w(ks[1], (E, H), H), 'w_gate': w(ks[2], (E, H, I_MOE), H), 'w_up': w(ks[3], (E, H, I_MOE), H), 'w_down': w(ks[4], (E, I_MOE, H), I_MOE), 'sh_gate': w(ks[5], (H, I_SH), H), 'sh_up': w(ks[6], (H, I_SH), H), 'sh_down': w(ks[7], (I_SH, H), I_SH), 'sh_gate_w': w(ks[8], (H, 1), H)}
    _L2_ffn_all = _L2_ffn_setup()
    _L2_ffn_in = {k: v for k, v in _L2_ffn_all.items() if k in ('router_w', 'w_gate', 'w_up', 'w_down', 'sh_gate', 'sh_up', 'sh_down', 'sh_gate_w')}
    del _L2_ffn_all

    def _L3_attn_setup():
        import jax, jax.numpy as jnp
        import numpy as np
        B, T, D = (2, 256, 256)
        QH, KVH = (16, 4)
        HD = D // QH

        def rotate_half(x):
            d = x.shape[-1] // 2
            return jnp.concatenate([-x[..., d:], x[..., :d]], axis=-1)

        def rope_tables(head_dim, seq_len, theta=10000.0):
            freqs = 1.0 / theta ** (jnp.arange(0, head_dim, 2, dtype=jnp.float32) / head_dim)
            t = jnp.arange(seq_len, dtype=jnp.float32)
            ang = t[:, None] * freqs[None, :]
            cos = jnp.tile(jnp.cos(ang), (1, 2))
            sin = jnp.tile(jnp.sin(ang), (1, 2))
            return (cos, sin)

        def apply_rope(x, cos, sin):
            c = cos[None, None, :, :]
            s = sin[None, None, :, :]
            return x * c + rotate_half(x) * s
        key = jax.random.key(seed)
        kx, kq, kk, kv, ko = jax.random.split(key, 5)
        scale = D ** (-0.5)
        return {'x': jax.random.normal(kx, (B, T, D), dtype=jnp.float32), 'wq': jax.random.normal(kq, (D, D), dtype=jnp.float32) * scale, 'wk': jax.random.normal(kk, (D, KVH * HD), dtype=jnp.float32) * scale, 'wv': jax.random.normal(kv, (D, KVH * HD), dtype=jnp.float32) * scale, 'wo': jax.random.normal(ko, (D, D), dtype=jnp.float32) * scale}
    _L3_attn_all = _L3_attn_setup()
    _L3_attn_in = {k: v for k, v in _L3_attn_all.items() if k in ('wq', 'wk', 'wv', 'wo')}
    del _L3_attn_all

    def _L3_xattn_setup():
        import jax, jax.numpy as jnp
        import numpy as np
        B_DIM, T_DIM, C_DIM = (16, 128, 256)

        def _wkv(w, u, k, v):
            Bn, Tn, Cn = k.shape
            NEG_INF = jnp.float32(-1e+38)

            def step(carry, kv_t):
                p, q, o = carry
                kt, vt = kv_t
                no = jnp.maximum(o, u + kt)
                A = jnp.exp(o - no)
                E = jnp.exp(u + kt - no)
                y = (A * p + E * vt) / (A * q + E)
                no2 = jnp.maximum(w + o, kt)
                A2 = jnp.exp(w + o - no2)
                E2 = jnp.exp(kt - no2)
                return ((A2 * p + E2 * vt, A2 * q + E2, no2), y)
            init = (jnp.zeros((Bn, Cn), k.dtype), jnp.zeros((Bn, Cn), k.dtype), jnp.full((Bn, Cn), NEG_INF, k.dtype))
            kT = jnp.moveaxis(k, 1, 0)
            vT = jnp.moveaxis(v, 1, 0)
            _, yT = jax.lax.scan(step, init, (kT, vT))
            return jnp.moveaxis(yT, 0, 1)
        key = jax.random.key(seed)
        k1, k2, k3, k4 = jax.random.split(key, 4)
        w = -jnp.exp(jax.random.normal(k1, (C_DIM,), jnp.float32))
        u = jax.random.normal(k2, (C_DIM,), jnp.float32)
        k = jax.random.normal(k3, (B_DIM, T_DIM, C_DIM), jnp.float32)
        v = jax.random.normal(k4, (B_DIM, T_DIM, C_DIM), jnp.float32)
        return {'B': B_DIM, 'T': T_DIM, 'C': C_DIM, 'w': w, 'u': u, 'k': k, 'v': v}
    _L3_xattn_all = _L3_xattn_setup()
    _L3_xattn_in = {k: v for k, v in _L3_xattn_all.items() if k in ('w', 'u')}
    del _L3_xattn_all

    def _L3_ffn_setup():
        import jax, jax.numpy as jnp
        import numpy as np
        D_MODEL = 256
        D_EXPERT = 1024
        EPS = 1e-08

        def ternary_quant(w):
            scale = jnp.mean(jnp.abs(w)) + EPS
            q = jnp.clip(jnp.round(w / scale), -1.0, 1.0) * scale
            return w + jax.lax.stop_gradient(q - w)
        key = jax.random.key(seed)
        k_x, k_up, k_gate, k_down = jax.random.split(key, 4)
        std_in = 1.0 / np.sqrt(D_MODEL)
        std_exp = 1.0 / np.sqrt(D_EXPERT)
        return {'x': jax.random.normal(k_x, (4, 256, D_MODEL), dtype=jnp.float32), 'W_up': jax.random.normal(k_up, (D_EXPERT, D_MODEL), dtype=jnp.float32) * std_in, 'W_gate': jax.random.normal(k_gate, (D_EXPERT, D_MODEL), dtype=jnp.float32) * std_in, 'W_down': jax.random.normal(k_down, (D_MODEL, D_EXPERT), dtype=jnp.float32) * std_exp}
    _L3_ffn_all = _L3_ffn_setup()
    _L3_ffn_in = {k: v for k, v in _L3_ffn_all.items() if k in ('W_up', 'W_gate', 'W_down')}
    del _L3_ffn_all
    return {'x': x, 'ctx_2048': ctx_2048, 'L0_attn_Wq': _L0_attn_in['Wq'], 'L0_attn_Wk': _L0_attn_in['Wk'], 'L0_attn_Wv': _L0_attn_in['Wv'], 'L0_attn_Wo': _L0_attn_in['Wo'], 'L0_ffn_up_kernel': _L0_ffn_in['up_kernel'], 'L0_ffn_up_bias': _L0_ffn_in['up_bias'], 'L0_ffn_down_kernel': _L0_ffn_in['down_kernel'], 'L0_ffn_down_bias': _L0_ffn_in['down_bias'], 'L1_attn_ln1_g': _L1_attn_in['ln1_g'], 'L1_attn_ln1_b': _L1_attn_in['ln1_b'], 'L1_attn_ln2_g': _L1_attn_in['ln2_g'], 'L1_attn_ln2_b': _L1_attn_in['ln2_b'], 'L1_attn_tm_w': _L1_attn_in['tm_w'], 'L1_attn_tm_u': _L1_attn_in['tm_u'], 'L1_attn_tm_mu_r': _L1_attn_in['tm_mu_r'], 'L1_attn_tm_mu_k': _L1_attn_in['tm_mu_k'], 'L1_attn_tm_mu_v': _L1_attn_in['tm_mu_v'], 'L1_attn_tm_Wr': _L1_attn_in['tm_Wr'], 'L1_attn_tm_Wk': _L1_attn_in['tm_Wk'], 'L1_attn_tm_Wv': _L1_attn_in['tm_Wv'], 'L1_attn_tm_Wout': _L1_attn_in['tm_Wout'], 'L1_attn_cm_mu_r': _L1_attn_in['cm_mu_r'], 'L1_attn_cm_mu_k': _L1_attn_in['cm_mu_k'], 'L1_attn_cm_Wr': _L1_attn_in['cm_Wr'], 'L1_attn_cm_Wk': _L1_attn_in['cm_Wk'], 'L1_attn_cm_Wv': _L1_attn_in['cm_Wv'], 'L1_xattn_gamma': _L1_xattn_in['gamma'], 'L1_ffn_down_w': _L1_ffn_in['down_w'], 'L1_ffn_down_b': _L1_ffn_in['down_b'], 'L1_ffn_up_w': _L1_ffn_in['up_w'], 'L1_ffn_up_b': _L1_ffn_in['up_b'], 'L1_ffn_router_w': _L1_ffn_in['router_w'], 'L1_ffn_router_b': _L1_ffn_in['router_b'], 'L1_ffn_shared_w1': _L1_ffn_in['shared_w1'], 'L1_ffn_shared_b1': _L1_ffn_in['shared_b1'], 'L1_ffn_shared_w2': _L1_ffn_in['shared_w2'], 'L1_ffn_shared_b2': _L1_ffn_in['shared_b2'], 'L1_ffn_core_w': _L1_ffn_in['core_w'], 'L1_ffn_core_b': _L1_ffn_in['core_b'], 'L1_ffn_e0_w1': _L1_ffn_in['e0_w1'], 'L1_ffn_e0_b1': _L1_ffn_in['e0_b1'], 'L1_ffn_e0_w2': _L1_ffn_in['e0_w2'], 'L1_ffn_e0_b2': _L1_ffn_in['e0_b2'], 'L1_ffn_e1_w1': _L1_ffn_in['e1_w1'], 'L1_ffn_e1_b1': _L1_ffn_in['e1_b1'], 'L1_ffn_e1_w2': _L1_ffn_in['e1_w2'], 'L1_ffn_e1_b2': _L1_ffn_in['e1_b2'], 'L1_ffn_e2_w1': _L1_ffn_in['e2_w1'], 'L1_ffn_e2_b1': _L1_ffn_in['e2_b1'], 'L1_ffn_e2_w2': _L1_ffn_in['e2_w2'], 'L1_ffn_e2_b2': _L1_ffn_in['e2_b2'], 'L1_ffn_e3_w1': _L1_ffn_in['e3_w1'], 'L1_ffn_e3_b1': _L1_ffn_in['e3_b1'], 'L1_ffn_e3_w2': _L1_ffn_in['e3_w2'], 'L1_ffn_e3_b2': _L1_ffn_in['e3_b2'], 'L1_ffn_e4_w1': _L1_ffn_in['e4_w1'], 'L1_ffn_e4_b1': _L1_ffn_in['e4_b1'], 'L1_ffn_e4_w2': _L1_ffn_in['e4_w2'], 'L1_ffn_e4_b2': _L1_ffn_in['e4_b2'], 'L1_ffn_e5_w1': _L1_ffn_in['e5_w1'], 'L1_ffn_e5_b1': _L1_ffn_in['e5_b1'], 'L1_ffn_e5_w2': _L1_ffn_in['e5_w2'], 'L1_ffn_e5_b2': _L1_ffn_in['e5_b2'], 'L1_ffn_e6_w1': _L1_ffn_in['e6_w1'], 'L1_ffn_e6_b1': _L1_ffn_in['e6_b1'], 'L1_ffn_e6_w2': _L1_ffn_in['e6_w2'], 'L1_ffn_e6_b2': _L1_ffn_in['e6_b2'], 'L1_ffn_e7_w1': _L1_ffn_in['e7_w1'], 'L1_ffn_e7_b1': _L1_ffn_in['e7_b1'], 'L1_ffn_e7_w2': _L1_ffn_in['e7_w2'], 'L1_ffn_e7_b2': _L1_ffn_in['e7_b2'], 'L2_attn_wq': _L2_attn_in['wq'], 'L2_attn_wk': _L2_attn_in['wk'], 'L2_attn_wv': _L2_attn_in['wv'], 'L2_attn_wo': _L2_attn_in['wo'], 'L2_ffn_router_w': _L2_ffn_in['router_w'], 'L2_ffn_w_gate': _L2_ffn_in['w_gate'], 'L2_ffn_w_up': _L2_ffn_in['w_up'], 'L2_ffn_w_down': _L2_ffn_in['w_down'], 'L2_ffn_sh_gate': _L2_ffn_in['sh_gate'], 'L2_ffn_sh_up': _L2_ffn_in['sh_up'], 'L2_ffn_sh_down': _L2_ffn_in['sh_down'], 'L2_ffn_sh_gate_w': _L2_ffn_in['sh_gate_w'], 'L3_attn_wq': _L3_attn_in['wq'], 'L3_attn_wk': _L3_attn_in['wk'], 'L3_attn_wv': _L3_attn_in['wv'], 'L3_attn_wo': _L3_attn_in['wo'], 'L3_xattn_w': _L3_xattn_in['w'], 'L3_xattn_u': _L3_xattn_in['u'], 'L3_ffn_W_up': _L3_ffn_in['W_up'], 'L3_ffn_W_gate': _L3_ffn_in['W_gate'], 'L3_ffn_W_down': _L3_ffn_in['W_down']}

def reference(x, ctx_2048, L0_attn_Wq, L0_attn_Wk, L0_attn_Wv, L0_attn_Wo, L0_ffn_up_kernel, L0_ffn_up_bias, L0_ffn_down_kernel, L0_ffn_down_bias, L1_attn_ln1_g, L1_attn_ln1_b, L1_attn_ln2_g, L1_attn_ln2_b, L1_attn_tm_w, L1_attn_tm_u, L1_attn_tm_mu_r, L1_attn_tm_mu_k, L1_attn_tm_mu_v, L1_attn_tm_Wr, L1_attn_tm_Wk, L1_attn_tm_Wv, L1_attn_tm_Wout, L1_attn_cm_mu_r, L1_attn_cm_mu_k, L1_attn_cm_Wr, L1_attn_cm_Wk, L1_attn_cm_Wv, L1_xattn_gamma, L1_ffn_down_w, L1_ffn_down_b, L1_ffn_up_w, L1_ffn_up_b, L1_ffn_router_w, L1_ffn_router_b, L1_ffn_shared_w1, L1_ffn_shared_b1, L1_ffn_shared_w2, L1_ffn_shared_b2, L1_ffn_core_w, L1_ffn_core_b, L1_ffn_e0_w1, L1_ffn_e0_b1, L1_ffn_e0_w2, L1_ffn_e0_b2, L1_ffn_e1_w1, L1_ffn_e1_b1, L1_ffn_e1_w2, L1_ffn_e1_b2, L1_ffn_e2_w1, L1_ffn_e2_b1, L1_ffn_e2_w2, L1_ffn_e2_b2, L1_ffn_e3_w1, L1_ffn_e3_b1, L1_ffn_e3_w2, L1_ffn_e3_b2, L1_ffn_e4_w1, L1_ffn_e4_b1, L1_ffn_e4_w2, L1_ffn_e4_b2, L1_ffn_e5_w1, L1_ffn_e5_b1, L1_ffn_e5_w2, L1_ffn_e5_b2, L1_ffn_e6_w1, L1_ffn_e6_b1, L1_ffn_e6_w2, L1_ffn_e6_b2, L1_ffn_e7_w1, L1_ffn_e7_b1, L1_ffn_e7_w2, L1_ffn_e7_b2, L2_attn_wq, L2_attn_wk, L2_attn_wv, L2_attn_wo, L2_ffn_router_w, L2_ffn_w_gate, L2_ffn_w_up, L2_ffn_w_down, L2_ffn_sh_gate, L2_ffn_sh_up, L2_ffn_sh_down, L2_ffn_sh_gate_w, L3_attn_wq, L3_attn_wk, L3_attn_wv, L3_attn_wo, L3_xattn_w, L3_xattn_u, L3_ffn_W_up, L3_ffn_W_gate, L3_ffn_W_down):
    import jax
    import jax.numpy as jnp

    def _L0_attn_ref(X, Wq, Wk, Wv, Wo):
        import jax, jax.numpy as jnp
        import numpy as np
        B, T, C = (2, 256, 256)
        NH, NKV, HD = (16, 8, 32)
        SOFTCAP = 50.0
        ROPE_BASE = 10000.0

        def _rotate_half(x):
            x1, x2 = (x[..., :x.shape[-1] // 2], x[..., x.shape[-1] // 2:])
            return jnp.concatenate((-x2, x1), axis=-1)

        def _rope_cos_sin(t, head_dim, dtype):
            inv_freq = 1.0 / ROPE_BASE ** (jnp.arange(0, head_dim, 2, dtype=jnp.int32).astype(jnp.float32) / head_dim)
            pos = jnp.arange(t, dtype=jnp.float32)
            freqs = pos[:, None] * inv_freq[None, :]
            emb = jnp.concatenate((freqs, freqs), axis=-1)
            return (jnp.cos(emb).astype(dtype)[None, None], jnp.sin(emb).astype(dtype)[None, None])
        b, t, c = X.shape
        n_rep = NH // NKV
        q = (X @ Wq).reshape(b, t, NH, HD).transpose(0, 2, 1, 3)
        k = (X @ Wk).reshape(b, t, NKV, HD).transpose(0, 2, 1, 3)
        v = (X @ Wv).reshape(b, t, NKV, HD).transpose(0, 2, 1, 3)
        cos, sin = _rope_cos_sin(t, HD, X.dtype)
        q = q * cos + _rotate_half(q) * sin
        k = k * cos + _rotate_half(k) * sin
        k = jnp.repeat(k, n_rep, axis=1)
        v = jnp.repeat(v, n_rep, axis=1)
        scale = 256.0 ** (-0.5)
        att = jnp.einsum('bhqd,bhkd->bhqk', q, k) * scale
        att = SOFTCAP * jnp.tanh(att / SOFTCAP)
        causal = jnp.tril(jnp.ones((t, t), dtype=bool))
        att = jnp.where(causal[None, None], att, -jnp.inf)
        att = jax.nn.softmax(att, axis=-1)
        y = jnp.einsum('bhqk,bhkd->bhqd', att, v)
        y = y.transpose(0, 2, 1, 3).reshape(b, t, NH * HD)
        return y @ Wo

    def _L0_xattn_ref(q, k, v):
        import jax, jax.numpy as jnp
        import numpy as np
        N_HEAD = 8
        b, d, m = q.shape
        c = v.shape[1]
        h = N_HEAD
        qh = q.reshape(b * h, d // h, m)
        kh = k.reshape(b * h, d // h, -1)
        vh = v.reshape(b * h, c // h, -1)
        scale = 1.0 / jnp.sqrt(jnp.asarray(d // h, dtype=q.dtype))
        qk = jnp.einsum('bdm,bdn->bmn', qh, kh) * scale
        sm = jax.nn.softmax(qk, axis=-1)
        ret = jnp.einsum('bmn,bcn->bcm', sm, vh)
        return ret.reshape(b, c, m)

    def _L0_ffn_ref(inputs, up_kernel, up_bias, down_kernel, down_bias):
        import jax, jax.numpy as jnp
        import numpy as np
        BLOCK_SIZE = 32
        FP4_GRID = jnp.array([0.0, 0.5, 1.0, 1.5, 2.0, 3.0, 4.0, 6.0], dtype=jnp.float32)
        FP4_MIDS = jnp.array([0.25, 0.75, 1.25, 1.75, 2.5, 3.5, 5.0], dtype=jnp.float32)

        def quantize_to_mxfp4(w, block_size=BLOCK_SIZE):
            K, N = w.shape
            wb = w.reshape(K // block_size, block_size, N)
            amax = jnp.max(jnp.abs(wb), axis=1, keepdims=True)
            exp = jnp.floor(jnp.log2(jnp.maximum(amax, 1e-30))) - 2.0
            scales = jnp.exp2(exp)
            x = wb / scales
            idx = jnp.digitize(jnp.abs(x), FP4_MIDS)
            q = jnp.sign(x) * FP4_GRID[idx]
            return (q, scales)

        def mxfp4_matmul(inputs, q, scales, block_size=BLOCK_SIZE):
            K = inputs.shape[-1]
            N = q.shape[-1]
            w = (q * scales).reshape(K, N)
            return inputs @ w
        q_up, s_up = quantize_to_mxfp4(up_kernel, BLOCK_SIZE)
        x = mxfp4_matmul(inputs, q_up, s_up, BLOCK_SIZE) + up_bias
        x = jax.nn.gelu(x)
        q_dn, s_dn = quantize_to_mxfp4(down_kernel, BLOCK_SIZE)
        x = mxfp4_matmul(x, q_dn, s_dn, BLOCK_SIZE) + down_bias
        return x

    def _L1_attn_ref(x, ln1_g, ln1_b, ln2_g, ln2_b, tm_w, tm_u, tm_mu_r, tm_mu_k, tm_mu_v, tm_Wr, tm_Wk, tm_Wv, tm_Wout, cm_mu_r, cm_mu_k, cm_Wr, cm_Wk, cm_Wv):
        import jax, jax.numpy as jnp
        import numpy as np
        DIM = 256
        B, T = (8, 256)

        def _layernorm(x, g, b, eps=1e-05):
            m = jnp.mean(x, axis=-1, keepdims=True)
            v = jnp.mean(jnp.square(x - m), axis=-1, keepdims=True)
            return (x - m) / jnp.sqrt(v + eps) * g + b

        def _shift(x):
            return jnp.pad(x[:, :-1, :], ((0, 0), (1, 0), (0, 0)))
        h = _layernorm(x, ln1_g, ln1_b)
        hp = _shift(h)
        xr = tm_mu_r * h + (1.0 - tm_mu_r) * hp
        xk = tm_mu_k * h + (1.0 - tm_mu_k) * hp
        xv = tm_mu_v * h + (1.0 - tm_mu_v) * hp
        r = jax.nn.sigmoid(jnp.einsum('btc,dc->btd', xr, tm_Wr))
        k = jnp.einsum('btc,dc->btd', xk, tm_Wk)
        v = jnp.einsum('btc,dc->btd', xv, tm_Wv)
        ek = jnp.exp(tm_u + k)
        wkv = ek * v / (ek + 1e-08)
        x = x + jnp.einsum('btc,dc->btd', r * wkv, tm_Wout)
        h2 = _layernorm(x, ln2_g, ln2_b)
        h2p = _shift(h2)
        xr2 = cm_mu_r * h2 + (1.0 - cm_mu_r) * h2p
        xk2 = cm_mu_k * h2 + (1.0 - cm_mu_k) * h2p
        r2 = jax.nn.sigmoid(jnp.einsum('btc,dc->btd', xr2, cm_Wr))
        k2 = jnp.square(jax.nn.relu(jnp.einsum('btc,dc->btd', xk2, cm_Wk)))
        x = x + r2 * jnp.einsum('btc,dc->btd', k2, cm_Wv)
        return x

    def _L1_xattn_ref(q, k, v, gamma):
        import jax, jax.numpy as jnp
        import numpy as np
        N_HEAD = 8
        B, Dq, Lq = q.shape
        Dv, Lk = (v.shape[-2], v.shape[-1])
        h = N_HEAD
        dq = Dq // h
        dv = Dv // h
        qh = q.reshape(B, h, dq, Lq)
        kh = k.reshape(B, h, dq, Lk)
        vh = v.reshape(B, h, dv, Lk)
        scale = 1.0 / jnp.sqrt(jnp.asarray(dq, dtype=q.dtype))
        qk = jnp.einsum('bhdq,bhdl->bhql', qh, kh) * scale
        sm = jax.nn.softmax(qk, axis=-1)
        ret = jnp.einsum('bhql,bhdl->bhdq', sm, vh)
        ret = ret.reshape(B, Dv, Lq)
        return gamma * ret

    def _L1_ffn_ref(x, down_w, down_b, up_w, up_b, router_w, router_b, shared_w1, shared_b1, shared_w2, shared_b2, core_w, core_b, e0_w1, e0_b1, e0_w2, e0_b2, e1_w1, e1_b1, e1_w2, e1_b2, e2_w1, e2_b1, e2_w2, e2_b2, e3_w1, e3_b1, e3_w2, e3_b2, e4_w1, e4_b1, e4_w2, e4_b2, e5_w1, e5_b1, e5_w2, e5_b2, e6_w1, e6_b1, e6_w2, e6_b2, e7_w1, e7_b1, e7_w2, e7_b2):
        import jax, jax.numpy as jnp
        import numpy as np
        COST_LAMBDA = 1e-07
        HID = [128, 256, 384, 512, 128, 256, 384, 512]
        TOP_K = 2

        def _gelu(v):
            return jax.nn.gelu(v, approximate=False)

        def _forward(x, down_w, down_b, up_w, up_b, router_w, router_b, shared_w1, shared_b1, shared_w2, shared_b2, core_w, core_b, expert_params):
            E = len(expert_params)
            h = x @ down_w + down_b
            cost = jnp.array([w1.shape[0] * w1.shape[1] + w2.shape[0] * w2.shape[1] for w1, _, w2, _ in expert_params], jnp.float32)
            logits = x @ router_w + router_b - COST_LAMBDA * cost
            probs = jax.nn.softmax(logits, axis=-1)
            topv, topi = jax.lax.top_k(probs, TOP_K)
            gate = jax.nn.softmax(topv, axis=-1)
            out = jnp.zeros_like(h)
            for k in range(TOP_K):
                mask = jax.nn.one_hot(topi[..., k], E, dtype=h.dtype)
                acc = jnp.zeros_like(h)
                for e, (w1, b1, w2, b2) in enumerate(expert_params):
                    hm = h * mask[..., e:e + 1]
                    acc = acc + (_gelu(_gelu(hm) @ w1 + b1) @ w2 + b2)
                out = out + acc * gate[..., k:k + 1]
            out = out + 0.1 * (_gelu(_gelu(h) @ shared_w1 + shared_b1) @ shared_w2 + shared_b2)
            out = out @ up_w + up_b
            out = out + (_gelu(x) @ core_w + core_b)
            return out
        ep = [(e0_w1, e0_b1, e0_w2, e0_b2), (e1_w1, e1_b1, e1_w2, e1_b2), (e2_w1, e2_b1, e2_w2, e2_b2), (e3_w1, e3_b1, e3_w2, e3_b2), (e4_w1, e4_b1, e4_w2, e4_b2), (e5_w1, e5_b1, e5_w2, e5_b2), (e6_w1, e6_b1, e6_w2, e6_b2), (e7_w1, e7_b1, e7_w2, e7_b2)]
        return _forward(x, down_w, down_b, up_w, up_b, router_w, router_b, shared_w1, shared_b1, shared_w2, shared_b2, core_w, core_b, ep)

    def _L2_attn_ref(x, wq, wk, wv, wo):
        import jax, jax.numpy as jnp
        import numpy as np
        DIM = 256
        N_HEADS = 32
        N_KV_HEADS = 8
        HEAD_DIM = DIM // N_HEADS
        ROPE_BASE = 10000.0
        BATCH = 2
        SEQ = 256

        def _rope_cos_sin(seq_len, dtype=jnp.float32):
            inv_freq = 1.0 / ROPE_BASE ** (jnp.arange(0, HEAD_DIM, 2, dtype=jnp.float32) / HEAD_DIM)
            pos = jnp.arange(seq_len, dtype=jnp.float32)
            freqs = pos[:, None] * inv_freq[None, :]
            return (jnp.cos(freqs).astype(dtype), jnp.sin(freqs).astype(dtype))

        def _apply_rope(x, cos, sin):
            cos = cos[None, None, :, :]
            sin = sin[None, None, :, :]
            x_even = x[..., ::2]
            x_odd = x[..., 1::2]
            rot_even = x_even * cos - x_odd * sin
            rot_odd = x_even * sin + x_odd * cos
            out = jnp.stack((rot_even, rot_odd), axis=-1)
            return out.reshape(x.shape)
        b, s, _ = x.shape
        q = (x @ wq).reshape(b, s, N_HEADS, HEAD_DIM).transpose(0, 2, 1, 3)
        k = (x @ wk).reshape(b, s, N_KV_HEADS, HEAD_DIM).transpose(0, 2, 1, 3)
        v = (x @ wv).reshape(b, s, N_KV_HEADS, HEAD_DIM).transpose(0, 2, 1, 3)
        cos, sin = _rope_cos_sin(s, x.dtype)
        q = _apply_rope(q, cos, sin)
        k = _apply_rope(k, cos, sin)
        rep = N_HEADS // N_KV_HEADS
        if rep > 1:
            k = jnp.repeat(k, rep, axis=1)
            v = jnp.repeat(v, rep, axis=1)
        scores = jnp.einsum('bhqd,bhkd->bhqk', q, k) / HEAD_DIM ** 0.5
        causal = jnp.tril(jnp.ones((s, s), dtype=bool))
        scores = jnp.where(causal[None, None], scores, -jnp.inf)
        probs = jax.nn.softmax(scores, axis=-1)
        out = jnp.einsum('bhqk,bhkd->bhqd', probs, v)
        out = out.transpose(0, 2, 1, 3).reshape(b, s, DIM)
        return out @ wo

    def _L2_xattn_ref(qkv, y):
        import math
        import jax, jax.numpy as jnp
        import numpy as np
        N_HEADS = 16
        bs, width, length = qkv.shape
        ch = width // N_HEADS
        q = qkv.reshape(bs * N_HEADS, ch, length)
        k = v = y.reshape(bs * N_HEADS, ch, -1)
        scale = 1.0 / math.sqrt(math.sqrt(ch))
        weight = jnp.einsum('bct,bcs->bts', q * scale, k * scale)
        weight = jax.nn.softmax(weight.astype(jnp.float32), axis=-1).astype(weight.dtype)
        a = jnp.einsum('bts,bcs->bct', weight, v)
        return a.reshape(bs, -1, length)

    def _L2_ffn_ref(hidden_states, router_w, w_gate, w_up, w_down, sh_gate, sh_up, sh_down, sh_gate_w):
        import jax, jax.numpy as jnp
        import numpy as np
        B, S, H = (2, 256, 256)
        E, K = (16, 4)
        I_MOE, I_SH = (176, 704)
        orig = hidden_states.shape
        h = hidden_states.reshape(-1, orig[-1])
        N = h.shape[0]
        logits = h @ router_w.T
        probs = jax.nn.softmax(logits.astype(jnp.float32), axis=-1)
        top_vals, top_idx = jax.lax.top_k(probs, K)
        top_vals = top_vals / jnp.maximum(top_vals.sum(-1, keepdims=True), 1e-09)
        top_vals = top_vals.astype(h.dtype)
        comb = jnp.zeros((N, E), h.dtype).at[jnp.arange(N)[:, None], top_idx].add(top_vals)
        g = jnp.einsum('nh,ehi->eni', h, w_gate)
        u = jnp.einsum('nh,ehi->eni', h, w_up)
        y = jnp.einsum('eni,eih->enh', jax.nn.silu(g) * u, w_down)
        routed = jnp.einsum('enh,ne->nh', y, comb)
        shared = jax.nn.silu(h @ sh_gate) * (h @ sh_up) @ sh_down
        sg = jax.nn.sigmoid(h @ sh_gate_w)
        return (routed + sg * shared).reshape(orig)

    def _L3_attn_ref(x, wq, wk, wv, wo):
        import jax, jax.numpy as jnp
        import numpy as np
        B, T, D = (2, 256, 256)
        QH, KVH = (16, 4)
        HD = D // QH

        def rotate_half(x):
            d = x.shape[-1] // 2
            return jnp.concatenate([-x[..., d:], x[..., :d]], axis=-1)

        def rope_tables(head_dim, seq_len, theta=10000.0):
            freqs = 1.0 / theta ** (jnp.arange(0, head_dim, 2, dtype=jnp.float32) / head_dim)
            t = jnp.arange(seq_len, dtype=jnp.float32)
            ang = t[:, None] * freqs[None, :]
            cos = jnp.tile(jnp.cos(ang), (1, 2))
            sin = jnp.tile(jnp.sin(ang), (1, 2))
            return (cos, sin)

        def apply_rope(x, cos, sin):
            c = cos[None, None, :, :]
            s = sin[None, None, :, :]
            return x * c + rotate_half(x) * s
        b, t, d = x.shape
        cos, sin = rope_tables(HD, t)
        q = (x @ wq).reshape(b, t, QH, HD).transpose(0, 2, 1, 3)
        k = (x @ wk).reshape(b, t, KVH, HD).transpose(0, 2, 1, 3)
        v = (x @ wv).reshape(b, t, KVH, HD).transpose(0, 2, 1, 3)
        q = apply_rope(q, cos, sin)
        k = apply_rope(k, cos, sin)
        g = QH // KVH
        k = jnp.repeat(k, g, axis=1)
        v = jnp.repeat(v, g, axis=1)
        attn = jnp.einsum('bhqd,bhkd->bhqk', q, k) / np.sqrt(HD)
        mask = jnp.triu(jnp.ones((t, t), dtype=bool), k=1)
        attn = jnp.where(mask[None, None], -jnp.inf, attn)
        attn = jax.nn.softmax(attn, axis=-1)
        out = jnp.einsum('bhqk,bhkd->bhqd', attn, v)
        out = out.transpose(0, 2, 1, 3).reshape(b, t, d)
        return out @ wo

    def _L3_xattn_ref(B, T, C, w, u, k, v):
        import jax, jax.numpy as jnp
        import numpy as np
        B_DIM, T_DIM, C_DIM = (16, 128, 256)

        def _wkv(w, u, k, v):
            Bn, Tn, Cn = k.shape
            NEG_INF = jnp.float32(-1e+38)

            def step(carry, kv_t):
                p, q, o = carry
                kt, vt = kv_t
                no = jnp.maximum(o, u + kt)
                A = jnp.exp(o - no)
                E = jnp.exp(u + kt - no)
                y = (A * p + E * vt) / (A * q + E)
                no2 = jnp.maximum(w + o, kt)
                A2 = jnp.exp(w + o - no2)
                E2 = jnp.exp(kt - no2)
                return ((A2 * p + E2 * vt, A2 * q + E2, no2), y)
            init = (jnp.zeros((Bn, Cn), k.dtype), jnp.zeros((Bn, Cn), k.dtype), jnp.full((Bn, Cn), NEG_INF, k.dtype))
            kT = jnp.moveaxis(k, 1, 0)
            vT = jnp.moveaxis(v, 1, 0)
            _, yT = jax.lax.scan(step, init, (kT, vT))
            return jnp.moveaxis(yT, 0, 1)
        return _wkv(w, u, k, v)

    def _L3_ffn_ref(x, W_up, W_gate, W_down):
        import jax, jax.numpy as jnp
        import numpy as np
        D_MODEL = 256
        D_EXPERT = 1024
        EPS = 1e-08

        def ternary_quant(w):
            scale = jnp.mean(jnp.abs(w)) + EPS
            q = jnp.clip(jnp.round(w / scale), -1.0, 1.0) * scale
            return w + jax.lax.stop_gradient(q - w)
        wu = ternary_quant(W_up)
        wg = ternary_quant(W_gate)
        wd = ternary_quant(W_down)
        up = jnp.einsum('bsd,ed->bse', x, wu)
        gate = jnp.einsum('bsd,ed->bse', x, wg)
        hidden = jax.nn.silu(up) * gate
        return jnp.einsum('bse,de->bsd', hidden, wd)
    x = x + _L0_attn_ref(_layernorm(x, axis=-1), L0_attn_Wq, L0_attn_Wk, L0_attn_Wv, L0_attn_Wo)
    x = x + _L0_xattn_ref(_layernorm(x, axis=-1), ctx_2048, ctx_2048)
    x = x + _L0_ffn_ref(_layernorm(x, axis=-1), L0_ffn_up_kernel, L0_ffn_up_bias, L0_ffn_down_kernel, L0_ffn_down_bias)
    x = x + _L1_attn_ref(_layernorm(x, axis=-1), L1_attn_ln1_g, L1_attn_ln1_b, L1_attn_ln2_g, L1_attn_ln2_b, L1_attn_tm_w, L1_attn_tm_u, L1_attn_tm_mu_r, L1_attn_tm_mu_k, L1_attn_tm_mu_v, L1_attn_tm_Wr, L1_attn_tm_Wk, L1_attn_tm_Wv, L1_attn_tm_Wout, L1_attn_cm_mu_r, L1_attn_cm_mu_k, L1_attn_cm_Wr, L1_attn_cm_Wk, L1_attn_cm_Wv)
    x = x + _L1_xattn_ref(_layernorm(x, axis=-1), ctx_2048, ctx_2048, L1_xattn_gamma)
    x = x + _L1_ffn_ref(_layernorm(x, axis=-1), L1_ffn_down_w, L1_ffn_down_b, L1_ffn_up_w, L1_ffn_up_b, L1_ffn_router_w, L1_ffn_router_b, L1_ffn_shared_w1, L1_ffn_shared_b1, L1_ffn_shared_w2, L1_ffn_shared_b2, L1_ffn_core_w, L1_ffn_core_b, L1_ffn_e0_w1, L1_ffn_e0_b1, L1_ffn_e0_w2, L1_ffn_e0_b2, L1_ffn_e1_w1, L1_ffn_e1_b1, L1_ffn_e1_w2, L1_ffn_e1_b2, L1_ffn_e2_w1, L1_ffn_e2_b1, L1_ffn_e2_w2, L1_ffn_e2_b2, L1_ffn_e3_w1, L1_ffn_e3_b1, L1_ffn_e3_w2, L1_ffn_e3_b2, L1_ffn_e4_w1, L1_ffn_e4_b1, L1_ffn_e4_w2, L1_ffn_e4_b2, L1_ffn_e5_w1, L1_ffn_e5_b1, L1_ffn_e5_w2, L1_ffn_e5_b2, L1_ffn_e6_w1, L1_ffn_e6_b1, L1_ffn_e6_w2, L1_ffn_e6_b2, L1_ffn_e7_w1, L1_ffn_e7_b1, L1_ffn_e7_w2, L1_ffn_e7_b2)
    x = x + _L2_attn_ref(_layernorm(x, axis=-1), L2_attn_wq, L2_attn_wk, L2_attn_wv, L2_attn_wo)
    x = x + _L2_xattn_ref(_layernorm(x, axis=-1), ctx_2048)
    x = x + _L2_ffn_ref(_layernorm(x, axis=-1), L2_ffn_router_w, L2_ffn_w_gate, L2_ffn_w_up, L2_ffn_w_down, L2_ffn_sh_gate, L2_ffn_sh_up, L2_ffn_sh_down, L2_ffn_sh_gate_w)
    x = x + _L3_attn_ref(_layernorm(x, axis=-1), L3_attn_wq, L3_attn_wk, L3_attn_wv, L3_attn_wo)
    x = x + _L3_xattn_ref(4, 256, 256, L3_xattn_w, L3_xattn_u, _layernorm(x, axis=-1), ctx_2048)
    x = x + _L3_ffn_ref(_layernorm(x, axis=-1), L3_ffn_W_up, L3_ffn_W_gate, L3_ffn_W_down)
    return x

_drawn_inputs = setup_inputs


def setup_inputs(seed=0):
    import zlib

    import numpy as np

    out = dict(_drawn_inputs(seed))
    spreads = {'L0_ffn_up_bias': (0.0, 0.1),
     'L0_ffn_down_bias': (0.0, 0.1),
     'L1_attn_ln1_g': (1.0, 0.2),
     'L1_attn_ln1_b': (0.0, 0.1),
     'L1_attn_ln2_g': (1.0, 0.2),
     'L1_attn_ln2_b': (0.0, 0.1),
     'L1_attn_tm_w': (0.0, 0.1),
     'L1_attn_tm_u': (0.0, 0.1),
     'L1_ffn_down_b': (0.0, 0.1),
     'L1_ffn_up_b': (0.0, 0.1),
     'L1_ffn_router_b': (0.0, 0.1),
     'L1_ffn_shared_b1': (0.0, 0.1),
     'L1_ffn_shared_b2': (0.0, 0.1),
     'L1_ffn_core_b': (0.0, 0.1),
     'L1_ffn_e0_b1': (0.0, 0.1),
     'L1_ffn_e0_b2': (0.0, 0.1),
     'L1_ffn_e1_b1': (0.0, 0.1),
     'L1_ffn_e1_b2': (0.0, 0.1),
     'L1_ffn_e2_b1': (0.0, 0.1),
     'L1_ffn_e2_b2': (0.0, 0.1),
     'L1_ffn_e3_b1': (0.0, 0.1),
     'L1_ffn_e3_b2': (0.0, 0.1),
     'L1_ffn_e4_b1': (0.0, 0.1),
     'L1_ffn_e4_b2': (0.0, 0.1),
     'L1_ffn_e5_b1': (0.0, 0.1),
     'L1_ffn_e5_b2': (0.0, 0.1),
     'L1_ffn_e6_b1': (0.0, 0.1),
     'L1_ffn_e6_b2': (0.0, 0.1),
     'L1_ffn_e7_b1': (0.0, 0.1),
     'L1_ffn_e7_b2': (0.0, 0.1)}
    factors = {}
    for name, (base, spread) in spreads.items():
        noise = np.random.default_rng([zlib.crc32(name.encode()), seed]).standard_normal(out[name].shape)
        drawn = base * np.exp(spread * noise) if base else spread * noise
        out[name] = jnp.asarray(drawn.astype(out[name].dtype))
    for name, factor in factors.items():
        out[name] = (out[name] * factor).astype(out[name].dtype)
    return out
```

```python
from contextlib import ExitStack

import numpy as np

import concourse.bass as bass
from concourse import mybir

F32 = mybir.dt.float32
BF16 = mybir.dt.bfloat16
U32 = mybir.dt.uint32
ALU = mybir.AluOpType
ACT = mybir.ActivationFunctionType
AX = mybir.AxisListType.X

P = 128
B, T, D = 4, 256, 256
TT = B * T // P
KD = D // P
CH = 512
NCH = B * T // CH
TPC = CH // P
EPS = 1e-5
NEG = -1e30

HID = [128, 256, 384, 512, 128, 256, 384, 512]
E1 = len(HID)
FB1 = [h // P for h in HID]
E2, I2, ISH = 16, 176, 704
NI2 = -(-(E2 * I2 + ISH) // P)
F3 = 1024
F0 = 1024

A_SIZES = {
    "q0": 2 * 512, "qp0": 2 * 512, "k0": 512, "kp0": 512, "v0": 512, "o0": 4 * 256,
    "upT0": 2048, "dnT0": 2048, "up0": 2048, "dn0": 2048,
    "wr": 512, "wk": 512, "wv": 512, "wout": 512, "cr": 512, "ck": 512, "cv": 512,
}
B_SIZES = {"down": KD * P, "up": D, "router": KD * E1, "sh1": P, "sh2": P, "core": KD * D,
           "w1": sum(HID), "w2": sum(FB1) * P}
L_SIZES = {"q2": 512, "qp2": 512, "k2": 512, "kp2": 512, "v2": 512, "o2": 512,
           "q3": 512, "qp3": 512, "k3": 512, "kp3": 512, "v3": 512, "o3": 512,
           "up3": 2048, "gate3": 2048, "dn3": 2048,
           "router2": KD * (E2 + 1)}
V_SIZES = {"b_up0": 8, "ln1_g": 2, "ln1_b": 2, "ln2_g": 2, "ln2_b": 2, "u": 2,
           "mu_r": 2, "mu_k": 2, "mu_v": 2, "cmu_r": 2, "cmu_k": 2,
           "b_down1": 1, "b_sh1": 1, "b_sh2": 1, "b1": sum(FB1), "b2": E1, "w3": 2, "u3": 2}
R_SIZES = {"b_dn0": D, "b_up1": D, "b_core": D, "b_router": E1, "gamma": 1}
HD_OF = {"32": 32, "8": 8, "16": 16}


def columns(sizes):
    at, n = {}, 0
    for name, size in sizes.items():
        at[name] = (n, size)
        n += size
    return at, n


A_AT, A_N = columns(A_SIZES)
B_AT, B_N = columns(B_SIZES)
L_AT, L_N = columns(L_SIZES)
V_AT, V_N = columns(V_SIZES)
R_AT, R_N = columns(R_SIZES)
RING2 = 4
RINGG = 2
RAW_A = ["q0", "qp0", "k0", "kp0", "v0", "o0", "upT0", "dnT0"]

C_SIZES = {"ident": P, "ones": P, "cos32": T, "sin32": T, "cos8": T, "sin8": T, "cos16": T, "sin16": T,
           "tril": P, "lower8": E1 * E1, "lower16": E2 * E2, "cost": E1, "eps": 1,
           "rows32": 4, "rows8": 16, "rows16": 8, "cols32": 32, "cols8": 4 * 32, "cols16": 2 * 32}
C_AT, C_N = columns(C_SIZES)


def shape_constants():
    c = np.zeros((P, C_N), np.float32)

    def put(name, a):
        at, n = C_AT[name]
        c[:, at:at + n] = np.asarray(a, np.float32).reshape(P, n)

    put("ident", np.eye(P))
    put("ones", np.ones((P, P)))
    pos = np.arange(T, dtype=np.float32)
    row = np.arange(P)
    for hd, paired in ((32, False), (8, True), (16, False)):
        inv = (np.float32(1.0) / np.float32(10000.0) ** (np.arange(0, hd, 2).astype(np.float32) / np.float32(hd))).astype(np.float32)
        ang = pos[None, :] * inv[:, None]
        d = row % hd
        freq = d // 2 if paired else d % (hd // 2)
        first = d % 2 == 0 if paired else d < hd // 2
        put(f"cos{hd}", np.cos(ang)[freq])
        put(f"sin{hd}", np.sin(ang)[freq] * np.where(first, -1.0, 1.0)[:, None])
        r = 32 // hd
        rows = np.zeros((P, r, 4))
        for s in range(4):
            for v in range(r):
                rows[32 * s + v * hd:32 * s + (v + 1) * hd, v, s] = 1.0
        put(f"rows{hd}", rows)
        cols = np.zeros((P, r, 32))
        for v in range(r):
            cols[:, v, v * hd:(v + 1) * hd] = 1.0
        put(f"cols{hd}", cols)
    put("tril", np.tril(np.ones((P, P))))
    for e in (E1, E2):
        put(f"lower{e}", np.broadcast_to(np.tril(np.ones((e, e)), -1), (P, e, e)))
    cost = np.float32(1e-07) * np.array([2 * P * h for h in HID], np.float32)
    put("cost", np.broadcast_to(cost, (P, E1)))
    put("eps", np.full((P, 1), EPS))
    return c


def build_decoder(nc, x, ctx, wa, wb, wl, w2f, vec, rowv, const, out):
    es = ExitStack()

    def sb(name, shape, dt=F32):
        return es.enter_context(nc.sbuf_tensor(name, shape, dt))

    def sem(name):
        return es.enter_context(nc.semaphore(name))

    X = sb("X", [P, TT, D])
    H = sb("H", [P, TT, D])
    HT = sb("HT", [P, KD, B * T])
    CX = sb("CX", [P, TT, D])
    CXT = sb("CXT", [P, KD, B * T])
    WA = sb("WA", [P, A_N])
    WB = sb("WB", [P, B_N])
    VEC = sb("VEC", [P, V_N])
    ROW = sb("ROW", [P, R_N])
    CST = sb("CST", [P, C_N])
    identb = sb("identb", [P, P], BF16)
    maskb = sb("maskb", [P, P], BF16)
    PS = es.enter_context(nc.psum_tensor("PS", [P, 8, 512], F32))
    gate_rows = nc.dram_tensor("gate_rows", [E2 + 1, B * T], F32, kind="Internal").ap()

    def part(store, at, name, k=None):
        a, n = at[name]
        v = store[:, a:a + n]
        return v if k is None else v.rearrange("p (k n) -> p k n", k=k)

    wA = lambda name, k=None: part(WA, A_AT, name, k)
    wB = lambda name, k=None: part(WB, B_AT, name, k)
    wL = lambda name, k=None: part(WA, L_AT, name, k)
    vv = lambda name: part(VEC, V_AT, name)
    rv = lambda name: part(ROW, R_AT, name)
    cst = lambda name, k=None: part(CST, C_AT, name, k)
    ident = cst("ident")

    def tok(a):
        return a.rearrange("b (h p) d -> p (b h) d", p=P)

    names = ["x_in", "ctx_in", "const_in", "a_in", "b_in", "late_in", "ctx_turned", "ctx_copied", "masks_made",
             "stats", "moments", "std", "rstd", "normed", "turned", "turned_out",
             "q_staged", "k_staged", "v_staged", "scores", "row_max", "bias", "exps", "turn_a", "turn_b",
             "copied_a", "copied_b", "pv", "den_inv", "heads_out", "head_tmp", "masked",
             "proj", "proj_rot", "rot_free", "rope_cos", "rope_sin", "rope_sum", "v_proj", "v_out", "o_proj", "x_added",
             "up_ps", "act_out", "down_ps", "gate_ps", "mult_out", "dve_chain", "pool_chain", "act_chain", "pe_mark",
             "dve_mark", "act_mark", "pool_mark", "bias_in", "gates", "gates_sent", "gates_back",
             "out_done"] + [f"w_slot{j}" for j in range(RING2)] + [f"g_slot{j}" for j in range(RINGG)]
    S = {n: sem(n) for n in names}
    done = dict.fromkeys(names, 0)

    def link(eng, ins, name):
        done[name] += 1
        ins.then_inc(S[name], 1)
        eng.wait_ge(S[name], done[name])

    def load_all():
        with nc.Block() as block:
            @block.sync
            def _(sp):
                sp.dma_start(X[:], tok(x)).then_inc(S["x_in"], 16)
                sp.dma_start(CST[:], const).then_inc(S["const_in"], 16)
                raw = sum(A_SIZES[n] for n in RAW_A)
                last = A_AT["wr"][0]
                sp.dma_start(WA[:, 0:raw], wa[:, 0:raw]).then_inc(S["a_in"], 16)
                sp.dma_start(CX[:], tok(ctx)).then_inc(S["ctx_in"], 16)
                sp.dma_start(VEC[:], vec).then_inc(S["b_in"], 16)
                sp.dma_start(ROW[:], rowv.to_broadcast([P, R_N])).then_inc(S["b_in"], 16)
                sp.dma_start(WA[:, last:A_N], wa[:, raw:]).then_inc(S["b_in"], 16)
                sp.dma_start(WB[:], wb).then_inc(S["b_in"], 16)

            @block.vector
            def _(dve):
                dve.wait_ge(S["const_in"], 16)
                dve.tensor_copy(identb[:], ident).then_inc(S["masks_made"], 1)
                dve.tensor_scalar(maskb[:], cst("tril"), -1.0, -NEG, ALU.add, ALU.mult).then_inc(S["masks_made"], 1)

            @block.tensor
            def _(pe):
                pe.wait_ge(S["const_in"], 16)
                pe.wait_ge(S["ctx_in"], 16)
                for g in range(TT // 2):
                    for k in range(KD):
                        for j in range(2):
                            last = pe.transpose(PS[:, g, k * 256 + j * P:k * 256 + (j + 1) * P],
                                                CX[:, 2 * g + j, k * P:(k + 1) * P], ident)
                    last.then_inc(S["ctx_turned"], 1)

            @block.scalar
            def _(act):
                for g in range(TT // 2):
                    act.wait_ge(S["ctx_turned"], g + 1)
                    act.activation(CXT[:, :, g * 256:(g + 1) * 256],
                                   PS[:, g, :].rearrange("p (k n) -> p k n", k=KD), ACT.Copy).then_inc(S["ctx_copied"], 1)

    def layernorm(src, dst, dstT=None, gain=None, shift=None, first=False):
        with ExitStack() as st:
            stats = st.enter_context(nc.sbuf_tensor(f"stats{nc.next_id()}", [P, TT, 6], F32))
            mom = st.enter_context(nc.sbuf_tensor(f"mom{nc.next_id()}", [P, TT, 2], F32))
            std = st.enter_context(nc.sbuf_tensor(f"std{nc.next_id()}", [P, TT], F32))
            rstd = st.enter_context(nc.sbuf_tensor(f"rstd{nc.next_id()}", [P, TT], F32))
            d = dict(done)
            with nc.Block() as block:
                @block.vector
                def _(dve):
                    if first:
                        dve.wait_ge(S["x_in"], 16)
                        dve.wait_ge(S["const_in"], 16)
                    for t in range(TT):
                        dve.bn_stats(stats[:, t, :], src[:, t, :]).then_inc(S["stats"], 1)
                    for t in range(TT):
                        dve.wait_ge(S["stats"], d["stats"] + t + 1)
                        dve.bn_aggr(mom[:, t, :], stats[:, t, :]).then_inc(S["moments"], 1)
                    dve.wait_ge(S["std"], d["std"] + 1)
                    dve.reciprocal(rstd[:], std[:]).then_inc(S["rstd"], 1)
                    dve.wait_ge(S["rstd"], d["rstd"] + 1)
                    for t in range(TT):
                        dve.tensor_scalar(dst[:, t, :], src[:, t, :], mom[:, t, 0:1], rstd[:, t:t + 1],
                                          ALU.subtract, ALU.mult).then_inc(S["normed"], 1)

                @block.scalar
                def _(act):
                    act.wait_ge(S["moments"], d["moments"] + TT)
                    act.activation(std[:], mom[:, :, 1], ACT.Sqrt, bias=cst("eps")).then_inc(S["std"], 1)
                    if dstT is not None:
                        for g in range(TT // 2):
                            act.wait_ge(S["turned"], d["turned"] + g + 1)
                            src_ps = PS[:, g, :].rearrange("p (k n) -> p k n", k=KD)
                            if gain is None:
                                act.activation(dstT(slice(0, KD), g), src_ps, ACT.Copy)
                            else:
                                for k in range(KD):
                                    act.activation(dstT(k, g), src_ps[:, k, :], ACT.Identity,
                                                   bias=shift[:, k:k + 1], scale=gain[:, k:k + 1])

                if dstT is not None:
                    @block.tensor
                    def _(pe):
                        for g in range(TT // 2):
                            pe.wait_ge(S["normed"], d["normed"] + 2 * g + 2)
                            for k in range(KD):
                                for j in range(2):
                                    last = pe.transpose(PS[:, g, k * 256 + j * P:k * 256 + (j + 1) * P],
                                                        dst[:, 2 * g + j, k * P:(k + 1) * P], ident)
                            last.then_inc(S["turned"], 1)
            for n, k in (("stats", TT), ("moments", TT), ("std", 1), ("rstd", 1), ("normed", TT),
                         ("turned", TT // 2 if dstT is not None else 0)):
                done[n] += k

    def to_HT(k, g):
        return HT[:, k, g * 256:(g + 1) * 256]

    def attention(hd, units, causal, scale, q_of, k_of, v_of, out_of, softcap=None, gamma=None):
        r = 32 // hd
        npair = 2 * r
        width = 384 if causal else 512
        d = dict(done)
        tag = str(nc.next_id())
        with ExitStack() as st:
            def tmp(name, shape, dt=F32):
                return st.enter_context(nc.sbuf_tensor(name + tag, shape, dt))

            QS = tmp("QS", [P, 2, T])
            KM = tmp("KM", [P, 2, 4, T])
            VM = tmp("VM", [P, 2, 2, r, P])
            PR = tmp("PR", [P, 2, 2, 512])
            PT = tmp("PT", [P, 2, 2, 512])
            MX = tmp("MX", [P, 2, 4])
            NB = tmp("NB", [P, 2, 4])
            DI = tmp("DI", [P, 2, T])
            rows = cst(f"rows{hd}", r)
            cols = cst(f"cols{hd}", r)

            def where(u, p):
                quad = p // 2
                slots = (2 * (p % 2), 2 * (p % 2) + 1)
                return quad, slots, (u * r + quad) % 2

            def steps():
                return [(u, p) for u in range(units) for p in range(npair)]

            NU = units * npair

            def ahead(bb, i, last):
                if i + 2 < NU:
                    return bb, i + 2
                return None if last else (bb + 1, i + 2 - NU)

            def batches(eng, body):
                with eng.Fori(0, B - 1) as bb:
                    body(bb, False)
                body(B - 1, True)

            with nc.Block() as block:
                @block.gpsimd
                def _(pool):
                    def batch(bb, last):
                        for u in range(units):
                            U = bb * units + u
                            pool.wait_ge(S["scores"], (U + 1) * npair + d["scores"])
                            pool.tensor_copy(QS[:, u % 2, :], q_of(bb, u)).then_inc(S["q_staged"], 1)
                            for q in range(r):
                                n = u * r + q
                                Q = bb * (units * r) + n
                                pool.wait_ge(S["scores"], Q * 2 + (2 * npair - 2 + d["scores"]))
                                pool.tensor_tensor(
                                    KM[:, n % 2], k_of(bb, u).rearrange("p (a t) -> p a t", a=1).to_broadcast([P, 4, T]),
                                    rows[:, q, :].rearrange("p (s a) -> p s a", a=1).to_broadcast([P, 4, T]),
                                    ALU.mult).then_inc(S["k_staged"], 1)
                                if q == 0:
                                    pool.wait_ge(S["pv"], (U + 1) * npair + d["pv"])
                                    for n2 in range(2):
                                        pool.tensor_tensor(
                                            VM[:, u % 2, n2].rearrange("p r (s c) -> p r s c", s=4),
                                            v_of(bb, u, n2).rearrange("p (a s c) -> p a s c", a=1, s=4).to_broadcast([P, r, 4, 32]),
                                            cols.rearrange("p r (a c) -> p r a c", a=1).to_broadcast([P, r, 4, 32]),
                                            ALU.mult).then_inc(S["v_staged"], 1)

                    for bb in range(B):
                        batch(bb, bb == B - 1)

                @block.tensor
                def _(pe):
                    pe.nop().then_inc(S["scores"], 2 * npair)
                    pe.nop().then_inc(S["pv"], 2 * npair)
                    pe.nop().then_inc(S["turn_b"], 2)

                    def score(bb, i):
                        u, p = i // npair, i % npair
                        quad, slots, kb = where(u, p)
                        G = bb * NU + i
                        if p == 0:
                            pe.wait_ge(S["q_staged"], bb * units + (u + 1 + d["q_staged"]))
                        if p % 2 == 0:
                            pe.wait_ge(S["k_staged"], bb * (units * r) + (u * r + quad + 1 + d["k_staged"]))
                        pe.wait_ge(S["exps"], G + (1 + d["exps"]))
                        for h in range(2):
                            bank = PS[:, 2 * (i % 2) + h, :]
                            for m in range(2):
                                n = P * (m + 1) if causal else T
                                last = pe.matmul(bank[:, m * T:m * T + n], QS[:, u % 2, m * P:(m + 1) * P],
                                                 KM[:, kb, slots[h], 0:n], start=True, stop=softcap is not None or not causal,
                                                 skip_group_check=True)
                                if causal and softcap is None:
                                    last = pe.matmul(bank[:, m * T + m * P:m * T + (m + 1) * P], identb[:], maskb[:],
                                                     start=False, stop=True, skip_group_check=True)
                        last.then_inc(S["scores"], 1)

                    def turn(bb, i):
                        G = bb * NU + i
                        ready = "masked" if softcap is not None else "exps"
                        pe.wait_ge(S[ready], G + ((1 if softcap is not None else 3) + d[ready]))
                        for h in range(2):
                            pe.wait_ge(S["copied_a" if h == 0 else "copied_b"], G + (1 + d["copied_a" if h == 0 else "copied_b"]))
                            for n in range(2):
                                for m in range(n if causal else 0, 2):
                                    col = n * T + m * P - (P if causal and n else 0)
                                    last = pe.transpose(PS[:, 4 + h, col:col + P],
                                                        PR[:, i % 2, h, m * T + n * P:m * T + (n + 1) * P], ident)
                            last.then_inc(S["turn_a" if h == 0 else "turn_b"], 1)

                    def product(bb, i):
                        u, p = i // npair, i % npair
                        quad, slots, _ = where(u, p)
                        G = bb * NU + i
                        pe.wait_ge(S["copied_a"], G + (2 + d["copied_a"]))
                        pe.wait_ge(S["copied_b"], G + (2 + d["copied_b"]))
                        if p == 0:
                            pe.wait_ge(S["v_staged"], bb * (2 * units) + (2 * u + 2 + d["v_staged"]))
                            pe.wait_ge(S["heads_out"], bb * units + (u + 1 + d["heads_out"]))
                        bank = PS[:, 6 + u % 2, :]
                        for what in range(2):
                            for n in range(2):
                                for h in range(2):
                                    s = slots[h]
                                    lo = P if causal and n else 0
                                    src = PT[:, i % 2, h, T:width] if n else PT[:, i % 2, h, 0:T]
                                    lhs = VM[:, u % 2, n, quad, 32 * s:32 * s + 32] if what == 0 else cols[:, quad, :]
                                    last = pe.matmul(bank[32 * s:32 * s + 32, what * T + lo:what * T + T], lhs, src,
                                                     start=(quad == 0 and what == 0 and n == 0),
                                                     stop=(quad == r - 1 and what == 1 and n == 1),
                                                     skip_group_check=True, tile_position=(0, 32 * s))
                        last.then_inc(S["pv"], 1)

                    score(0, 0)
                    score(0, 1)

                    def batch(bb, last):
                        for i in range(NU):
                            turn(bb, i)
                            nxt = ahead(bb, i, last)
                            if nxt is not None:
                                score(*nxt)
                            product(bb, i)

                    batches(pe, batch)

                @block.vector
                def _(dve):
                    dve.nop().then_inc(S["copied_a"], 1)
                    dve.nop().then_inc(S["heads_out"], 2)

                    def maxima(bb, i):
                        G = bb * NU + i
                        pr = i % 2
                        if softcap is not None:
                            dve.wait_ge(S["bias"], G + (1 + d["bias"]))
                            v = PR[:, pr].rearrange("p h (a n) -> p h a n", a=4)[:, :, 0:4:3, :]
                            tri = cst("tril", 1).rearrange("p a (b n) -> p a b n", b=1).to_broadcast([P, 2, 2, P])
                            dve.tensor_tensor(v, v, tri, ALU.mult).then_inc(S["masked"], 1)
                            return
                        dve.wait_ge(S["scores"], G + (1 + 2 * npair + d["scores"]))
                        mx = MX[:, pr].rearrange("p (h m) -> p h m", h=2)
                        if causal:
                            v = PS[:, 2 * pr:2 * pr + 2, :]
                            dve.tensor_reduce(mx[:, :, 0], v[:, :, 0:P], AX, ALU.max).then_inc(S["row_max"], 1)
                            dve.tensor_reduce(mx[:, :, 1], v[:, :, T:2 * T], AX, ALU.max).then_inc(S["row_max"], 1)
                        else:
                            v = PS[:, 2 * pr:2 * pr + 2, :].rearrange("p h (m n) -> p (h m) n", m=2)
                            dve.tensor_reduce(MX[:, pr], v, AX, ALU.max).then_inc(S["row_max"], 2)
                        dve.wait_ge(S["row_max"], 2 * G + (2 + d["row_max"]))
                        dve.tensor_scalar(NB[:, pr], MX[:, pr], -scale, None, ALU.mult).then_inc(S["bias"], 1)

                    def copy(bb, i):
                        G = bb * NU + i
                        dve.wait_ge(S["turn_a"], G + (1 + d["turn_a"]))
                        dve.wait_ge(S["pv"], G + (2 * npair - 1 + d["pv"]))
                        dve.tensor_copy(PT[:, i % 2, 0, 0:width], PS[:, 4, 0:width]).then_inc(S["copied_a"], 1)

                    def normalise(bb, u):
                        U = bb * units + u
                        bank = PS[:, 6 + u % 2, :]
                        dve.wait_ge(S["pv"], (U + 3) * npair + d["pv"])
                        dve.reciprocal(DI[:, u % 2, :], bank[:, T:2 * T]).then_inc(S["den_inv"], 1)
                        dve.wait_ge(S["den_inv"], U + (1 + d["den_inv"]))
                        dst, add = out_of(bb, u)
                        if add is None:
                            dve.tensor_tensor(dst, bank[:, 0:T], DI[:, u % 2, :], ALU.mult).then_inc(S["heads_out"], 1)
                            return
                        dve.tensor_tensor(DI[:, u % 2, :], bank[:, 0:T], DI[:, u % 2, :], ALU.mult).then_inc(S["heads_out"], 1)
                        dve.wait_ge(S["heads_out"], U + (3 + d["heads_out"]))
                        dve.scalar_tensor_tensor(dst, DI[:, u % 2, :], 1.0 if gamma is None else gamma, dst,
                                                 ALU.mult, ALU.add)

                    maxima(0, 0)
                    maxima(0, 1)

                    def batch(bb, last):
                        for i in range(NU):
                            copy(bb, i)
                            nxt = ahead(bb, i, last)
                            if nxt is not None:
                                maxima(*nxt)
                            if i % npair == npair - 1:
                                normalise(bb, i // npair)

                    batches(dve, batch)

                @block.scalar
                def _(act):
                    act.nop().then_inc(S["copied_b"], 1)
                    act.nop().then_inc(S["exps"], 2)

                    def exps(bb, i):
                        G = bb * NU + i
                        pr = i % 2
                        act.wait_ge(S["turn_b"], G + (1 + d["turn_b"]))
                        if softcap is not None:
                            act.wait_ge(S["scores"], G + (1 + 2 * npair + d["scores"]))
                            for m in range(2):
                                n = P * (m + 1) if causal else T
                                v = PR[:, pr, :, m * T:m * T + n]
                                ins = act.activation(v, PS[:, 2 * pr:2 * pr + 2, m * T:m * T + n], ACT.Tanh, scale=scale / softcap)
                                if m == 1:
                                    ins.then_inc(S["exps"], 1)
                            act.wait_ge(S["exps"], G + (3 + d["exps"]))
                            for m in range(2):
                                n = P * (m + 1) if causal else T
                                v = PR[:, pr, :, m * T:m * T + n]
                                ins = act.activation(v, v, ACT.Exp, scale=softcap)
                            ins.then_inc(S["bias"], 1)
                            return
                        act.wait_ge(S["bias"], G + (1 + d["bias"]))
                        for h in range(2):
                            for m in range(2):
                                n = P * (m + 1) if causal else T
                                ins = act.activation(PR[:, pr, h, m * T:m * T + n], PS[:, 2 * pr + h, m * T:m * T + n],
                                                     ACT.Exp, bias=NB[:, pr, 2 * h + m:2 * h + m + 1], scale=scale)
                        ins.then_inc(S["exps"], 1)

                    def copy(bb, i):
                        G = bb * NU + i
                        act.wait_ge(S["turn_b"], G + (3 + d["turn_b"]))
                        act.wait_ge(S["pv"], G + (2 * npair - 1 + d["pv"]))
                        act.activation(PT[:, i % 2, 1, 0:width], PS[:, 5, 0:width], ACT.Copy).then_inc(S["copied_b"], 1)

                    exps(0, 0)
                    exps(0, 1)

                    def batch(bb, last):
                        for i in range(NU):
                            copy(bb, i)
                            nxt = ahead(bb, i, last)
                            if nxt is not None:
                                exps(*nxt)

                    batches(act, batch)

            n = B * NU
            for name, k in (("q_staged", B * units), ("k_staged", B * units * r), ("v_staged", 2 * B * units),
                            ("scores", n + 2 * npair), ("row_max", 0 if softcap is not None else 2 * n), ("bias", n),
                            ("exps", n + 2), ("turn_a", n), ("turn_b", n + 2), ("copied_a", n + 1),
                            ("copied_b", n + 1), ("pv", n + 2 * npair), ("den_inv", B * units),
                            ("heads_out", B * units + 2), ("masked", n if softcap is not None else 0)):
                done[name] += k

    def project(w, nq, hd, QT, KT, V, arrived=None):
        d = dict(done)
        cos = cst(f"cos{hd}", 1)
        sin = cst(f"sin{hd}", 1)
        nchunk = CH // T
        work = [(w["q"], w["qp"], QT, j, c) for j in range(nq) for c in range(NCH)]
        work += [(w["k"], w["kp"], KT, j, c) for j in range(2) for c in range(NCH)]
        with ExitStack() as st:
            tag = str(nc.next_id())
            RC = st.enter_context(nc.sbuf_tensor("RC" + tag, [P, 2, CH], F32))
            RS = st.enter_context(nc.sbuf_tensor("RS" + tag, [P, 2, CH], F32))
            with nc.Block() as block:
                @block.tensor
                def _(pe):
                    if arrived is not None:
                        pe.wait_ge(*arrived)
                    for n, (a, ap, _, j, c) in enumerate(work):
                        if n >= 2:
                            pe.wait_ge(S["rope_sin"], d["rope_sin"] + n - 1)
                        for half, wt in enumerate((a, ap)):
                            for k in range(KD):
                                last = pe.matmul(PS[:, 2 * (n % 2) + half, :], wt[:, k, j * P:(j + 1) * P],
                                                 HT[:, k, c * CH:(c + 1) * CH], start=k == 0, stop=k == KD - 1)
                        last.then_inc(S["proj"], 1)
                    for t in range(TT):
                        if t >= 2:
                            pe.wait_ge(S["v_out"], d["v_out"] + t - 1)
                        for k in range(KD):
                            last = pe.matmul(PS[:, 4 + t % 2, 0:D], HT[:, k, t * P:(t + 1) * P], w["v"][:, k, :],
                                             start=k == 0, stop=k == KD - 1)
                        last.then_inc(S["v_proj"], 1)

                @block.vector
                def _(dve):
                    for n, (_, _, dst, j, c) in enumerate(work):
                        dve.wait_ge(S["proj"], d["proj"] + n + 1)
                        ps = lambda half: PS[:, 2 * (n % 2) + half, :].rearrange("p (b t) -> p b t", t=T)
                        tm = lambda a: a[:, n % 2].rearrange("p (b t) -> p b t", t=T)
                        dve.tensor_tensor(tm(RC), ps(0), cos.to_broadcast([P, nchunk, T]), ALU.mult).then_inc(S["rope_cos"], 1)
                        dve.tensor_tensor(tm(RS), ps(1), sin.to_broadcast([P, nchunk, T]), ALU.mult).then_inc(S["rope_sin"], 1)
                        dve.wait_ge(S["rope_cos"], d["rope_cos"] + n + 1)
                        dve.wait_ge(S["rope_sin"], d["rope_sin"] + n + 1)
                        dve.tensor_tensor(dst[:, j, c * CH:(c + 1) * CH], RC[:, n % 2], RS[:, n % 2], ALU.add)

                @block.scalar
                def _(act):
                    for t in range(TT):
                        act.wait_ge(S["v_proj"], d["v_proj"] + t + 1)
                        act.activation(V[:, t, :], PS[:, 4 + t % 2, 0:D], ACT.Copy).then_inc(S["v_out"], 1)
        done["proj"] += len(work)
        done["rope_cos"] += len(work)
        done["rope_sin"] += len(work)
        done["v_proj"] += TT
        done["v_out"] += TT

    def add_rows(lhs, rhs, nk, dst=X, mult=None):
        d = dict(done)
        with nc.Block() as block:
            @block.tensor
            def _(pe):
                for t in range(TT):
                    for k in range(nk):
                        last = pe.matmul(PS[:, t, 0:D], lhs(k, t), rhs(k), start=k == 0, stop=k == nk - 1)
                    last.then_inc(S["o_proj"], 1)

            @block.vector
            def _(dve):
                for t in range(TT):
                    dve.wait_ge(S["o_proj"], d["o_proj"] + t + 1)
                    if mult is None:
                        dve.tensor_tensor(dst[:, t, :], dst[:, t, :], PS[:, t, 0:D], ALU.add).then_inc(S["x_added"], 1)
                    else:
                        mult(dve, t, d)
        done["o_proj"] += TT
        done["x_added"] += TT

    def self_attention(layer, w, nq, hd, scale, softcap=None, arrived=None):
        with ExitStack() as st:
            QT = st.enter_context(nc.sbuf_tensor(f"QT{layer}", [P, nq, B * T], F32))
            KT = st.enter_context(nc.sbuf_tensor(f"KT{layer}", [P, 2, B * T], F32))
            V = st.enter_context(nc.sbuf_tensor(f"V{layer}", [P, TT, D], F32))
            project(w, nq, hd, QT, KT, V, arrived)
            per = nq // 2
            attention(hd, nq, True, scale,
                      q_of=lambda b, u: QT[:, u, bass.ds(b * T, T)],
                      k_of=lambda b, u: KT[:, u // per, bass.ds(b * T, T)],
                      v_of=lambda b, u, n: V[:, 2 * b + n, (u // per) * P:(u // per + 1) * P],
                      out_of=lambda b, u: (QT[:, u, bass.ds(b * T, T)], None), softcap=softcap)
            add_rows(lambda k, t: QT[:, k, t * P:(t + 1) * P], lambda k: w["o"][:, k, :], nq)

    def cross_attention(hd, gamma=None):
        attention(hd, 2, False, float(hd) ** -0.5,
                  q_of=lambda b, u: H[:, 2 * b + u, :],
                  k_of=lambda b, u: CX[:, 2 * b + u, :],
                  v_of=lambda b, u, n: CXT[:, n, bass.ds((2 * b + u) * P, P)],
                  out_of=lambda b, u: (X[:, 2 * b + u, :], True), gamma=gamma)

    def quantise_fp4():
        raw = WA[:, A_AT["upT0"][0]:A_AT["upT0"][0] + 4096]
        n = 2048
        tag = str(nc.next_id())
        with ExitStack() as st:
            def tmp(name, shape, dt=F32):
                return st.enter_context(nc.sbuf_tensor(name + tag, shape, dt))
            AB, SG, LO, HI = (tmp(x, [P, n]) for x in ("AB", "SG", "LO", "HI"))
            am, pw, iv = (tmp(x, [P, n // 32]) for x in ("am", "pw", "iv"))
            grp = lambda a: a[:].rearrange("p (g w) -> p g w", w=32)
            wide = lambda a: a[:].rearrange("p (g w) -> p g w", w=1).to_broadcast([P, n // 32, 32])
            d = dict(done)
            with nc.Block() as block:
                @block.scalar
                def _(act):
                    for h in range(2):
                        if h:
                            act.wait_ge(S["dve_mark"], d["dve_mark"] + 1)
                        act.activation(AB[:], raw[:, h * n:(h + 1) * n], ACT.Abs).then_inc(S["act_mark"], 1)
                        act.activation(SG[:], raw[:, h * n:(h + 1) * n], ACT.Sign).then_inc(S["act_mark"], 1)
                    for g in range(8):
                        act.wait_ge(S["turned"], d["turned"] + g + 1)
                        if g < 4:
                            k, f = g // 2, 4 * (g % 2)
                            dst = wA("up0", KD)[:, k, f * P:(f + 4) * P]
                            act.activation(dst, PS[:, g, :], ACT.Copy)
                        else:
                            f = 2 * (g - 4)
                            act.activation(wA("dn0")[:, f * D:(f + 2) * D], PS[:, g, :], ACT.Copy)

                @block.vector
                def _(dve):
                    L = lambda ins: link(dve, ins, "dve_chain")
                    for h in range(2):
                        dve.wait_ge(S["act_mark"], d["act_mark"] + 2 * h + 2)
                        L(dve.tensor_reduce(am[:], grp(AB), AX, ALU.max))
                        L(dve.tensor_scalar(am[:], am[:], 1e-30, None, ALU.max))
                        L(dve.tensor_scalar(pw[:].bitcast(U32), am[:].bitcast(U32), 0x7F800000, None, ALU.bitwise_and))
                        L(dve.reciprocal(iv[:], pw[:]))
                        L(dve.tensor_scalar(iv[:], iv[:], 4.0, None, ALU.mult))
                        L(dve.tensor_tensor(grp(AB), grp(AB), wide(iv), ALU.mult))
                        L(dve.tensor_scalar(pw[:], pw[:], 0.25, None, ALU.mult))
                        L(dve.tensor_scalar(HI[:], AB[:], 5.0, 2.0, ALU.is_ge, ALU.mult))
                        for mid in (3.5, 2.5):
                            L(dve.scalar_tensor_tensor(HI[:], AB[:], mid, HI[:], ALU.is_ge, ALU.add))
                        L(dve.tensor_scalar(LO[:], AB[:], 1.75, None, ALU.is_ge))
                        for mid in (1.25, 0.75, 0.25):
                            L(dve.scalar_tensor_tensor(LO[:], AB[:], mid, LO[:], ALU.is_ge, ALU.add))
                        L(dve.scalar_tensor_tensor(HI[:], LO[:], 0.5, HI[:], ALU.mult, ALU.add))
                        L(dve.tensor_tensor(HI[:], HI[:], SG[:], ALU.mult))
                        dve.tensor_tensor(raw[:, h * n:(h + 1) * n].rearrange("p (g w) -> p g w", w=32),
                                          grp(HI), wide(pw), ALU.mult).then_inc(S["dve_mark"], 1)

                @block.tensor
                def _(pe):
                    upT, dnT = wA("upT0", 8), wA("dnT0", KD)
                    for g in range(8):
                        pe.wait_ge(S["dve_mark"], d["dve_mark"] + 1 + g // 4)
                        for j in range(4):
                            if g < 4:
                                src = upT[:, 4 * (g % 2) + j, (g // 2) * P:(g // 2 + 1) * P]
                            else:
                                f = 2 * (g - 4) + j // 2
                                src = dnT[:, j % 2, f * P:(f + 1) * P]
                            last = pe.transpose(PS[:, g, j * P:(j + 1) * P], src, ident)
                        last.then_inc(S["turned"], 1)
            done["act_mark"] += 4
            done["dve_mark"] += 2
            done["turned"] += 8

    def mlp(n, up, gate, down, mode, bias=None, scales=None, load=None, gates=None):
        two = mode == "silu"
        d = dict(done)
        tag = str(nc.next_id())
        with ExitStack() as st:
            def tmp(name, shape, dt=F32):
                return st.enter_context(nc.sbuf_tensor(name + tag, shape, dt))
            AO = tmp("AO", [P, NCH, CH])
            MO = tmp("MO", [P, NCH, CH])
            HO = tmp("HO", [P, NCH, CH])
            with nc.Block() as block:
                if load is not None:
                    @block.sync
                    def _(sp):
                        load(sp, d)

                @block.tensor
                def _(pe):
                    def go_up(i, c):
                        if load is not None and c == 0:
                            pe.wait_ge(S[f"w_slot{i % RING2}"], 16 * (i // RING2 + 1))
                        if i >= 1:
                            name = "mult_out" if two else "act_out"
                            pe.wait_ge(S[name], d[name] + NCH * (i - 1) + c + 1)
                        for half, w in enumerate((up, gate) if two else (up,)):
                            for k in range(KD):
                                last = pe.matmul(PS[:, 2 * c + half, :], w(i, k), HT[:, k, c * CH:(c + 1) * CH],
                                                 start=k == 0, stop=k == KD - 1)
                        last.then_inc(S["up_ps"], 1)

                    def go_down(i, c):
                        src, name = (HO, "pool_mark") if gates is not None else (MO, "mult_out") if two else (AO, "act_out")
                        pe.wait_ge(S[name], d[name] + NCH * i + c + 1)
                        for j in range(TPC):
                            t = c * TPC + j
                            last = pe.matmul(PS[:, 4 + t // 2, (t % 2) * D:(t % 2 + 1) * D], src[:, c, j * P:(j + 1) * P],
                                             down(i), start=i == 0 and t % 2 == 0, stop=i == n - 1,
                                             skip_group_check=True)
                        last.then_inc(S["down_ps"], 1)

                    for c in range(NCH):
                        go_up(0, c)
                    for i in range(n):
                        for c in range(NCH):
                            if i + 1 < n:
                                go_up(i + 1, c)
                            go_down(i, c)

                @block.scalar
                def _(act):
                    for i in range(n):
                        for c in range(NCH):
                            act.wait_ge(S["up_ps"], d["up_ps"] + NCH * i + c + 1)
                            if i >= 1:
                                name = "mult_out" if two else "down_ps"
                                act.wait_ge(S[name], d[name] + NCH * (i - 1) + c + 1)
                            if two:
                                ins = act.activation(AO[:, c], PS[:, 2 * c, :], ACT.Silu,
                                                     scale=1.0 if scales is None else scales[:, 0:1])
                            else:
                                ins = act.activation(AO[:, c], PS[:, 2 * c, :], ACT.Gelu_apprx_tanh, bias=bias[:, i:i + 1])
                            ins.then_inc(S["act_out"], 1)

                @block.vector
                def _(dve):
                    if two:
                        for i in range(n):
                            for c in range(NCH):
                                dve.wait_ge(S["act_out"], d["act_out"] + NCH * i + c + 1)
                                if i >= 1:
                                    name = "pool_mark" if gates is not None else "down_ps"
                                    dve.wait_ge(S[name], d[name] + NCH * (i - 1) + c + 1)
                                if scales is None:
                                    ins = dve.tensor_tensor(MO[:, c], PS[:, 2 * c + 1, :], AO[:, c], ALU.mult)
                                else:
                                    ins = dve.scalar_tensor_tensor(MO[:, c], PS[:, 2 * c + 1, :], scales[:, 1:2],
                                                                   AO[:, c], ALU.mult, ALU.mult)
                                ins.then_inc(S["mult_out"], 1)
                    dve.wait_ge(S["down_ps"], d["down_ps"] + NCH * n)
                    if bias is not None:
                        dve.wait_ge(S["pool_mark"], d["pool_mark"] + 1)
                    for g in range(TT // 2):
                        v = X[:, 2 * g:2 * g + 2, :]
                        ps = PS[:, 4 + g, :].rearrange("p (t n) -> p t n", t=2)
                        if scales is None:
                            dve.tensor_tensor(v, ps, v, ALU.add)
                        else:
                            dve.scalar_tensor_tensor(v, ps, scales[:, 2:3], v, ALU.mult, ALU.add)

                if bias is not None:
                    @block.gpsimd
                    def _(pool):
                        row = rv("b_dn0").rearrange("p (a n) -> p a n", a=1).to_broadcast([P, TT, D])
                        pool.tensor_tensor(X[:], X[:], row, ALU.add).then_inc(S["pool_mark"], 1)

                if gates is not None:
                    @block.gpsimd
                    def _(pool):
                        for i in range(n):
                            for c in range(NCH):
                                pool.wait_ge(S["mult_out"], d["mult_out"] + NCH * i + c + 1)
                                if c == 0:
                                    pool.wait_ge(S[f"g_slot{i % RINGG}"], 32 * (i // RINGG + 1))
                                if i >= 1:
                                    pool.wait_ge(S["down_ps"], d["down_ps"] + NCH * (i - 1) + c + 1)
                                pool.tensor_tensor(HO[:, c], MO[:, c], gates(i)[:, c * CH:(c + 1) * CH],
                                                   ALU.mult).then_inc(S["pool_mark"], 1)
            for name, k in (("up_ps", NCH * n), ("down_ps", NCH * n), ("act_out", NCH * n),
                            ("mult_out", NCH * n if two else 0),
                            ("pool_mark", NCH * n if gates is not None else 1 if bias is not None else 0)):
                done[name] += k

    def mixing():
        tag = str(nc.next_id())
        NB_ = KD * B
        with ExitStack() as st:
            def tmp(name, shape, dt=F32):
                return st.enter_context(nc.sbuf_tensor(name + tag, shape, dt))
            N = tmp("N", [P, TT, D])
            AP_ = tmp("AP", [P, KD, B, T + 1])
            DF = tmp("DF", [P, KD, B, T])
            XM = tmp("XM", [P, KD, B, T])
            RR = tmp("RR", [P, KD, B * T])
            EK = tmp("EK", [P, KD, B * T])
            TM = tmp("TM", [P, 2, CH])

            def to_padded(k, g):
                return AP_[:, k, g, 1:T + 1]

            cur = AP_[:, :, :, 1:T + 1]
            prev = AP_[:, :, :, 0:T]
            flat = lambda a: a.rearrange("p b t -> p (b t)")

            def differences(zero):
                with nc.Block() as block:
                    @block.vector
                    def _(dve):
                        if zero:
                            dve.memset(AP_[:, :, :, 0:1], 0.0).then_inc(S["dve_mark"], 1)
                        else:
                            dve.tensor_tensor(DF[:], cur, prev, ALU.subtract)
                done["dve_mark"] += zero

            def mixed(mu, w, out, func):
                d = dict(done)
                with nc.Block() as block:
                    @block.vector
                    def _(dve):
                        for k in range(KD):
                            dve.scalar_tensor_tensor(XM[:, k], DF[:, k], mu[:, k:k + 1], prev[:, k], ALU.mult,
                                                     ALU.add).then_inc(S["dve_mark"], 1)
                        if func[0] == "dve":
                            for n in range(KD * NCH):
                                dve.wait_ge(S["up_ps"], d["up_ps"] + n + 1)
                                func[1](dve, n // NCH, n % NCH, PS[:, n, :])

                    @block.tensor
                    def _(pe):
                        pe.wait_ge(S["dve_mark"], d["dve_mark"] + KD)
                        for n in range(KD * NCH):
                            j, c = n // NCH, n % NCH
                            for k in range(KD):
                                last = pe.matmul(PS[:, n, :], w[:, k, j * P:(j + 1) * P],
                                                 flat(XM[:, k])[:, c * CH:(c + 1) * CH], start=k == 0, stop=k == KD - 1)
                            last.then_inc(S["up_ps"], 1)

                    if func[0] == "act":
                        @block.scalar
                        def _(act):
                            for n in range(KD * NCH):
                                act.wait_ge(S["up_ps"], d["up_ps"] + n + 1)
                                j, c = n // NCH, n % NCH
                                act.activation(out[:, j, c * CH:(c + 1) * CH], PS[:, n, :], func[1],
                                               **({} if func[2] is None else {"bias": func[2][:, j:j + 1]}))
                done["dve_mark"] += KD
                done["up_ps"] += KD * NCH

            def wkv(dve, j, c, ps):
                L = lambda ins: link(dve, ins, "dve_chain")
                r_, e_ = (a[:, j, c * CH:(c + 1) * CH] for a in (RR, EK))
                L(dve.tensor_tensor(r_, r_, e_, ALU.mult))
                L(dve.tensor_scalar(e_, e_, 1e-8, None, ALU.add))
                L(dve.reciprocal(TM[:, 0], e_))
                L(dve.tensor_tensor(TM[:, 0], TM[:, 0], ps, ALU.mult))
                L(dve.tensor_tensor(r_, r_, TM[:, 0], ALU.mult))

            def squares(dve, j, c, ps):
                L = lambda ins: link(dve, ins, "dve_chain")
                e_ = EK[:, j, c * CH:(c + 1) * CH]
                L(dve.tensor_scalar(e_, ps, 0.0, None, ALU.max))
                dve.tensor_tensor(e_, e_, e_, ALU.mult)

            differences(True)
            layernorm(H, N, to_padded, vv("ln1_g"), vv("ln1_b"))
            differences(False)
            mixed(vv("mu_r"), wA("wr", KD), RR, ("act", ACT.Sigmoid, None))
            mixed(vv("mu_k"), wA("wk", KD), EK, ("act", ACT.Exp, vv("u")))
            mixed(vv("mu_v"), wA("wv", KD), None, ("dve", wkv))
            add_rows(lambda k, t: RR[:, k, t * P:(t + 1) * P], lambda k: wA("wout", KD)[:, k, :], KD, dst=H)
            layernorm(H, N, to_padded, vv("ln2_g"), vv("ln2_b"))
            differences(False)
            mixed(vv("cmu_k"), wA("ck", KD), None, ("dve", squares))
            d = dict(done)
            with nc.Block() as block:
                @block.vector
                def _(dve):
                    for k in range(KD):
                        dve.scalar_tensor_tensor(XM[:, k], DF[:, k], vv("cmu_r")[:, k:k + 1], prev[:, k], ALU.mult,
                                                 ALU.add).then_inc(S["dve_mark"], 1)

                @block.tensor
                def _(pe):
                    pe.wait_ge(S["dve_mark"], d["dve_mark"] + KD)
                    for t in range(TT):
                        for k in range(KD):
                            last = pe.matmul(PS[:, t, 0:D], flat(XM[:, k])[:, t * P:(t + 1) * P], wA("cr", KD)[:, k, :],
                                             start=k == 0, stop=k == KD - 1)
                        last.then_inc(S["up_ps"], 1)

                @block.scalar
                def _(act):
                    for t in range(TT):
                        act.wait_ge(S["up_ps"], d["up_ps"] + t + 1)
                        act.activation(N[:, t, :], PS[:, t, 0:D], ACT.Sigmoid)
            done["dve_mark"] += KD
            done["up_ps"] += TT

            def gated(dve, t, d):
                L = lambda ins: link(dve, ins, "dve_chain")
                L(dve.tensor_tensor(N[:, t, :], N[:, t, :], PS[:, t, 0:D], ALU.mult))
                L(dve.tensor_tensor(H[:, t, :], H[:, t, :], N[:, t, :], ALU.add))
                dve.tensor_tensor(X[:, t, :], X[:, t, :], H[:, t, :], ALU.add).then_inc(S["x_added"], 1)

            add_rows(lambda k, t: EK[:, k, t * P:(t + 1) * P], lambda k: wA("cv", KD)[:, k, :], KD, mult=gated)

    def route(E, extra, weights, logits_of, gates_of, G, GT):
        EW = E + extra
        tag = str(nc.next_id())
        d = dict(done)
        with ExitStack() as st:
            def tmp(name, shape, dt=F32):
                return st.enter_context(nc.sbuf_tensor(name + tag, shape, dt))
            LG, PRB, RK = (tmp(x, [P, TT, E]) for x in ("LG", "PRB", "RK"))
            C1, C2 = (tmp(x, [P, TT, E, E]) for x in ("CA", "CB"))
            r1, r2 = (tmp(x, [P, TT]) for x in ("ra", "rb"))
            wide = lambda a: a[:].rearrange("p (t e) -> p t e", e=1).to_broadcast([P, TT, E])
            with nc.Block() as block:
                @block.tensor
                def _(pe):
                    for t in range(TT):
                        for k in range(KD):
                            last = pe.matmul(PS[:, 0, t * EW:(t + 1) * EW], HT[:, k, t * P:(t + 1) * P], weights[:, k, :],
                                             start=k == 0, stop=k == KD - 1)
                    last.then_inc(S["pe_mark"], 1)
                    pe.wait_ge(S["gates"], d["gates"] + 1)
                    for t in range(TT):
                        last = pe.transpose(PS[0:EW, 1 + t // 4, (t % 4) * P:(t % 4 + 1) * P], G[:, t, :], ident)
                    last.then_inc(S["turned"], 1)

                @block.scalar
                def _(act):
                    act.wait_ge(S["dve_mark"], d["dve_mark"] + 1)
                    act.activation(PRB[:], PRB[:], ACT.Exp).then_inc(S["act_mark"], 1)
                    if extra:
                        ps = PS[:, 0, 0:TT * EW].rearrange("p (t e) -> p t e", e=EW)
                        act.activation(G[:, :, E:EW], ps[:, :, E:EW], ACT.Sigmoid).then_inc(S["act_mark"], 1)
                    else:
                        act.wait_ge(S["dve_mark"], d["dve_mark"] + 2)
                        act.activation(LG[:], LG[:], ACT.Exp).then_inc(S["act_mark"], 1)

                @block.vector
                def _(dve):
                    L = lambda ins: link(dve, ins, "dve_chain")
                    dve.wait_ge(S["pe_mark"], d["pe_mark"] + 1)
                    ps = PS[:, 0, 0:TT * EW].rearrange("p (t e) -> p t e", e=EW)
                    logits_of(dve, L, LG, ps[:, :, 0:E])
                    L(dve.tensor_reduce(r1[:], LG[:], AX, ALU.max))
                    dve.tensor_tensor(PRB[:], LG[:], wide(r1), ALU.subtract).then_inc(S["dve_mark"], 1)
                    dve.wait_ge(S["act_mark"], d["act_mark"] + 1)
                    L(dve.tensor_reduce(r1[:], PRB[:], AX, ALU.add))
                    L(dve.reciprocal(r1[:], r1[:]))
                    L(dve.tensor_tensor(PRB[:], PRB[:], wide(r1), ALU.mult))
                    mine = PRB[:].rearrange("p t (e a) -> p t e a", a=1).to_broadcast([P, TT, E, E])
                    theirs = PRB[:].rearrange("p t (a e) -> p t a e", a=1).to_broadcast([P, TT, E, E])
                    low = cst(f"lower{E}").rearrange("p (a e f) -> p a (e f)", a=1, e=E).to_broadcast([P, TT, E * E])
                    L(dve.tensor_tensor(C1[:], theirs, mine, ALU.is_gt))
                    L(dve.tensor_tensor(C2[:], theirs, mine, ALU.is_equal))
                    c2 = C2[:].rearrange("p t e f -> p t (e f)")
                    L(dve.tensor_tensor(c2, c2, low, ALU.mult))
                    L(dve.tensor_tensor(C1[:], C1[:], C2[:], ALU.add))
                    L(dve.tensor_reduce(RK[:], C1[:], AX, ALU.add))
                    gates_of(dve, L, PRB, RK, LG, r1, r2, wide, d)
                    dve.wait_ge(S["turned"], d["turned"] + 1)
                    L(dve.tensor_copy(GT[0:EW, :].rearrange("p (a n) -> p a n", a=2), PS[0:EW, 1:3, :]))
            done["pe_mark"] += 1
            done["gates"] += 1
            done["turned"] += 1
            done["act_mark"] += 2
            done["dve_mark"] += 1 if extra else 2

    def experts1():
        NF = sum(FB1)
        tag = str(nc.next_id())
        owner = [e for e in range(E1) for _ in range(FB1[e])]
        with ExitStack() as st:
            def tmp(name, shape, dt=F32):
                return st.enter_context(nc.sbuf_tensor(name + tag, shape, dt))
            G = tmp("G", [P, TT, E1])
            GT = tmp("GT", [P, B * T])
            GH = tmp("GH", [P, B * T])
            GX = H[:].rearrange("p t d -> p (t d)").rearrange("p (k n) -> p k n", k=KD)
            GB = tmp("GB", [P, E1, B * T])
            gb1 = tmp("gb1", [P, NF])
            cc = tmp("cc", [P, 4])
            HA = tmp("HA", [P, 4, CH])
            HB = tmp("HB", [P, 4, CH])
            MT = tmp("MT", [P, B * T])

            def logits_of(dve, L, LG, ps):
                row = rv("b_router").rearrange("p (a e) -> p a e", a=1).to_broadcast([P, TT, E1])
                cost = cst("cost").rearrange("p (a e) -> p a e", a=1).to_broadcast([P, TT, E1])
                L(dve.tensor_tensor(LG[:], ps, row, ALU.add))
                L(dve.tensor_tensor(LG[:], LG[:], cost, ALU.subtract))

            def gates_of(dve, L, PRB, RK, LG, r1, r2, wide, d):
                L(dve.tensor_reduce(r2[:], PRB[:], AX, ALU.max))
                dve.tensor_tensor(LG[:], PRB[:], wide(r2), ALU.subtract).then_inc(S["dve_mark"], 1)
                dve.wait_ge(S["act_mark"], d["act_mark"] + 2)
                L(dve.scalar_tensor_tensor(LG[:], RK[:], 2.0, LG[:], ALU.is_lt, ALU.mult))
                L(dve.tensor_reduce(r2[:], LG[:], AX, ALU.add))
                L(dve.reciprocal(r2[:], r2[:]))
                dve.tensor_tensor(G[:], LG[:], wide(r2), ALU.mult).then_inc(S["gates"], 1)

            route(E1, 0, wB("router", KD), logits_of, gates_of, G, GT)
            d = dict(done)
            n_all = NF + 1
            work = [(f, c) for f in range(n_all) for c in range(NCH)]
            with nc.Block() as block:
                @block.sync
                def _(sp):
                    sp.dma_start(gate_rows[0:E1, :], GT[0:E1, :]).then_inc(S["gates_sent"], 16)
                    sp.wait_ge(S["gates_sent"], d["gates_sent"] + 16)
                    sp.dma_start(GB[:], gate_rows[0:E1, :].rearrange("(a e) n -> a e n", a=1).to_broadcast([P, E1, B * T])
                                 ).then_inc(S["gates_back"], 16)

                @block.tensor
                def _(pe):
                    for c in range(NCH):
                        for k in range(KD):
                            last = pe.matmul(PS[:, 2 + c, :], wB("down", KD)[:, k, :], HT[:, k, c * CH:(c + 1) * CH],
                                             start=k == 0, stop=k == KD - 1)
                        last.then_inc(S["proj"], 1)

                    def go_up(n):
                        f, c = work[n]
                        if n >= 2:
                            pe.wait_ge(S["act_out"], d["act_out"] + n - 1)
                        w = wB("w1")[:, f * P:(f + 1) * P] if f < NF else wB("sh1")
                        pe.matmul(PS[:, n % 2, :], w, GH[:, c * CH:(c + 1) * CH], start=True, stop=True).then_inc(S["up_ps"], 1)

                    def go_down(n):
                        f, c = work[n]
                        pe.wait_ge(S["mult_out"], d["mult_out"] + n + 1)
                        w = wB("w2")[:, f * P:(f + 1) * P] if f < NF else wB("sh2")
                        pe.matmul(PS[:, 4 + c, :], w, HB[:, n % 4, :], start=f == 0, stop=f == n_all - 1
                                  ).then_inc(S["down_ps"], 1)

                    pe.wait_ge(S["act_mark"], d["act_mark"] + 2)
                    go_up(0)
                    go_up(1)
                    pe.wait_ge(S["act_mark"], d["act_mark"] + 3)
                    for f in range(NF):
                        last = pe.matmul(PS[:, 6, 0:1], wB("w2")[:, f * P:(f + 1) * P], gb1[:, f:f + 1],
                                         start=f == 0, stop=f == NF - 1)
                    last.then_inc(S["pe_mark"], 1)
                    for n in range(len(work)):
                        if n + 2 < len(work):
                            go_up(n + 2)
                        go_down(n)
                    pe.wait_ge(S["dve_mark"], d["dve_mark"] + 1)
                    pe.wait_ge(S["act_mark"], d["act_mark"] + 4)
                    for t in range(TT):
                        bank = PS[:, t % 4, 0:D]
                        if t >= 4:
                            pe.wait_ge(S["x_added"], d["x_added"] + t - 3)
                        pe.matmul(bank, MT[:, t * P:(t + 1) * P], wB("up"), start=True, stop=False)
                        for k in range(KD):
                            last = pe.matmul(bank, GX[:, k, t * P:(t + 1) * P], wB("core", KD)[:, k, :],
                                             start=False, stop=k == KD - 1)
                        last.then_inc(S["o_proj"], 1)

                @block.scalar
                def _(act):
                    for c in range(NCH):
                        act.wait_ge(S["proj"], d["proj"] + c + 1)
                        act.activation(GH[:, c * CH:(c + 1) * CH], PS[:, 2 + c, :], ACT.Gelu,
                                       bias=vv("b_down1")).then_inc(S["act_mark"], 1)
                    act.activation(gb1[:], vv("b1"), ACT.Gelu).then_inc(S["act_mark"], 1)
                    act.activation(GX, HT[:], ACT.Gelu).then_inc(S["act_mark"], 1)
                    for n, (f, c) in enumerate(work):
                        act.wait_ge(S["up_ps"], d["up_ps"] + n + 1)
                        if n >= 4:
                            act.wait_ge(S["mult_out"], d["mult_out"] + n - 3)
                        b = vv("b1")[:, f:f + 1] if f < NF else vv("b_sh1")
                        act.activation(HA[:, n % 4, :], PS[:, n % 2, :], ACT.Gelu, bias=b).then_inc(S["act_out"], 1)

                @block.gpsimd
                def _(pool):
                    for i, name in enumerate(("b_up1", "b_core")):
                        row = rv(name).rearrange("p (a n) -> p a n", a=1).to_broadcast([P, TT, D])
                        if i:
                            pool.wait_ge(S["pool_mark"], d["pool_mark"] + 1)
                        pool.tensor_tensor(X[:], X[:], row, ALU.add).then_inc(S["pool_mark"], 1)

                @block.vector
                def _(dve):
                    L = lambda ins: link(dve, ins, "dve_chain")
                    dve.wait_ge(S["act_mark"], d["act_mark"] + 3)
                    dve.wait_ge(S["gates_back"], d["gates_back"] + 16)
                    for n, (f, c) in enumerate(work):
                        dve.wait_ge(S["act_out"], d["act_out"] + n + 1)
                        if n >= 4:
                            dve.wait_ge(S["down_ps"], d["down_ps"] + n - 3)
                        if f < NF:
                            ins = dve.scalar_tensor_tensor(HB[:, n % 4, :], HA[:, n % 4, :], gb1[:, f:f + 1],
                                                           GB[:, owner[f], c * CH:(c + 1) * CH], ALU.subtract, ALU.mult)
                        else:
                            ins = dve.tensor_scalar(HB[:, n % 4, :], HA[:, n % 4, :], 0.1, None, ALU.mult)
                        ins.then_inc(S["mult_out"], 1)
                    L(dve.tensor_reduce(cc[:, 0:1], vv("b2"), AX, ALU.add))
                    L(dve.scalar_tensor_tensor(cc[:, 1:2], vv("b_sh2"), 0.1, cc[:, 0:1], ALU.mult, ALU.add))
                    dve.wait_ge(S["pe_mark"], d["pe_mark"] + 1)
                    L(dve.tensor_tensor(cc[:, 2:3], PS[:, 6, 0:1], cc[:, 1:2], ALU.add))
                    dve.wait_ge(S["down_ps"], d["down_ps"] + len(work))
                    dve.tensor_scalar(MT[:].rearrange("p (a n) -> p a n", a=2), PS[:, 4:6, :], cc[:, 2:3], None,
                                      ALU.add).then_inc(S["dve_mark"], 1)
                    dve.wait_ge(S["pool_mark"], d["pool_mark"] + 2)
                    for t in range(TT):
                        dve.wait_ge(S["o_proj"], d["o_proj"] + t + 1)
                        dve.tensor_tensor(X[:, t, :], X[:, t, :], PS[:, t % 4, 0:D], ALU.add).then_inc(S["x_added"], 1)
            for name, k in (("gates_sent", 16), ("gates_back", 16), ("proj", NCH), ("up_ps", len(work)),
                            ("act_out", len(work)), ("mult_out", len(work)), ("down_ps", len(work)), ("pe_mark", 1),
                            ("act_mark", 4), ("dve_mark", 1), ("pool_mark", 2), ("o_proj", TT), ("x_added", TT)):
                done[name] += k

    def experts2():
        tag = str(nc.next_id())
        with ExitStack() as st:
            def tmp(name, shape, dt=F32):
                return st.enter_context(nc.sbuf_tensor(name + tag, shape, dt))
            G = tmp("G", [P, TT, E2 + 1])
            GT = tmp("GT", [P, B * T])
            W2 = tmp("W2", [P, RING2, 3 * D])
            GR = tmp("GR", [P, RINGG, B * T])

            def logits_of(dve, L, LG, ps):
                L(dve.tensor_copy(LG[:], ps))

            def gates_of(dve, L, PRB, RK, LG, r1, r2, wide, d):
                L(dve.scalar_tensor_tensor(LG[:], RK[:], 4.0, PRB[:], ALU.is_lt, ALU.mult))
                L(dve.tensor_reduce(r2[:], LG[:], AX, ALU.add))
                L(dve.tensor_scalar(r2[:], r2[:], 1e-9, None, ALU.max))
                L(dve.reciprocal(r2[:], r2[:]))
                dve.wait_ge(S["act_mark"], d["act_mark"] + 2)
                dve.tensor_tensor(G[:, :, 0:E2], LG[:], wide(r2), ALU.mult).then_inc(S["gates"], 1)

            route(E2, 1, wL("router2", KD), logits_of, gates_of, G, GT)

            def load(sp, d):
                sp.dma_start(gate_rows[:, :], GT[0:E2 + 1, :]).then_inc(S["gates_sent"], 16)

                def weights(i):
                    if i >= RING2:
                        sp.wait_ge(S["down_ps"], d["down_ps"] + NCH * (i - RING2 + 1))
                    sp.dma_start(W2[:, i % RING2, :], w2f[i]).then_inc(S[f"w_slot{i % RING2}"], 16)

                def gates(i):
                    if i >= RINGG:
                        sp.wait_ge(S["pool_mark"], d["pool_mark"] + NCH * (i - RINGG + 1))
                    owner = [min((i * P + r) // I2, E2) for r in range(P)]
                    cut = next((r for r in range(P) if owner[r] != owner[0]), P // 2)
                    for lo, hi in ((0, cut), (cut, P)):
                        e = owner[lo]
                        sp.dma_start(GR[lo:hi, i % RINGG, :], gate_rows[e:e + 1, :].to_broadcast([hi - lo, B * T])
                                     ).then_inc(S[f"g_slot{i % RINGG}"], 16)

                for i in range(NI2):
                    weights(i)
                    if i == 0:
                        sp.wait_ge(S["gates_sent"], d["gates_sent"] + 16)
                    gates(i)

            chunk = lambda i, j: W2[:, i % RING2, j * D:(j + 1) * D]
            mlp(NI2, up=lambda i, k: chunk(i, 0)[:, k * P:(k + 1) * P], gate=lambda i, k: chunk(i, 1)[:, k * P:(k + 1) * P],
                down=lambda i: chunk(i, 2), mode="silu", load=load, gates=lambda i: GR[:, i % RINGG, :])
            done["gates_sent"] += 16

    def wkv_scan():
        NS = KD * B
        d = dict(done)
        tag = str(nc.next_id())
        with ExitStack() as st:
            def tmp(name, shape, dt=F32):
                return st.enter_context(nc.sbuf_tensor(name + tag, shape, dt))
            O, PN, QN = (tmp(x, [P, NS, T + 1]) for x in ("O", "PN", "QN"))
            A2, E2_, EV, A1 = (tmp(x, [P, NS, T]) for x in ("A2", "E2", "EV", "A1"))
            K = HT[:].rearrange("p k (b t) -> p (k b) t", t=T)
            V = CXT[:].rearrange("p k (b t) -> p (k b) t", t=T)
            w, u = vv("w3"), vv("u3")
            half = lambda a, k: a[:, k * B:(k + 1) * B]
            old, new = (lambda a: a[:, :, 0:T]), (lambda a: a[:, :, 1:T + 1])
            with nc.Block() as block:
                @block.vector
                def _(dve):
                    L = lambda ins: link(dve, ins, "dve_chain")
                    dve.memset(O[:, :, 0:1], -1e38)
                    dve.memset(PN[:, :, 0:1], 0.0)
                    L(dve.memset(QN[:, :, 0:1], 0.0))
                    for s in range(NS):
                        k = s // B
                        ins = dve.tensor_tensor_scan(O[:, s, 1:T + 1], w[:, k:k + 1].to_broadcast([P, T]), K[:, s, :], -1e38,
                                                     ALU.add, ALU.max)
                    L(ins)
                    dve.tensor_tensor(E2_[:], K, new(O), ALU.subtract).then_inc(S["dve_mark"], 1)
                    for k in range(KD):
                        ins = dve.scalar_tensor_tensor(half(A2, k), half(old(O), k), w[:, k:k + 1], half(new(O), k),
                                                       ALU.add, ALU.subtract)
                    ins.then_inc(S["dve_mark"], 1)
                    dve.wait_ge(S["act_mark"], d["act_mark"] + 1)
                    L(dve.tensor_tensor(EV[:], E2_[:], V, ALU.mult))
                    dve.wait_ge(S["act_mark"], d["act_mark"] + 2)
                    for s in range(NS):
                        dve.tensor_tensor_scan(PN[:, s, 1:T + 1], A2[:, s, :], EV[:, s, :], 0.0, ALU.mult, ALU.add)
                        ins = dve.tensor_tensor_scan(QN[:, s, 1:T + 1], A2[:, s, :], E2_[:, s, :], 0.0, ALU.mult, ALU.add)
                    L(ins)
                    for k in range(KD):
                        ins = dve.scalar_tensor_tensor(half(EV, k), half(K, k), u[:, k:k + 1], half(old(O), k), ALU.add, ALU.max)
                    L(ins)
                    dve.tensor_tensor(A1[:], old(O), EV[:], ALU.subtract).then_inc(S["dve_mark"], 1)
                    for k in range(KD):
                        ins = dve.scalar_tensor_tensor(half(E2_, k), half(K, k), u[:, k:k + 1], half(EV, k), ALU.add, ALU.subtract)
                    ins.then_inc(S["dve_mark"], 1)
                    dve.wait_ge(S["act_mark"], d["act_mark"] + 3)
                    L(dve.tensor_tensor(A2[:], A1[:], old(PN), ALU.mult))
                    L(dve.tensor_tensor(A1[:], A1[:], old(QN), ALU.mult))
                    dve.wait_ge(S["act_mark"], d["act_mark"] + 4)
                    L(dve.tensor_tensor(EV[:], E2_[:], V, ALU.mult))
                    L(dve.tensor_tensor(A2[:], A2[:], EV[:], ALU.add))
                    L(dve.tensor_tensor(A1[:], A1[:], E2_[:], ALU.add))
                    L(dve.reciprocal(A1[:], A1[:]))
                    dve.tensor_tensor(A2[:], A2[:], A1[:], ALU.mult).then_inc(S["dve_mark"], 1)
                    for g in range(TT // 2):
                        dve.wait_ge(S["turned"], d["turned"] + g + 1)
                        v = X[:, 2 * g:2 * g + 2, :].rearrange("p t d -> p (t d)")
                        dve.tensor_tensor(v, v, PS[:, g, :], ALU.add)

                @block.scalar
                def _(act):
                    for n, a in enumerate((E2_, A2, A1, E2_)):
                        act.wait_ge(S["dve_mark"], d["dve_mark"] + n + 1)
                        act.activation(a[:], a[:], ACT.Exp).then_inc(S["act_mark"], 1)

                @block.tensor
                def _(pe):
                    pe.wait_ge(S["dve_mark"], d["dve_mark"] + 5)
                    for g in range(TT // 2):
                        for j in range(2):
                            for k in range(KD):
                                last = pe.transpose(PS[:, g, j * D + k * P:j * D + (k + 1) * P],
                                                    A2[:, k * B + g, j * P:(j + 1) * P], ident)
                        last.then_inc(S["turned"], 1)
            done["dve_mark"] += 5
            done["act_mark"] += 4
            done["turned"] += TT // 2

    def ternary(SC):
        d = dict(done)
        tag = str(nc.next_id())
        with ExitStack() as st:
            def tmp(name, shape, dt=F32):
                return st.enter_context(nc.sbuf_tensor(name + tag, shape, dt))
            AB = tmp("AB", [P, 2, 2048])
            rs = tmp("rs", [P, 4])
            th = tmp("th", [P, 2, 4])
            mats = [wL(x) for x in ("up3", "gate3", "dn3")]
            with nc.Block() as block:
                @block.scalar
                def _(act):
                    for j, w in enumerate(mats):
                        if j == 0:
                            act.wait_ge(S["late_in"], 16)
                        if j == 2:
                            act.wait_ge(S["dve_mark"], d["dve_mark"] + 1)
                        act.activation(AB[:, j % 2], w, ACT.Abs).then_inc(S["act_mark"], 1)

                @block.tensor
                def _(pe):
                    pe.wait_ge(S["dve_mark"], d["dve_mark"] + 3)
                    pe.matmul(PS[:, 0, 0:3], cst("ones"), rs[:, 0:3], start=True, stop=True).then_inc(S["pe_mark"], 1)

                @block.vector
                def _(dve):
                    L = lambda ins: link(dve, ins, "dve_chain")
                    for j in range(3):
                        dve.wait_ge(S["act_mark"], d["act_mark"] + j + 1)
                        dve.tensor_reduce(rs[:, j:j + 1], AB[:, j % 2], AX, ALU.add).then_inc(S["dve_mark"], 1)
                    dve.wait_ge(S["dve_mark"], d["dve_mark"] + 3)
                    dve.wait_ge(S["pe_mark"], d["pe_mark"] + 1)
                    L(dve.tensor_scalar(SC[:, 0:3], PS[:, 0, 0:3], 1.0 / (F3 * D), 1e-8, ALU.mult, ALU.add))
                    L(dve.tensor_scalar(th[:, 0, 0:3], SC[:, 0:3], 0.5, None, ALU.mult))
                    L(dve.tensor_scalar(th[:, 1, 0:3], SC[:, 0:3], -0.5, None, ALU.mult))
                    for j, w in enumerate(mats):
                        L(dve.tensor_scalar(AB[:, 0], w, th[:, 1, j:j + 1], None, ALU.is_lt))
                        L(dve.scalar_tensor_tensor(w, w, th[:, 0, j:j + 1], AB[:, 0], ALU.is_gt, ALU.subtract))
            done["act_mark"] += 3
            done["dve_mark"] += 3
            done["pe_mark"] += 1

    load_all()
    stop = STOP

    def store():
        with nc.Block() as block:
            @block.sync
            def _(sp):
                sp.dma_start(tok(out), X[:]).then_inc(S["out_done"], 16)
                sp.wait_ge(S["out_done"], 16)

    def layers():
        layernorm(X, H, to_HT, first=True)
        self_attention(0, {"q": wA("q0", KD), "qp": wA("qp0", KD), "k": wA("k0", KD), "kp": wA("kp0", KD),
                           "v": wA("v0", KD), "o": wA("o0", 4)}, 4, 32, D ** -0.5, softcap=50.0,
                       arrived=(S["a_in"], 16))
        yield
        layernorm(X, H)
        cross_attention(32)
        yield
        quantise_fp4()
        layernorm(X, H, to_HT)
        up0 = wA("up0", KD)
        dn0 = wA("dn0", 8)
        with nc.Block() as block:
            @block.gpsimd
            def _(pool):
                pool.wait_ge(S["b_in"], 64)
        mlp(F0 // P, up=lambda i, k: up0[:, k, i * P:(i + 1) * P], gate=None, down=lambda i: dn0[:, i, :], mode="gelu",
            bias=vv("b_up0"))
        yield
        layernorm(X, H)
        mixing()
        yield
        with nc.Block() as block:
            @block.sync
            def _(sp):
                sp.dma_start(WA[:, 0:L_N], wl).then_inc(S["late_in"], 16)
        layernorm(X, H)
        cross_attention(32, gamma=rv("gamma"))
        yield
        layernorm(X, H, to_HT)
        experts1()
        yield
        layernorm(X, H, to_HT)
        self_attention(2, {"q": wL("q2", KD), "qp": wL("qp2", KD), "k": wL("k2", KD), "kp": wL("kp2", KD),
                           "v": wL("v2", KD), "o": wL("o2", KD)}, 2, 8, 8 ** -0.5, arrived=(S["late_in"], 16))
        yield
        layernorm(X, H)
        cross_attention(16)
        yield
        layernorm(X, H, to_HT)
        experts2()
        yield
        layernorm(X, H, to_HT)
        self_attention(3, {"q": wL("q3", KD), "qp": wL("qp3", KD), "k": wL("k3", KD), "kp": wL("kp3", KD),
                           "v": wL("v3", KD), "o": wL("o3", KD)}, 2, 16, 0.25)
        yield
        layernorm(X, H, to_HT)
        wkv_scan()
        yield
        SC = sb("SC", [P, 4])
        ternary(SC)
        layernorm(X, H, to_HT)
        up3, gate3, dn3 = wL("up3", KD), wL("gate3", KD), wL("dn3", 8)
        mlp(F3 // P, up=lambda i, k: up3[:, k, i * P:(i + 1) * P], gate=lambda i, k: gate3[:, k, i * P:(i + 1) * P],
            down=lambda i: dn3[:, i, :], mode="silu", scales=SC)
        yield

    for n, _ in enumerate(layers()):
        if n + 1 == stop:
            break
    store()
    es.close()


STOP = 12


def blocks(w):
    k = w.shape[0] // P
    return w.reshape(k, P, -1).transpose(1, 0, 2).reshape(P, -1)


def column_of(v):
    return v.reshape(-1, P).T


def swapped(w, hd, paired):
    i = np.arange(w.shape[1])
    h, dd = i // hd, i % hd
    other = dd ^ 1 if paired else (dd + hd // 2) % hd
    return w[:, h * hd + other]


def gqa(wq, wk, wv, wo, hd, group, paired):
    if hd == 32:
        order = [2 * (4 * kb + s) + r for kb in range(2) for r in range(2) for s in range(4)]
        cols = np.concatenate([np.arange(h * hd, (h + 1) * hd) for h in order])
        wq, wo = wq[:, cols], wo[cols]
    else:
        cols = np.concatenate([np.arange(h // group * hd, (h // group + 1) * hd) for h in range(D // hd)])
        wk, wv = wk[:, cols], wv[:, cols]
    return [blocks(a) for a in (wq, swapped(wq, hd, paired), wk, swapped(wk, hd, paired), wv, wo)]


def layout(i):
    n = {k: np.asarray(v) for k, v in i.items()}
    cat = lambda xs: np.ascontiguousarray(np.concatenate(xs, axis=1))
    g0 = gqa(n["L0_attn_Wq"], n["L0_attn_Wk"], n["L0_attn_Wv"], n["L0_attn_Wo"], 32, 2, False)
    wa = cat(g0 + [blocks(n["L0_ffn_up_kernel"].T), blocks(n["L0_ffn_down_kernel"].T)]
             + [blocks(n["L1_attn_" + k].T) for k in ("tm_Wr", "tm_Wk", "tm_Wv", "tm_Wout", "cm_Wr", "cm_Wk", "cm_Wv")])
    f = lambda k: n["L1_ffn_" + k]
    wb = cat([blocks(f("down_w")), blocks(f("up_w")), blocks(f("router_w")), f("shared_w1"), f("shared_w2"),
              blocks(f("core_w"))] + [f(f"e{e}_w1") for e in range(E1)] + [blocks(f(f"e{e}_w2")) for e in range(E1)])
    g2 = gqa(n["L2_attn_wq"], n["L2_attn_wk"], n["L2_attn_wv"], n["L2_attn_wo"], 8, 4, True)
    g3 = gqa(n["L3_attn_wq"], n["L3_attn_wk"], n["L3_attn_wv"], n["L3_attn_wo"], 16, 4, False)
    router2 = np.concatenate([n["L2_ffn_router_w"].T, n["L2_ffn_sh_gate_w"]], axis=1)
    wl = cat(g2 + g3 + [blocks(n["L3_ffn_W_up"].T), blocks(n["L3_ffn_W_gate"].T), blocks(n["L3_ffn_W_down"].T),
                        blocks(router2)])
    pad = NI2 * P - E2 * I2 - ISH
    wide = lambda w, s: np.concatenate([w.transpose(1, 0, 2).reshape(D, -1), s, np.zeros((D, pad), np.float32)], axis=1)
    gate, up = wide(n["L2_ffn_w_gate"], n["L2_ffn_sh_gate"]), wide(n["L2_ffn_w_up"], n["L2_ffn_sh_up"])
    down = np.concatenate([n["L2_ffn_w_down"].reshape(-1, D), n["L2_ffn_sh_down"], np.zeros((pad, D), np.float32)])
    halves = lambda w: w.reshape(KD, P, NI2, P).transpose(2, 1, 0, 3).reshape(NI2, P, KD * P)
    w2f = np.ascontiguousarray(np.concatenate([halves(gate), halves(up), down.reshape(NI2, P, D)], axis=2))
    a = lambda k: column_of(n["L1_attn_" + k])
    vec = cat([column_of(n["L0_ffn_up_bias"])] + [a(k) for k in ("ln1_g", "ln1_b", "ln2_g", "ln2_b", "tm_u", "tm_mu_r",
              "tm_mu_k", "tm_mu_v", "cm_mu_r", "cm_mu_k")]
              + [column_of(f(k)) for k in ("down_b", "shared_b1", "shared_b2")] + [column_of(f(f"e{e}_b1")) for e in range(E1)]
              + [column_of(f(f"e{e}_b2")) for e in range(E1)] + [column_of(n["L3_xattn_w"]), column_of(n["L3_xattn_u"])])
    rowv = cat([n["L0_ffn_down_bias"][None], f("up_b")[None], f("core_b")[None], f("router_b")[None],
                n["L1_xattn_gamma"].reshape(1, 1)])
    return {"x": n["x"], "ctx": n["ctx_2048"], "wa": wa, "wb": wb, "wl": wl, "w2f": w2f, "vec": vec, "rowv": rowv,
            "const": shape_constants()}


def kernel(**inputs):
    import concourse.bacc as bacc
    from concourse.bass_utils import run_bass_kernel_spmd

    nc = bacc.Bacc("TRN2", target_bir_lowering=False, num_devices=1)
    arrays = layout(inputs)
    aps = {k: nc.dram_tensor(k + "_in", a.shape, mybir.dt.from_np(a.dtype), kind="ExternalInput").ap()
           for k, a in arrays.items()}
    out = nc.dram_tensor("out", (B, T, D), F32, kind="ExternalOutput").ap()
    build_decoder(nc, out=out, **aps)
    r = run_bass_kernel_spmd(nc, [{k + "_in": a for k, a in arrays.items()}], core_ids=[0])
    return r.results[0]["out"]
```

```python
from contextlib import ExitStack

import numpy as np

import concourse.bass as bass
from concourse import mybir

F32 = mybir.dt.float32
BF16 = mybir.dt.bfloat16
U32 = mybir.dt.uint32
ALU = mybir.AluOpType
ACT = mybir.ActivationFunctionType
AX = mybir.AxisListType.X

P = 128
B, T, D = 4, 256, 256
TT = B * T // P
KD = D // P
CH = 512
NCH = B * T // CH
TPC = CH // P
EPS = 1e-5
NEG = -1e30

HID = [128, 256, 384, 512, 128, 256, 384, 512]
E1 = len(HID)
FB1 = [h // P for h in HID]
E2, I2, ISH = 16, 176, 704
NI2 = -(-(E2 * I2 + ISH) // P)
F3 = 1024
F0 = 1024

A_SIZES = {
    "q0": 2 * 512, "qp0": 2 * 512, "k0": 512, "kp0": 512, "v0": 512, "o0": 4 * 256,
    "upT0": 2048, "dnT0": 2048, "up0": 2048, "dn0": 2048,
    "wr": 512, "wk": 512, "wv": 512, "wout": 512, "cr": 512, "ck": 512, "cv": 512,
}
B_SIZES = {"down": KD * P, "up": D, "router": KD * E1, "sh1": P, "sh2": P, "core": KD * D,
           "w1": sum(HID), "w2": sum(FB1) * P}
L_SIZES = {"q2": 512, "qp2": 512, "k2": 512, "kp2": 512, "v2": 512, "o2": 512,
           "q3": 512, "qp3": 512, "k3": 512, "kp3": 512, "v3": 512, "o3": 512,
           "up3": 2048, "gate3": 2048, "dn3": 2048,
           "router2": KD * (E2 + 1)}
V_SIZES = {"b_up0": 8, "ln1_g": 2, "ln1_b": 2, "ln2_g": 2, "ln2_b": 2, "u": 2,
           "mu_r": 2, "mu_k": 2, "mu_v": 2, "cmu_r": 2, "cmu_k": 2,
           "b_down1": 1, "b_sh1": 1, "b_sh2": 1, "b1": sum(FB1), "b2": E1, "w3": 2, "u3": 2}
R_SIZES = {"b_dn0": D, "b_up1": D, "b_core": D, "b_router": E1, "gamma": 1}

PARTS_Q = (0, 0, 1, 0, 1, 2, 1, 2)
PARTS_K = (0, 1, 0, 2, 1, 0, 2, 1)
NSTACK = {8: 8, 16: 6}


def columns(sizes):
    at, n = {}, 0
    for name, size in sizes.items():
        at[name] = (n, size)
        n += size
    return at, n


A_AT, A_N = columns(A_SIZES)
B_AT, B_N = columns(B_SIZES)
L_AT, L_N = columns(L_SIZES)
V_AT, V_N = columns(V_SIZES)
R_AT, R_N = columns(R_SIZES)
RING2 = 4
RINGG = 2
RAW_A = ["q0", "qp0", "k0", "kp0", "v0", "o0", "upT0", "dnT0"]

C_SIZES = {"ident": P, "ones": P, "cos32": T, "sin32": T, "cos8": T, "sin8": T, "cos16": T, "sin16": T,
           "tril": P, "lower8": E1 * E1, "lower16": E2 * E2, "cost": E1, "eps": 1,
           "rows32": 4, "rows8": 16, "rows16": 8, "cols32": 32, "cols8": 4 * 32, "cols16": 2 * 32}
C_AT, C_N = columns(C_SIZES)


def shape_constants():
    c = np.zeros((P, C_N), np.float32)

    def put(name, a):
        at, n = C_AT[name]
        c[:, at:at + n] = np.asarray(a, np.float32).reshape(P, n)

    put("ident", np.eye(P))
    put("ones", np.ones((P, P)))
    pos = np.arange(T, dtype=np.float32)
    row = np.arange(P)
    for hd, paired in ((32, False), (8, True), (16, False)):
        inv = (np.float32(1.0) / np.float32(10000.0) ** (np.arange(0, hd, 2).astype(np.float32) / np.float32(hd))).astype(np.float32)
        ang = pos[None, :] * inv[:, None]
        d = row % hd
        freq = d // 2 if paired else d % (hd // 2)
        first = d % 2 == 0 if paired else d < hd // 2
        put(f"cos{hd}", np.cos(ang)[freq])
        put(f"sin{hd}", np.sin(ang)[freq] * np.where(first, -1.0, 1.0)[:, None])
        r = 32 // hd
        rows = np.zeros((P, r, 4))
        for s in range(4):
            for v in range(r):
                rows[32 * s + v * hd:32 * s + (v + 1) * hd, v, s] = 1.0
        put(f"rows{hd}", rows)
        cols = np.zeros((P, r, 32))
        for v in range(r):
            cols[:, v, v * hd:(v + 1) * hd] = 1.0
        put(f"cols{hd}", cols)
    put("tril", np.tril(np.ones((P, P))))
    for e in (E1, E2):
        put(f"lower{e}", np.broadcast_to(np.tril(np.ones((e, e)), -1), (P, e, e)))
    cost = np.float32(1e-07) * np.array([2 * P * h for h in HID], np.float32)
    put("cost", np.broadcast_to(cost, (P, E1)))
    put("eps", np.full((P, 1), EPS))
    return c


def build_decoder(nc, x, ctx, wa, wb, wl, w2f, vec, rowv, const, out):
    es = ExitStack()

    def sb(name, shape, dt=F32):
        return es.enter_context(nc.sbuf_tensor(name, shape, dt))

    def sem(name):
        return es.enter_context(nc.semaphore(name))

    X = sb("X", [P, TT, D])
    H = sb("H", [P, TT, D])
    HT = sb("HT", [P, KD, B * T])
    CX = sb("CX", [P, TT, D])
    CXT = sb("CXT", [P, KD, B * T])
    WA = sb("WA", [P, A_N])
    VEC = sb("VEC", [P, V_N])
    ROW = sb("ROW", [P, R_N])
    CST = sb("CST", [P, C_N])
    identb = sb("identb", [P, P], BF16)
    maskb = sb("maskb", [P, P], BF16)
    wb_store = ExitStack()
    WB = wb_store.enter_context(nc.sbuf_tensor("WB", [P, B_N], F32))
    PS = es.enter_context(nc.psum_tensor("PS", [P, 8, 512], F32))
    gate_rows = nc.dram_tensor("gate_rows", [E2 + 1, B * T], F32, kind="Internal").ap()
    q_parts, k_parts = (nc.dram_tensor(x, [3, D, B * T], BF16, kind="Internal").ap() for x in ("q_parts", "k_parts"))
    xq_parts, xk_parts = (nc.dram_tensor(x, [3, TT * P, D], BF16, kind="Internal").ap() for x in ("xq_parts", "xk_parts"))

    def part(store, at, name, k=None):
        a, n = at[name]
        v = store[:, a:a + n]
        return v if k is None else v.rearrange("p (k n) -> p k n", k=k)

    wA = lambda name, k=None: part(WA, A_AT, name, k)
    wB = lambda name, k=None: part(WB, B_AT, name, k)
    wL = lambda name, k=None: part(WA, L_AT, name, k)
    vv = lambda name: part(VEC, V_AT, name)
    rv = lambda name: part(ROW, R_AT, name)
    cst = lambda name, k=None: part(CST, C_AT, name, k)
    ident = cst("ident")

    def tok(a):
        return a.rearrange("b (h p) d -> p (b h) d", p=P)

    names = ["x_in0", "x_in1", "ctx_in", "const_in", "a_in", "b_in", "late_in", "ctx_turned", "ctx_copied", "masks_made",
             "stats", "moments", "std", "rstd", "normed", "turned", "turned_out",
             "q_staged", "k_staged", "v_staged", "scores", "row_max", "bias", "exps", "turn_a", "turn_b",
             "copied_a", "copied_b", "pv", "den_inv", "heads_out", "head_tmp", "masked",
             "proj", "proj_rot", "rot_free", "rope_cos", "rope_sin", "rope_sum", "v_proj", "v_out", "o_proj", "x_added",
             "up_ps", "act_out", "down_ps", "gate_ps", "mult_out", "dve_chain", "pool_chain", "act_chain", "pe_mark",
             "dve_mark", "act_mark", "pool_mark", "bias_in", "gates", "gates_sent", "gates_back",
             "part_h", "rest", "part_m", "part_l", "parts_out", "chunk_out0", "chunk_out1", "chunk_out2", "chunk_out3", "stacked0", "stacked1", "stacked2", "stacked3",
             "out_done"] + [f"w_slot{j}" for j in range(RING2)] + [f"g_slot{j}" for j in range(RINGG)]
    S = {n: sem(n) for n in names}
    done = dict.fromkeys(names, 0)

    def link(eng, ins, name):
        done[name] += 1
        ins.then_inc(S[name], 1)
        eng.wait_ge(S[name], done[name])

    def load_all():
        with nc.Block() as block:
            @block.sync
            def _(sp):
                half = TT // 2
                sp.dma_start(X[:, 0:half, :], tok(x)[:, 0:half, :]).then_inc(S["x_in0"], 16)
                sp.dma_start(X[:, half:TT, :], tok(x)[:, half:TT, :]).then_inc(S["x_in1"], 16)
                sp.dma_start(CST[:], const).then_inc(S["const_in"], 16)
                raw = sum(A_SIZES[n] for n in RAW_A)
                last = A_AT["wr"][0]
                sp.dma_start(WA[:, 0:raw], wa[:, 0:raw]).then_inc(S["a_in"], 16)
                sp.dma_start(CX[:], tok(ctx)).then_inc(S["ctx_in"], 16)
                sp.dma_start(VEC[:], vec).then_inc(S["b_in"], 16)
                sp.dma_start(ROW[:], rowv.to_broadcast([P, R_N])).then_inc(S["b_in"], 16)
                sp.dma_start(WA[:, last:A_N], wa[:, raw:]).then_inc(S["b_in"], 16)
                sp.dma_start(WB[:], wb).then_inc(S["b_in"], 16)

    def turn_context():
        with nc.Block() as block:
            @block.vector
            def _(dve):
                dve.tensor_copy(identb[:], ident)
                dve.tensor_scalar(maskb[:], cst("tril"), -1.0, -NEG, ALU.add, ALU.mult)

            @block.tensor
            def _(pe):
                pe.wait_ge(S["ctx_in"], 16)
                for g in range(TT // 2):
                    for k in range(KD):
                        for j in range(2):
                            last = pe.transpose(PS[:, g, k * 256 + j * P:k * 256 + (j + 1) * P],
                                                CX[:, 2 * g + j, k * P:(k + 1) * P], ident)
                    last.then_inc(S["ctx_turned"], 1)

            @block.scalar
            def _(act):
                for g in range(TT // 2):
                    act.wait_ge(S["ctx_turned"], g + 1)
                    act.activation(CXT[:, :, g * 256:(g + 1) * 256],
                                   PS[:, g, :].rearrange("p (k n) -> p k n", k=KD), ACT.Copy)

    def layernorm(src, dst, dstT=None, gain=None, shift=None, first=False, rows=None, pre=None, split=None):
        with ExitStack() as st:
            tag = str(nc.next_id())
            stats = st.enter_context(nc.sbuf_tensor("stats" + tag, [P, TT, 6], F32))
            mom = st.enter_context(nc.sbuf_tensor("mom" + tag, [P, TT, 2], F32))
            std = st.enter_context(nc.sbuf_tensor("std" + tag, [P, TT], F32))
            rstd = st.enter_context(nc.sbuf_tensor("rstd" + tag, [P, TT], F32))
            NG = TT // 2
            d = dict(done)
            tbank = (lambda g: 2 * g) if rows is not None else (lambda g: g)

            with nc.Block() as block:
                @block.vector
                def _(dve):
                    def measure(g):
                        if first:
                            dve.wait_ge(S[f"x_in{g // 2}"], 16)
                        if rows is not None:
                            dve.wait_ge(S["o_proj"], d["o_proj"] + 2 * g + 2)
                        if pre is not None:
                            pre(dve, g)
                        for t in (2 * g, 2 * g + 1):
                            dve.bn_stats(stats[:, t, :], src[:, t, :]).then_inc(S["stats"], 1)
                        for t in (2 * g, 2 * g + 1):
                            dve.wait_ge(S["stats"], d["stats"] + t + 1)
                            dve.bn_aggr(mom[:, t, :], stats[:, t, :]).then_inc(S["moments"], 1)

                    def apply(g):
                        dve.wait_ge(S["std"], d["std"] + g + 1)
                        dve.reciprocal(rstd[:, 2 * g:2 * g + 2], std[:, 2 * g:2 * g + 2]).then_inc(S["rstd"], 1)
                        dve.wait_ge(S["rstd"], d["rstd"] + g + 1)
                        for t in (2 * g, 2 * g + 1):
                            dve.tensor_scalar(dst[:, t, :], src[:, t, :], mom[:, t, 0:1], rstd[:, t:t + 1],
                                              ALU.subtract, ALU.mult).then_inc(S["normed"], 1)

                    for g in range(NG + 1):
                        if g < NG:
                            measure(g)
                        if g:
                            apply(g - 1)

                @block.scalar
                def _(act):
                    def root(g):
                        if first and g == 0:
                            act.wait_ge(S["const_in"], 16)
                        act.wait_ge(S["moments"], d["moments"] + 2 * g + 2)
                        act.activation(std[:, 2 * g:2 * g + 2], mom[:, 2 * g:2 * g + 2, 1], ACT.Sqrt,
                                       bias=cst("eps")).then_inc(S["std"], 1)

                    def copy(g):
                        act.wait_ge(S["turned"], d["turned"] + g + 1)
                        src_ps = PS[:, tbank(g), :].rearrange("p (k n) -> p k n", k=KD)
                        if gain is None:
                            act.activation(dstT(slice(0, KD), g), src_ps, ACT.Copy)
                        else:
                            for k in range(KD):
                                act.activation(dstT(k, g), src_ps[:, k, :], ACT.Identity,
                                               bias=shift[:, k:k + 1], scale=gain[:, k:k + 1])

                    def high(g):
                        act.wait_ge(S["normed"], d["normed"] + 2 * g + 2)
                        act.activation(split[0][:, g, 0], dst[:, 2 * g:2 * g + 2, :], ACT.Copy).then_inc(S["part_h"], 1)

                    def middle(g):
                        act.wait_ge(S["rest"], d["rest"] + g + 1)
                        act.activation(split[0][:, g, 1], split[1][:, g], ACT.Copy).then_inc(S["part_m"], 1)

                    for g in range(NG + 2):
                        if g < NG:
                            root(g)
                        if split is not None and 1 <= g <= NG:
                            high(g - 1)
                        if split is not None and g >= 2:
                            middle(g - 2)
                        if g >= 2 and dstT is not None:
                            copy(g - 2)

                if split is not None:
                    @block.gpsimd
                    def _(pool):
                        def low(g):
                            pool.wait_ge(S["part_m"], d["part_m"] + g + 1)
                            pool.tensor_tensor(split[0][:, g, 2], split[1][:, g], split[0][:, g, 1], ALU.subtract
                                               ).then_inc(S["part_l"], 1)

                        for g in range(NG + 1):
                            if g < NG:
                                pool.wait_ge(S["part_h"], d["part_h"] + g + 1)
                                pool.tensor_tensor(split[1][:, g], dst[:, 2 * g:2 * g + 2, :], split[0][:, g, 0], ALU.subtract
                                                   ).then_inc(S["rest"], 1)
                            if g:
                                low(g - 1)

                    @block.sync
                    def _(sp):
                        for g in range(NG):
                            split[2](sp, g, d)

                if dstT is not None or rows is not None:
                    @block.tensor
                    def _(pe):
                        def product(g):
                            lhs, rhs, nk = rows
                            for t in (2 * g, 2 * g + 1):
                                for k in range(nk):
                                    last = pe.matmul(PS[:, t, 0:D], lhs(k, t), rhs(k), start=k == 0, stop=k == nk - 1)
                                last.then_inc(S["o_proj"], 1)

                        def turn(g):
                            if first and g == 0:
                                pe.wait_ge(S["const_in"], 16)
                            pe.wait_ge(S["normed"], d["normed"] + 2 * g + 2)
                            for k in range(KD):
                                for j in range(2):
                                    last = pe.transpose(PS[:, tbank(g), k * 256 + j * P:k * 256 + (j + 1) * P],
                                                        dst[:, 2 * g + j, k * P:(k + 1) * P], ident)
                            last.then_inc(S["turned"], 1)

                        for g in range(NG + 2):
                            if rows is not None and g < NG:
                                product(g)
                            if g >= 2 and dstT is not None:
                                turn(g - 2)
            for n, k in (("stats", TT), ("moments", TT), ("std", NG), ("rstd", NG), ("normed", TT),
                         ("turned", NG if dstT is not None else 0), ("o_proj", TT if rows is not None else 0),
                         *((n, NG if split is not None else 0) for n in ("part_h", "rest", "part_m", "part_l"))):
                done[n] += k

    def add_product(dst):
        def pre(dve, g):
            v = dst[:, 2 * g:2 * g + 2, :]
            link(dve, dve.tensor_tensor(v, v, PS[:, 2 * g:2 * g + 2, 0:D], ALU.add), "dve_chain")
        return pre

    def add_sums(scale=None):
        def pre(dve, g):
            v = X[:, 2 * g:2 * g + 2, :]
            ps = PS[:, 4 + g, :].rearrange("p (t n) -> p t n", t=2)
            link(dve, dve.tensor_tensor(v, ps, v, ALU.add), "dve_chain")
        return pre

    def to_HT(k, g):
        return HT[:, k, g * 256:(g + 1) * 256]

    def attention(hd, units, causal, scale, q_of, k_of, v_of, out_of, softcap=None, gamma=None,
                  stack=None):
        r = 32 // hd
        npair = 2 * r
        width = 384 if causal else 512
        d = dict(done)
        tag = str(nc.next_id())
        with ExitStack() as st:
            def tmp(name, shape, dt=F32):
                return st.enter_context(nc.sbuf_tensor(name + tag, shape, dt))

            if stack is None:
                QS = tmp("QS", [P, 2, T])
                KM = tmp("KM", [P, 2, 4, T])
            VM = tmp("VM", [P, 2, 2, r, P])
            PR = tmp("PR", [P, 2, 2, 512])
            PT = tmp("PT", [P, 2, 2, 512])
            MX = tmp("MX", [P, 2, 4])
            NB = tmp("NB", [P, 2, 4])
            DI = tmp("DI", [P, 2, T])
            if not causal:
                OU = tmp("OU", [P, 2, T])
            rows = cst(f"rows{hd}", r)
            cols = cst(f"cols{hd}", r)

            def where(u, p):
                quad = p // 2
                slots = (2 * (p % 2), 2 * (p % 2) + 1)
                return quad, slots, (u * r + quad) % 2

            def steps():
                return [(u, p) for u in range(units) for p in range(npair)]

            NU = units * npair

            def ahead(bb, i, last):
                if i + 2 < NU:
                    return bb, i + 2
                return None if last else (bb + 1, i + 2 - NU)

            def batches(eng, body):
                body(0, False, True)
                with eng.Fori(1, B - 1) as bb:
                    body(bb, False)
                body(B - 1, True)

            with nc.Block() as block:
                if stack is not None:
                    @block.sync
                    def _(sp):
                        stack[3](sp)

                @block.gpsimd
                def _(pool):
                    def values(bb, u, U):
                        pool.wait_ge(S["pv"], (U + 1) * npair + d["pv"])
                        for n2 in range(2):
                            pool.tensor_tensor(
                                VM[:, u % 2, n2].rearrange("p r (s c) -> p r s c", s=4),
                                v_of(bb, u, n2).rearrange("p (a s c) -> p a s c", a=1, s=4).to_broadcast([P, r, 4, 32]),
                                cols.rearrange("p r (a c) -> p r a c", a=1).to_broadcast([P, r, 4, 32]),
                                ALU.mult).then_inc(S["v_staged"], 1)

                    def batch(bb, last):
                        for u in range(units):
                            U = bb * units + u
                            if stack is not None:
                                values(bb, u, U)
                                continue
                            pool.wait_ge(S["scores"], (U + 1) * npair + d["scores"])
                            pool.tensor_copy(QS[:, u % 2, :], q_of(bb, u)).then_inc(S["q_staged"], 1)
                            for q in range(r):
                                n = u * r + q
                                Q = bb * (units * r) + n
                                pool.wait_ge(S["scores"], Q * 2 + (2 * npair - 2 + d["scores"]))
                                pool.tensor_tensor(
                                    KM[:, n % 2], k_of(bb, u).rearrange("p (a t) -> p a t", a=1).to_broadcast([P, 4, T]),
                                    rows[:, q, :].rearrange("p (s a) -> p s a", a=1).to_broadcast([P, 4, T]),
                                    ALU.mult).then_inc(S["k_staged"], 1)
                                if q == 0:
                                    values(bb, u, U)

                    for bb in range(B):
                        batch(bb, bb == B - 1)

                @block.tensor
                def _(pe):
                    pe.nop().then_inc(S["scores"], 2 * npair)
                    pe.nop().then_inc(S["pv"], 2 * npair)
                    pe.nop().then_inc(S["turn_b"], 2)

                    def score(bb, i):
                        u, p = i // npair, i % npair
                        quad, slots, kb = where(u, p)
                        G = bb * NU + i
                        if stack is not None and i == 0:
                            for name, count in stack[2](bb):
                                pe.wait_ge(S[name], count)
                        if p == 0 and stack is None:
                            pe.wait_ge(S["q_staged"], bb * units + (u + 1 + d["q_staged"]))
                        if p % 2 == 0 and stack is None:
                            pe.wait_ge(S["k_staged"], bb * (units * r) + (u * r + quad + 1 + d["k_staged"]))
                        pe.wait_ge(S["exps"], G + (1 + d["exps"]))
                        for h in range(2):
                            bank = PS[:, 2 * (i % 2) + h, :]
                            for m in range(2):
                                n = P * (m + 1) if causal else T
                                if stack is None:
                                    q, k = QS[:, u % 2, m * P:(m + 1) * P], KM[:, kb, slots[h], 0:n]
                                else:
                                    q, k = stack[0](bb, u, slots[h], quad, m * P, P), stack[1](bb, u, slots[h], quad, 0, n)
                                last = pe.matmul(bank[:, m * T:m * T + n], q, k, start=True, stop=softcap is not None or not causal,
                                                 skip_group_check=True)
                                if causal and softcap is None:
                                    last = pe.matmul(bank[:, m * T + m * P:m * T + (m + 1) * P], identb[:], maskb[:],
                                                     start=False, stop=True, skip_group_check=True)
                        last.then_inc(S["scores"], 1)

                    def turn(bb, i):
                        G = bb * NU + i
                        ready = "masked" if softcap is not None else "exps"
                        pe.wait_ge(S[ready], G + ((1 if softcap is not None else 3) + d[ready]))
                        for h in range(2):
                            pe.wait_ge(S["copied_a" if h == 0 else "copied_b"], G + (1 + d["copied_a" if h == 0 else "copied_b"]))
                            for n in range(2):
                                for m in range(n if causal else 0, 2):
                                    col = n * T + m * P - (P if causal and n else 0)
                                    last = pe.transpose(PS[:, 4 + h, col:col + P],
                                                        PR[:, i % 2, h, m * T + n * P:m * T + (n + 1) * P], ident)
                            last.then_inc(S["turn_a" if h == 0 else "turn_b"], 1)

                    def product(bb, i):
                        u, p = i // npair, i % npair
                        quad, slots, _ = where(u, p)
                        G = bb * NU + i
                        pe.wait_ge(S["copied_a"], G + (2 + d["copied_a"]))
                        pe.wait_ge(S["copied_b"], G + (2 + d["copied_b"]))
                        if p == 0:
                            pe.wait_ge(S["v_staged"], bb * (2 * units) + (2 * u + 2 + d["v_staged"]))
                            pe.wait_ge(S["heads_out"], bb * units + (u + 1 + d["heads_out"]))
                        bank = PS[:, 6 + u % 2, :]
                        for n in range(2):
                            for what in range(2):
                                for h in range(2):
                                    s = slots[h]
                                    at = 32 * (s if what == 0 else (s + 2) % 4)
                                    lo = P if causal and n else 0
                                    src = PT[:, i % 2, h, T:width] if n else PT[:, i % 2, h, 0:T]
                                    lhs = VM[:, u % 2, n, quad, 32 * s:32 * s + 32] if what == 0 else cols[:, quad, :]
                                    last = pe.matmul(bank[at:at + 32, what * T + lo:what * T + T], lhs, src,
                                                     start=p == 0 and n == 0, stop=p == npair - 1 and n == 1,
                                                     skip_group_check=True, tile_position=(0, at))
                        last.then_inc(S["pv"], 1)

                    score(0, 0)
                    score(0, 1)

                    def batch(bb, last, first=False):
                        for i in range(NU):
                            nxt = ahead(bb, i, last)
                            if nxt is not None:
                                score(*nxt)
                            turn(bb, i)
                            if i:
                                product(bb, i - 1)
                            elif not first:
                                product(bb - 1, NU - 1)
                        if last:
                            product(bb, NU - 1)

                    batches(pe, batch)

                @block.vector
                def _(dve):
                    dve.nop().then_inc(S["copied_a"], 1)
                    dve.nop().then_inc(S["heads_out"], 2)

                    def maxima(bb, i):
                        G = bb * NU + i
                        pr = i % 2
                        if softcap is not None:
                            dve.wait_ge(S["bias"], G + (1 + d["bias"]))
                            v = PR[:, pr].rearrange("p h (a n) -> p h a n", a=4)[:, :, 0:4:3, :]
                            tri = cst("tril", 1).rearrange("p a (b n) -> p a b n", b=1).to_broadcast([P, 2, 2, P])
                            dve.tensor_tensor(v, v, tri, ALU.mult).then_inc(S["masked"], 1)
                            return
                        dve.wait_ge(S["scores"], G + (1 + 2 * npair + d["scores"]))
                        mx = MX[:, pr].rearrange("p (h m) -> p h m", h=2)
                        if causal:
                            v = PS[:, 2 * pr:2 * pr + 2, :]
                            dve.tensor_reduce(mx[:, :, 0], v[:, :, 0:P], AX, ALU.max).then_inc(S["row_max"], 1)
                            dve.tensor_reduce(mx[:, :, 1], v[:, :, T:2 * T], AX, ALU.max).then_inc(S["row_max"], 1)
                        else:
                            v = PS[:, 2 * pr:2 * pr + 2, :].rearrange("p h (m n) -> p (h m) n", m=2)
                            dve.tensor_reduce(MX[:, pr], v, AX, ALU.max).then_inc(S["row_max"], 2)
                        dve.wait_ge(S["row_max"], 2 * G + (2 + d["row_max"]))
                        dve.tensor_scalar(NB[:, pr], MX[:, pr], -scale, None, ALU.mult).then_inc(S["bias"], 1)

                    def copy(bb, i):
                        G = bb * NU + i
                        dve.wait_ge(S["turn_a"], G + (1 + d["turn_a"]))
                        dve.wait_ge(S["pv"], G + (2 * npair - 1 + d["pv"]))
                        dve.tensor_copy(PT[:, i % 2, 0, 0:width], PS[:, 4, 0:width]).then_inc(S["copied_a"], 1)

                    def invert(bb, u, half):
                        U = bb * units + u
                        if half == 0:
                            dve.wait_ge(S["pv"], (U + 3) * npair + d["pv"])
                        c = slice(half * P, (half + 1) * P)
                        dve.reciprocal(DI[:, u % 2, c], PS[:, 6 + u % 2, T + half * P:T + (half + 1) * P]
                                       ).then_inc(S["den_inv"], 1)

                    def normalise(bb, u):
                        U = bb * units + u
                        bank = PS[:, 6 + u % 2, :]
                        dve.wait_ge(S["den_inv"], 2 * U + (2 + d["den_inv"]))
                        dst, add = out_of(bb, u)
                        to = dst if add is None else OU[:, u % 2, :]
                        for lo in (0, P // 2):
                            hi = P // 2 - lo
                            ins = dve.tensor_tensor(to[lo:lo + P // 2], bank[lo:lo + P // 2, 0:T],
                                                    DI[hi:hi + P // 2, u % 2, :], ALU.mult)
                        ins.then_inc(S["heads_out"], 1)
                        if add is not None:
                            dve.wait_ge(S["heads_out"], U + (3 + d["heads_out"]))
                            dve.scalar_tensor_tensor(dst, OU[:, u % 2, :], 1.0 if gamma is None else gamma, dst,
                                                     ALU.mult, ALU.add)

                    late = 2 if npair == 2 else 3
                    after = [(2, lambda b, u: invert(b, u, 0)), (late, lambda b, u: invert(b, u, 1)), (late + 1, normalise)]

                    def finish_units(bb, i, first):
                        for delay, what in after:
                            if (i - delay + 1) % npair == 0:
                                u = (i - delay) // npair
                                if 0 <= u < units:
                                    what(bb, u)
                                elif u < 0 and not first:
                                    what(bb - 1, u + units)

                    maxima(0, 0)
                    maxima(0, 1)

                    def batch(bb, last, first=False):
                        for i in range(NU):
                            copy(bb, i)
                            nxt = ahead(bb, i, last)
                            if nxt is not None:
                                maxima(*nxt)
                            finish_units(bb, i, first)
                        if last:
                            for i in range(NU, NU + late + 1):
                                finish_units(bb, i, False)

                    batches(dve, batch)

                @block.scalar
                def _(act):
                    act.nop().then_inc(S["copied_b"], 1)
                    act.nop().then_inc(S["exps"], 2)

                    def exps(bb, i):
                        G = bb * NU + i
                        pr = i % 2
                        act.wait_ge(S["turn_b"], G + (1 + d["turn_b"]))
                        if softcap is not None:
                            act.wait_ge(S["scores"], G + (1 + 2 * npair + d["scores"]))
                            for m in range(2):
                                n = P * (m + 1) if causal else T
                                v = PR[:, pr, :, m * T:m * T + n]
                                ins = act.activation(v, PS[:, 2 * pr:2 * pr + 2, m * T:m * T + n], ACT.Tanh, scale=scale / softcap)
                                if m == 1:
                                    ins.then_inc(S["exps"], 1)
                            act.wait_ge(S["exps"], G + (3 + d["exps"]))
                            for m in range(2):
                                n = P * (m + 1) if causal else T
                                v = PR[:, pr, :, m * T:m * T + n]
                                ins = act.activation(v, v, ACT.Exp, scale=softcap)
                            ins.then_inc(S["bias"], 1)
                            return
                        act.wait_ge(S["bias"], G + (1 + d["bias"]))
                        for h in range(2):
                            for m in range(2):
                                n = P * (m + 1) if causal else T
                                ins = act.activation(PR[:, pr, h, m * T:m * T + n], PS[:, 2 * pr + h, m * T:m * T + n],
                                                     ACT.Exp, bias=NB[:, pr, 2 * h + m:2 * h + m + 1], scale=scale)
                        ins.then_inc(S["exps"], 1)

                    def copy(bb, i):
                        G = bb * NU + i
                        act.wait_ge(S["turn_b"], G + (3 + d["turn_b"]))
                        act.wait_ge(S["pv"], G + (2 * npair - 1 + d["pv"]))
                        act.activation(PT[:, i % 2, 1, 0:width], PS[:, 5, 0:width], ACT.Copy).then_inc(S["copied_b"], 1)

                    exps(0, 0)
                    exps(0, 1)

                    def batch(bb, last, first=False):
                        for i in range(NU):
                            copy(bb, i)
                            nxt = ahead(bb, i, last)
                            if nxt is not None:
                                exps(*nxt)

                    batches(act, batch)

            n = B * NU
            for name, k in (("q_staged", B * units if stack is None else 0),
                            ("k_staged", B * units * r if stack is None else 0), ("v_staged", 2 * B * units),
                            ("scores", n + 2 * npair), ("row_max", 0 if softcap is not None else 2 * n), ("bias", n),
                            ("exps", n + 2), ("turn_a", n), ("turn_b", n + 2), ("copied_a", n + 1),
                            ("copied_b", n + 1), ("pv", n + 2 * npair), ("den_inv", 2 * B * units),
                            ("heads_out", B * units + 2), ("masked", n if softcap is not None else 0)):
                done[name] += k

    def project(w, nq, hd, QT, KT, V, arrived=None, split=None, first=None):
        d = dict(done)
        cos = cst(f"cos{hd}", 1)
        sin = cst(f"sin{hd}", 1)
        nchunk = CH // T
        work = [(w["q"], w["qp"], QT, j, c) for j in range(nq) for c in range(NCH)]
        work += [(w["k"], w["kp"], KT, j, c) for j in range(2) for c in range(NCH)]
        if split is not None:
            work = [(a, ap, to, j, c) for c in range(NCH) for (a, ap, to, j, c2) in work if c2 == c]
        with ExitStack() as st:
            tag = str(nc.next_id())
            if split is not None:
                SPL = st.enter_context(nc.sbuf_tensor("SPL" + tag, [P, len(work), 3, CH], BF16))
            RC = st.enter_context(nc.sbuf_tensor("RC" + tag, [P, 2, CH], F32))
            RS = st.enter_context(nc.sbuf_tensor("RS" + tag, [P, 2, CH], F32))
            ROT = RC
            REST = H[:].rearrange("p (s t) d -> p s (t d)", t=2)
            NREST = TT // 2
            def values_out(eng):
                for t in range(TT):
                    eng.wait_ge(S["v_proj"], d["v_proj"] + t + 1)
                    dst, src = V[:, t, :], PS[:, 4 + t % 2, 0:D]
                    ins = eng.tensor_copy(dst, src) if split is not None else eng.activation(dst, src, ACT.Copy)
                    ins.then_inc(S["v_out"], 1)

            with nc.Block() as block:
                @block.tensor
                def _(pe):
                    if arrived is not None:
                        pe.wait_ge(*arrived)
                    for n, (a, ap, _, j, c) in enumerate(work):
                        if n >= 2:
                            pe.wait_ge(S["rope_sin"], d["rope_sin"] + n - 1)
                        for half, wt in enumerate((a, ap)):
                            for k in range(KD):
                                last = pe.matmul(PS[:, 2 * (n % 2) + half, :], wt[:, k, j * P:(j + 1) * P],
                                                 HT[:, k, c * CH:(c + 1) * CH], start=k == 0, stop=k == KD - 1)
                        last.then_inc(S["proj"], 1)
                    for t in range(TT):
                        if t >= 2:
                            pe.wait_ge(S["v_out"], d["v_out"] + t - 1)
                        for k in range(KD):
                            last = pe.matmul(PS[:, 4 + t % 2, 0:D], HT[:, k, t * P:(t + 1) * P], w["v"][:, k, :],
                                             start=k == 0, stop=k == KD - 1)
                        last.then_inc(S["v_proj"], 1)

                @block.vector
                def _(dve):
                    if first is not None:
                        first(dve)
                    for n, (_, _, dst, j, c) in enumerate(work):
                        dve.wait_ge(S["proj"], d["proj"] + n + 1)
                        if split is not None and n >= 2:
                            dve.wait_ge(S["rest"], d["rest"] + n - 1)
                        ps = lambda half: PS[:, 2 * (n % 2) + half, :].rearrange("p (b t) -> p b t", t=T)
                        tm = lambda a: a[:, n % 2].rearrange("p (b t) -> p b t", t=T)
                        dve.tensor_tensor(tm(RC), ps(0), cos.to_broadcast([P, nchunk, T]), ALU.mult).then_inc(S["rope_cos"], 1)
                        dve.tensor_tensor(tm(RS), ps(1), sin.to_broadcast([P, nchunk, T]), ALU.mult).then_inc(S["rope_sin"], 1)
                        dve.wait_ge(S["rope_cos"], d["rope_cos"] + n + 1)
                        dve.wait_ge(S["rope_sin"], d["rope_sin"] + n + 1)
                        if split is None:
                            dve.tensor_tensor(dst[:, j, c * CH:(c + 1) * CH], RC[:, n % 2], RS[:, n % 2], ALU.add)
                        else:
                            dve.tensor_tensor(ROT[:, n % 2], RC[:, n % 2], RS[:, n % 2], ALU.add).then_inc(S["rope_sum"], 1)
                    if split is not None:
                        values_out(dve)

                if split is not None:
                    @block.gpsimd
                    def _(pool):
                        for n in range(len(work) + 1):
                            if n < len(work):
                                pool.wait_ge(S["rope_sum"], d["rope_sum"] + n + 1)
                                pool.wait_ge(S["part_h"], d["part_h"] + n + 1)
                                pool.tensor_tensor(REST[:, n % NREST], ROT[:, n % 2], SPL[:, n, 0], ALU.subtract
                                                   ).then_inc(S["rest"], 1)
                            if n:
                                m = n - 1
                                pool.wait_ge(S["part_m"], d["part_m"] + m + 1)
                                pool.tensor_tensor(SPL[:, m, 2], REST[:, m % NREST], SPL[:, m, 1], ALU.subtract
                                                   ).then_inc(S["part_l"], 1)

                    @block.sync
                    def _(sp):
                        split[1](sp, d)

                @block.scalar
                def _(act):
                    if split is None:
                        values_out(act)
                        return
                    for n in range(len(work) + 2):
                        if n < len(work):
                            act.wait_ge(S["rope_sum"], d["rope_sum"] + n + 1)
                            act.activation(SPL[:, n, 0], ROT[:, n % 2], ACT.Copy).then_inc(S["part_h"], 1)
                        if 1 <= n <= len(work):
                            act.wait_ge(S["rest"], d["rest"] + n)
                            act.activation(SPL[:, n - 1, 1], REST[:, (n - 1) % NREST], ACT.Copy).then_inc(S["part_m"], 1)
                        if n >= 2:
                            split[0](act, SPL, d, n - 2)
        done["proj"] += len(work)
        done["rope_cos"] += len(work)
        done["rope_sin"] += len(work)
        done["v_proj"] += TT
        done["v_out"] += TT
        if split is not None:
            for name in ("rope_sum", "part_h", "rest", "part_m", "part_l"):
                done[name] += len(work)

    def fetch_parts(sp, hd, dst, src, order, name):
        for base in range(2 if hd == 8 else 1):
            for j in range(NSTACK[hd]):
                at = 64 * base + hd * j
                sp.dma_start(dst(base)[at:at + hd], src(order[j], base)).then_inc(S[name], 16)

    def stacked_attention(layer, w, nq, hd, scale, arrived=None):
        QT = HT
        with ExitStack() as s2:
            V = s2.enter_context(nc.sbuf_tensor(f"V{layer}", [P, TT, D], F32))
            r = 32 // hd
            nbase = 2 if hd == 8 else 1
            SQ = s2.enter_context(nc.sbuf_tensor(f"SQ{layer}", [P, D // hd // nbase, B * T], BF16))
            SK = s2.enter_context(nc.sbuf_tensor(f"SK{layer}", [P, nbase, 4, B * T], BF16))
            rows = nbase * NSTACK[hd] * hd
            at0 = dict(done)
            NR = nbase * NSTACK[hd] * 2 * 16

            def fetch(sp, c):
                cs = slice(c * CH, (c + 1) * CH)
                if hd == 8:
                    half = lambda a, which, u: a[which, u * P:(u + 1) * P, cs]
                    q_src = lambda which, u: half(q_parts, which, u).rearrange("(a d) t -> d a t", d=hd)
                    k_src = lambda which, u: half(k_parts, which, u).rearrange("(s r d) t -> d s r t", r=r, d=hd)[:, :, 0]
                else:
                    q_src = lambda which, base: q_parts[which, :, cs].rearrange("(a d) t -> d a t", d=hd)
                    k_src = lambda which, base: k_parts[which, :, cs].rearrange("(a b d) t -> d a b t", a=4, d=hd)[:, :, 0]
                fetch_parts(sp, hd, lambda u: SK[:, u, :, cs], k_src, PARTS_K, f"stacked{c}")
                fetch_parts(sp, hd, lambda u: SQ[:, :, cs], q_src, PARTS_Q, f"stacked{c}")

            NW = nq + 2

            def send(act, SPL, d, n):
                c, j = n // NW, n % NW
                dst, j2 = (q_parts, j) if j < nq else (k_parts, j - nq)
                act.wait_ge(S["part_l"], d["part_l"] + n + 1)
                act.dma_start(dst[:, j2 * P:(j2 + 1) * P, c * CH:(c + 1) * CH].rearrange("a p t -> p a t"), SPL[:, n]
                              ).then_inc(S[f"chunk_out{c}"], 16)

            def split(sp, d):
                sp.wait_ge(S["chunk_out0"], d["chunk_out0"] + 16 * NW)
                fetch(sp, 0)
                sp.wait_ge(S["chunk_out1"], d["chunk_out1"] + 16 * NW)

            def zeros(dve):
                dve.memset(SK[64:128, 0], 0.0)
                dve.memset(SK[0:64, 1], 0.0)

            project(w, nq, hd, None, None, V, arrived, (send, split), zeros if hd == 8 else None)
            for c in range(NCH):
                done[f"chunk_out{c}"] += 16 * NW

            def rest(sp):
                fetch(sp, 1)

            def arrivals(bb):
                c = bb * T // CH if isinstance(bb, int) else 1
                return [(f"stacked{c}", at0[f"stacked{c}"] + NR)]

            per = nq // 2

            def queries(b, u, s, quad, lo, n):
                blk = s * r + quad if hd == 8 else (4 * u + s) * r + quad
                return SQ[0:rows, blk, bass.ds(b * T + lo, n)]

            def keys(b, u, s, quad, lo, n):
                a = SK[0:rows, u, s] if hd == 8 else SK[0:rows, 0, 2 * u + s // 2]
                return a[:, bass.ds(b * T + lo, n)]

            attention(hd, nq, True, scale, q_of=None, k_of=None,
                      v_of=lambda b, u, n: V[:, 2 * b + n, (u // per) * P:(u // per + 1) * P],
                      out_of=lambda b, u: (QT[:, u, bass.ds(b * T, T)], None),
                      stack=(queries, keys, arrivals, rest))
            for c in range(NCH):
                done[f"stacked{c}"] += NR
        return ExitStack(), add_product(X), (lambda k, t: QT[:, k, t * P:(t + 1) * P], lambda k: w["o"][:, k, :], nq)

    def self_attention(layer, w, nq, hd, scale, softcap=None, arrived=None):
        st = ExitStack()
        if True:
            QT = st.enter_context(nc.sbuf_tensor(f"QT{layer}", [P, nq, B * T], F32))
            KT = st.enter_context(nc.sbuf_tensor(f"KT{layer}", [P, 2, B * T], F32))
            V = st.enter_context(nc.sbuf_tensor(f"V{layer}", [P, TT, D], F32))
            project(w, nq, hd, QT, KT, V, arrived)
            per = nq // 2
            attention(hd, nq, True, scale,
                      q_of=lambda b, u: QT[:, u, bass.ds(b * T, T)],
                      k_of=lambda b, u: KT[:, u // per, bass.ds(b * T, T)],
                      v_of=lambda b, u, n: V[:, 2 * b + n, (u // per) * P:(u // per + 1) * P],
                      out_of=lambda b, u: (QT[:, u, bass.ds(b * T, T)], None), softcap=softcap)
        return st, add_product(X), (lambda k, t: QT[:, k, t * P:(t + 1) * P], lambda k: w["o"][:, k, :], nq)

    def stacked_cross(hd, SQ, SK, after):
        r = 32 // hd
        rows = NSTACK[hd] * hd
        at = lambda a: a[0:rows].rearrange("p n c -> p (n c)")
        head = lambda b, u, s, q, lo, n: bass.ds(((2 * b + u) * 8 + s * r + q) * D + lo, n)
        attention(hd, 2, False, float(hd) ** -0.5, q_of=None, k_of=None,
                  v_of=lambda b, u, n: CXT[:, n, bass.ds((2 * b + u) * P, P)],
                  out_of=lambda b, u: (X[:, 2 * b + u, :], True),
                  stack=(lambda *a: at(SQ)[:, head(*a)], lambda *a: at(SK)[:, head(*a)], *after))

    def cross_attention(hd, gamma=None):
        attention(hd, 2, False, float(hd) ** -0.5,
                  q_of=lambda b, u: H[:, 2 * b + u, :],
                  k_of=lambda b, u: CX[:, 2 * b + u, :],
                  v_of=lambda b, u, n: CXT[:, n, bass.ds((2 * b + u) * P, P)],
                  out_of=lambda b, u: (X[:, 2 * b + u, :], True), gamma=gamma)

    def quantise_fp4():
        raw = WA[:, A_AT["upT0"][0]:A_AT["upT0"][0] + 4096]
        n = 2048
        tag = str(nc.next_id())
        with ExitStack() as st:
            def tmp(name, shape, dt=F32):
                return st.enter_context(nc.sbuf_tensor(name + tag, shape, dt))
            AB, SG, LO, HI = (tmp(x, [P, n]) for x in ("AB", "SG", "LO", "HI"))
            am, pw, iv = (tmp(x, [P, n // 32]) for x in ("am", "pw", "iv"))
            grp = lambda a: a[:].rearrange("p (g w) -> p g w", w=32)
            wide = lambda a: a[:].rearrange("p (g w) -> p g w", w=1).to_broadcast([P, n // 32, 32])
            d = dict(done)
            with nc.Block() as block:
                @block.scalar
                def _(act):
                    for h in range(2):
                        if h:
                            act.wait_ge(S["dve_mark"], d["dve_mark"] + 1)
                        act.activation(AB[:], raw[:, h * n:(h + 1) * n], ACT.Abs).then_inc(S["act_mark"], 1)
                        act.activation(SG[:], raw[:, h * n:(h + 1) * n], ACT.Sign).then_inc(S["act_mark"], 1)
                    for g in range(8):
                        act.wait_ge(S["turned"], d["turned"] + g + 1)
                        if g < 4:
                            k, f = g // 2, 4 * (g % 2)
                            dst = wA("up0", KD)[:, k, f * P:(f + 4) * P]
                            act.activation(dst, PS[:, g, :], ACT.Copy)
                        else:
                            f = 2 * (g - 4)
                            act.activation(wA("dn0")[:, f * D:(f + 2) * D], PS[:, g, :], ACT.Copy)

                @block.vector
                def _(dve):
                    L = lambda ins: link(dve, ins, "dve_chain")
                    for h in range(2):
                        dve.wait_ge(S["act_mark"], d["act_mark"] + 2 * h + 2)
                        L(dve.tensor_reduce(am[:], grp(AB), AX, ALU.max))
                        L(dve.tensor_scalar(am[:], am[:], 1e-30, None, ALU.max))
                        L(dve.tensor_scalar(pw[:].bitcast(U32), am[:].bitcast(U32), 0x7F800000, None, ALU.bitwise_and))
                        L(dve.reciprocal(iv[:], pw[:]))
                        L(dve.tensor_scalar(iv[:], iv[:], 4.0, None, ALU.mult))
                        L(dve.tensor_tensor(grp(AB), grp(AB), wide(iv), ALU.mult))
                        L(dve.tensor_scalar(pw[:], pw[:], 0.25, None, ALU.mult))
                        L(dve.tensor_scalar(HI[:], AB[:], 5.0, 2.0, ALU.is_ge, ALU.mult))
                        for mid in (3.5, 2.5):
                            L(dve.scalar_tensor_tensor(HI[:], AB[:], mid, HI[:], ALU.is_ge, ALU.add))
                        L(dve.tensor_scalar(LO[:], AB[:], 1.75, None, ALU.is_ge))
                        for mid in (1.25, 0.75, 0.25):
                            L(dve.scalar_tensor_tensor(LO[:], AB[:], mid, LO[:], ALU.is_ge, ALU.add))
                        L(dve.scalar_tensor_tensor(HI[:], LO[:], 0.5, HI[:], ALU.mult, ALU.add))
                        L(dve.tensor_tensor(HI[:], HI[:], SG[:], ALU.mult))
                        dve.tensor_tensor(raw[:, h * n:(h + 1) * n].rearrange("p (g w) -> p g w", w=32),
                                          grp(HI), wide(pw), ALU.mult).then_inc(S["dve_mark"], 1)

                @block.tensor
                def _(pe):
                    upT, dnT = wA("upT0", 8), wA("dnT0", KD)
                    for g in range(8):
                        pe.wait_ge(S["dve_mark"], d["dve_mark"] + 1 + g // 4)
                        for j in range(4):
                            if g < 4:
                                src = upT[:, 4 * (g % 2) + j, (g // 2) * P:(g // 2 + 1) * P]
                            else:
                                f = 2 * (g - 4) + j // 2
                                src = dnT[:, j % 2, f * P:(f + 1) * P]
                            last = pe.transpose(PS[:, g, j * P:(j + 1) * P], src, ident)
                        last.then_inc(S["turned"], 1)
            done["act_mark"] += 4
            done["dve_mark"] += 2
            done["turned"] += 8

    def mlp(n, up, gate, down, mode, bias=None, scales=None, load=None, gates=None, beside=None):
        two = mode == "silu"
        d = dict(done)
        tag = str(nc.next_id())
        with ExitStack() as st:
            def tmp(name, shape, dt=F32):
                return st.enter_context(nc.sbuf_tensor(name + tag, shape, dt))
            AO = tmp("AO", [P, NCH, CH])
            MO = tmp("MO", [P, NCH, CH])
            HO = tmp("HO", [P, NCH, CH])
            with nc.Block() as block:
                if load is not None:
                    @block.sync
                    def _(sp):
                        load(sp, d)

                @block.tensor
                def _(pe):
                    def go_up(i, c):
                        if gates is not None and c == 0:
                            pe.wait_ge(S[f"w_slot{i % RING2}"], 16 * (i // RING2 + 1))
                        if i >= 1:
                            name = "mult_out" if two else "act_out"
                            pe.wait_ge(S[name], d[name] + NCH * (i - 1) + c + 1)
                        for half, w in enumerate((up, gate) if two else (up,)):
                            for k in range(KD):
                                last = pe.matmul(PS[:, 2 * c + half, :], w(i, k), HT[:, k, c * CH:(c + 1) * CH],
                                                 start=k == 0, stop=k == KD - 1)
                        last.then_inc(S["up_ps"], 1)

                    def go_down(i, c):
                        src, name = (HO, "pool_mark") if gates is not None else (MO, "mult_out") if two else (AO, "act_out")
                        pe.wait_ge(S[name], d[name] + NCH * i + c + 1)
                        for j in range(TPC):
                            t = c * TPC + j
                            last = pe.matmul(PS[:, 4 + t // 2, (t % 2) * D:(t % 2 + 1) * D], src[:, c, j * P:(j + 1) * P],
                                             down(i), start=i == 0 and t % 2 == 0, stop=i == n - 1,
                                             skip_group_check=True)
                        last.then_inc(S["down_ps"], 1)

                    for c in range(NCH):
                        go_up(0, c)
                    for i in range(n):
                        for c in range(NCH):
                            if i + 1 < n:
                                go_up(i + 1, c)
                            go_down(i, c)

                @block.scalar
                def _(act):
                    for i in range(n):
                        for c in range(NCH):
                            act.wait_ge(S["up_ps"], d["up_ps"] + NCH * i + c + 1)
                            if i >= 1:
                                name = "mult_out" if two else "down_ps"
                                act.wait_ge(S[name], d[name] + NCH * (i - 1) + c + 1)
                            if two:
                                ins = act.activation(AO[:, c], PS[:, 2 * c, :], ACT.Silu,
                                                     scale=1.0 if scales is None else scales[:, 0:1])
                            else:
                                ins = act.activation(AO[:, c], PS[:, 2 * c, :], ACT.Gelu_apprx_tanh, bias=bias[:, i:i + 1])
                            ins.then_inc(S["act_out"], 1)

                if two:
                    @block.vector
                    def _(dve):
                        for i in range(n):
                            for c in range(NCH):
                                dve.wait_ge(S["act_out"], d["act_out"] + NCH * i + c + 1)
                                if i >= 1:
                                    name = "pool_mark" if gates is not None else "down_ps"
                                    dve.wait_ge(S[name], d[name] + NCH * (i - 1) + c + 1)
                                if scales is None:
                                    ins = dve.tensor_tensor(MO[:, c], PS[:, 2 * c + 1, :], AO[:, c], ALU.mult)
                                else:
                                    ins = dve.scalar_tensor_tensor(MO[:, c], PS[:, 2 * c + 1, :], scales[:, 1:2],
                                                                   AO[:, c], ALU.mult, ALU.mult)
                                ins.then_inc(S["mult_out"], 1)

                if beside is not None:
                    @block.vector
                    def _(dve):
                        beside(dve)

                if bias is not None:
                    @block.gpsimd
                    def _(pool):
                        row = rv("b_dn0").rearrange("p (a n) -> p a n", a=1).to_broadcast([P, TT, D])
                        pool.tensor_tensor(X[:], X[:], row, ALU.add).then_inc(S["pool_mark"], 1)

                if gates is not None:
                    @block.gpsimd
                    def _(pool):
                        for i in range(n):
                            for c in range(NCH):
                                pool.wait_ge(S["mult_out"], d["mult_out"] + NCH * i + c + 1)
                                if c == 0:
                                    pool.wait_ge(S[f"g_slot{i % RINGG}"], 32 * (i // RINGG + 1))
                                if i >= 1:
                                    pool.wait_ge(S["down_ps"], d["down_ps"] + NCH * (i - 1) + c + 1)
                                pool.tensor_tensor(HO[:, c], MO[:, c], gates(i)[:, c * CH:(c + 1) * CH],
                                                   ALU.mult).then_inc(S["pool_mark"], 1)
            for name, k in (("up_ps", NCH * n), ("down_ps", NCH * n), ("act_out", NCH * n),
                            ("mult_out", NCH * n if two else 0),
                            ("pool_mark", NCH * n if gates is not None else 1 if bias is not None else 0)):
                done[name] += k

    def mixing():
        tag = str(nc.next_id())
        st = ExitStack()

        def tmp(name, shape, dt=F32):
            return st.enter_context(nc.sbuf_tensor(name + tag, shape, dt))

        N = tmp("N", [P, TT, D])
        AP_ = tmp("AP", [P, KD, B, T + 1])
        DF = tmp("DF", [P, KD, B, T])
        XM = tmp("XM", [P, 3, KD, B, T])
        RR = tmp("RR", [P, KD, B * T])
        EK = tmp("EK", [P, KD, B * T])
        us = tmp("us", [P, KD])
        cur = AP_[:, :, :, 1:T + 1]
        prev = AP_[:, :, :, 0:T]
        flat = lambda a: a.rearrange("p b t -> p (b t)")
        halves = [(j, c) for c in range(NCH) for j in range(KD)]
        NHV = len(halves)
        piece = lambda a, j, c: a[:, j, c * CH:(c + 1) * CH]

        def to_padded(k, g):
            return AP_[:, k, g, 1:T + 1]

        def mix(dve, d, n, mu):
            for k in range(KD):
                dve.scalar_tensor_tensor(XM[:, n, k], DF[:, k], vv(mu)[:, k:k + 1], prev[:, k], ALU.mult,
                                         ALU.add).then_inc(S["dve_mark"], 1)

        def products(pe, d, n, w, bank, wait=None):
            pe.wait_ge(S["dve_mark"], d["dve_mark"] + KD * (n + 1))
            for m, (j, c) in enumerate(halves):
                if wait is not None:
                    pe.wait_ge(S[wait], d[wait] + m + 1)
                for k in range(KD):
                    last = pe.matmul(PS[:, bank + m, :], w[:, k, j * P:(j + 1) * P],
                                     flat(XM[:, n, k])[:, c * CH:(c + 1) * CH], start=k == 0, stop=k == KD - 1)
                last.then_inc(S["up_ps"], 1)

        with nc.Block() as block:
            @block.vector
            def _(dve):
                dve.memset(AP_[:, :, :, 0:1], 0.0)
                dve.tensor_scalar(us[:], vv("u"), -float(np.log(1e-8)), None, ALU.add)
        layernorm(H, N, to_padded, vv("ln1_g"), vv("ln1_b"))
        d = dict(done)
        with nc.Block() as block:
            @block.vector
            def _(dve):
                link(dve, dve.tensor_tensor(DF[:], cur, prev, ALU.subtract), "dve_chain")
                for n, mu in enumerate(("mu_r", "mu_k", "mu_v")):
                    mix(dve, d, n, mu)
                for m, (j, c) in enumerate(halves):
                    dve.wait_ge(S["act_out"], d["act_out"] + NHV + m + 1)
                    link(dve, dve.tensor_tensor(piece(RR, j, c), piece(RR, j, c), piece(EK, j, c), ALU.mult), "dve_chain")
                for m, (j, c) in enumerate(halves):
                    dve.wait_ge(S["up_ps"], d["up_ps"] + 2 * NHV + m + 1)
                    dve.tensor_tensor(piece(RR, j, c), piece(RR, j, c), PS[:, m, :], ALU.mult)

            @block.tensor
            def _(pe):
                products(pe, d, 0, wA("wr", KD), 0)
                products(pe, d, 1, wA("wk", KD), 4)
                products(pe, d, 2, wA("wv", KD), 0, "act_out")

            @block.scalar
            def _(act):
                for n in range(2):
                    for m, (j, c) in enumerate(halves):
                        act.wait_ge(S["up_ps"], d["up_ps"] + n * NHV + m + 1)
                        act.activation(piece((RR, EK)[n], j, c), PS[:, 4 * n + m, :], ACT.Sigmoid,
                                       **({"bias": us[:, j:j + 1]} if n else {})).then_inc(S["act_out"], 1)
        done["dve_mark"] += 3 * KD
        done["up_ps"] += 3 * NHV
        done["act_out"] += 2 * NHV
        layernorm(H, N, to_padded, vv("ln2_g"), vv("ln2_b"), pre=add_product(H),
                  rows=(lambda k, t: RR[:, k, t * P:(t + 1) * P], lambda k: wA("wout", KD)[:, k, :], KD))
        d = dict(done)
        with nc.Block() as block:
            @block.vector
            def _(dve):
                link(dve, dve.tensor_tensor(DF[:], cur, prev, ALU.subtract), "dve_chain")
                for n, mu in enumerate(("cmu_k", "cmu_r")):
                    mix(dve, d, n, mu)
                for m, (j, c) in enumerate(halves):
                    dve.wait_ge(S["act_out"], d["act_out"] + m + 1)
                    dve.tensor_tensor(piece(EK, j, c), piece(EK, j, c), PS[:, m, :], ALU.mult)

            @block.tensor
            def _(pe):
                products(pe, d, 0, wA("ck", KD), 0)
                pe.wait_ge(S["dve_mark"], d["dve_mark"] + 2 * KD)
                for t in range(TT):
                    for k in range(KD):
                        last = pe.matmul(PS[:, 4 + t // 2, (t % 2) * D:(t % 2 + 1) * D], flat(XM[:, 1, k])[:, t * P:(t + 1) * P],
                                         wA("cr", KD)[:, k, :], start=k == 0, stop=k == KD - 1)
                    if t % 2:
                        last.then_inc(S["up_ps"], 1)

            @block.scalar
            def _(act):
                for m, (j, c) in enumerate(halves):
                    act.wait_ge(S["up_ps"], d["up_ps"] + m + 1)
                    act.activation(piece(EK, j, c), PS[:, m, :], ACT.Relu).then_inc(S["act_out"], 1)
                for g in range(TT // 2):
                    act.wait_ge(S["up_ps"], d["up_ps"] + NHV + g + 1)
                    act.activation(N[:, 2 * g:2 * g + 2, :], PS[:, 4 + g, :].rearrange("p (t n) -> p t n", t=2), ACT.Sigmoid)
        done["dve_mark"] += 2 * KD
        done["up_ps"] += NHV + TT // 2
        done["act_out"] += NHV

        def pre(dve, g):
            L = lambda ins: link(dve, ins, "dve_chain")
            v = slice(2 * g, 2 * g + 2)
            L(dve.tensor_tensor(N[:, v, :], N[:, v, :], PS[:, v, 0:D], ALU.mult))
            L(dve.tensor_tensor(H[:, v, :], H[:, v, :], N[:, v, :], ALU.add))
            L(dve.tensor_tensor(X[:, v, :], X[:, v, :], H[:, v, :], ALU.add))

        return st, pre, (lambda k, t: EK[:, k, t * P:(t + 1) * P], lambda k: wA("cv", KD)[:, k, :], KD)

    def route(E, extra, weights, logits_of, gates_of, G, GT):
        EW = E + extra
        tag = str(nc.next_id())
        d = dict(done)
        with ExitStack() as st:
            def tmp(name, shape, dt=F32):
                return st.enter_context(nc.sbuf_tensor(name + tag, shape, dt))
            LG, PRB, RK = (tmp(x, [P, TT, E]) for x in ("LG", "PRB", "RK"))
            C1, C2 = (tmp(x, [P, TT, E, E]) for x in ("CA", "CB"))
            r1, r2 = (tmp(x, [P, TT]) for x in ("ra", "rb"))
            wide = lambda a: a[:].rearrange("p (t e) -> p t e", e=1).to_broadcast([P, TT, E])
            with nc.Block() as block:
                @block.tensor
                def _(pe):
                    for t in range(TT):
                        for k in range(KD):
                            last = pe.matmul(PS[:, 0, t * EW:(t + 1) * EW], HT[:, k, t * P:(t + 1) * P], weights[:, k, :],
                                             start=k == 0, stop=k == KD - 1)
                    last.then_inc(S["pe_mark"], 1)
                    pe.wait_ge(S["gates"], d["gates"] + 1)
                    for t in range(TT):
                        last = pe.transpose(PS[0:EW, 1 + t // 4, (t % 4) * P:(t % 4 + 1) * P], G[:, t, :], ident)
                    last.then_inc(S["turned"], 1)

                @block.scalar
                def _(act):
                    act.wait_ge(S["dve_mark"], d["dve_mark"] + 1)
                    act.activation(PRB[:], PRB[:], ACT.Exp).then_inc(S["act_mark"], 1)
                    if extra:
                        ps = PS[:, 0, 0:TT * EW].rearrange("p (t e) -> p t e", e=EW)
                        act.activation(G[:, :, E:EW], ps[:, :, E:EW], ACT.Sigmoid).then_inc(S["act_mark"], 1)
                    else:
                        act.wait_ge(S["dve_mark"], d["dve_mark"] + 2)
                        act.activation(LG[:], LG[:], ACT.Exp).then_inc(S["act_mark"], 1)

                @block.vector
                def _(dve):
                    L = lambda ins: link(dve, ins, "dve_chain")
                    dve.wait_ge(S["pe_mark"], d["pe_mark"] + 1)
                    ps = PS[:, 0, 0:TT * EW].rearrange("p (t e) -> p t e", e=EW)
                    logits_of(dve, L, LG, ps[:, :, 0:E])
                    L(dve.tensor_reduce(r1[:], LG[:], AX, ALU.max))
                    dve.tensor_tensor(PRB[:], LG[:], wide(r1), ALU.subtract).then_inc(S["dve_mark"], 1)
                    dve.wait_ge(S["act_mark"], d["act_mark"] + 1)
                    L(dve.tensor_reduce(r1[:], PRB[:], AX, ALU.add))
                    L(dve.reciprocal(r1[:], r1[:]))
                    L(dve.tensor_tensor(PRB[:], PRB[:], wide(r1), ALU.mult))
                    mine = PRB[:].rearrange("p t (e a) -> p t e a", a=1).to_broadcast([P, TT, E, E])
                    theirs = PRB[:].rearrange("p t (a e) -> p t a e", a=1).to_broadcast([P, TT, E, E])
                    low = cst(f"lower{E}").rearrange("p (a e f) -> p a (e f)", a=1, e=E).to_broadcast([P, TT, E * E])
                    L(dve.tensor_tensor(C1[:], theirs, mine, ALU.is_gt))
                    L(dve.tensor_tensor(C2[:], theirs, mine, ALU.is_equal))
                    c2 = C2[:].rearrange("p t e f -> p t (e f)")
                    L(dve.tensor_tensor(c2, c2, low, ALU.mult))
                    L(dve.tensor_tensor(C1[:], C1[:], C2[:], ALU.add))
                    L(dve.tensor_reduce(RK[:], C1[:], AX, ALU.add))
                    gates_of(dve, L, PRB, RK, LG, r1, r2, wide, d)
                    dve.wait_ge(S["turned"], d["turned"] + 1)
                    L(dve.tensor_copy(GT[0:EW, :].rearrange("p (a n) -> p a n", a=2), PS[0:EW, 1:3, :]))
            done["pe_mark"] += 1
            done["gates"] += 1
            done["turned"] += 1
            done["act_mark"] += 2
            done["dve_mark"] += 1 if extra else 2

    def experts1():
        NF = sum(FB1)
        tag = str(nc.next_id())
        owner = [e for e in range(E1) for _ in range(FB1[e])]
        with ExitStack() as st:
            def tmp(name, shape, dt=F32):
                return st.enter_context(nc.sbuf_tensor(name + tag, shape, dt))
            G = tmp("G", [P, TT, E1])
            GT = tmp("GT", [P, B * T])
            GH = tmp("GH", [P, B * T])
            GX = H[:].rearrange("p t d -> p (t d)").rearrange("p (k n) -> p k n", k=KD)
            GB = tmp("GB", [P, E1, B * T])
            gb1 = tmp("gb1", [P, NF])
            cc = tmp("cc", [P, 4])
            HA = tmp("HA", [P, 4, CH])
            HB = tmp("HB", [P, 4, CH])
            MT = tmp("MT", [P, B * T])

            def logits_of(dve, L, LG, ps):
                row = rv("b_router").rearrange("p (a e) -> p a e", a=1).to_broadcast([P, TT, E1])
                cost = cst("cost").rearrange("p (a e) -> p a e", a=1).to_broadcast([P, TT, E1])
                L(dve.tensor_tensor(LG[:], ps, row, ALU.add))
                L(dve.tensor_tensor(LG[:], LG[:], cost, ALU.subtract))

            def gates_of(dve, L, PRB, RK, LG, r1, r2, wide, d):
                L(dve.tensor_reduce(r2[:], PRB[:], AX, ALU.max))
                dve.tensor_tensor(LG[:], PRB[:], wide(r2), ALU.subtract).then_inc(S["dve_mark"], 1)
                dve.wait_ge(S["act_mark"], d["act_mark"] + 2)
                L(dve.scalar_tensor_tensor(LG[:], RK[:], 2.0, LG[:], ALU.is_lt, ALU.mult))
                L(dve.tensor_reduce(r2[:], LG[:], AX, ALU.add))
                L(dve.reciprocal(r2[:], r2[:]))
                dve.tensor_tensor(G[:], LG[:], wide(r2), ALU.mult).then_inc(S["gates"], 1)

            route(E1, 0, wB("router", KD), logits_of, gates_of, G, GT)
            d = dict(done)
            n_all = NF + 1
            work = [(f, c) for f in range(n_all) for c in range(NCH)]
            with nc.Block() as block:
                @block.sync
                def _(sp):
                    sp.dma_start(gate_rows[0:E1, :], GT[0:E1, :]).then_inc(S["gates_sent"], 16)
                    sp.wait_ge(S["gates_sent"], d["gates_sent"] + 16)
                    sp.dma_start(GB[:], gate_rows[0:E1, :].rearrange("(a e) n -> a e n", a=1).to_broadcast([P, E1, B * T])
                                 ).then_inc(S["gates_back"], 16)

                @block.tensor
                def _(pe):
                    for c in range(NCH):
                        for k in range(KD):
                            last = pe.matmul(PS[:, 2 + c, :], wB("down", KD)[:, k, :], HT[:, k, c * CH:(c + 1) * CH],
                                             start=k == 0, stop=k == KD - 1)
                        last.then_inc(S["proj"], 1)

                    def go_up(n):
                        f, c = work[n]
                        if n >= 2:
                            pe.wait_ge(S["act_out"], d["act_out"] + n - 1)
                        w = wB("w1")[:, f * P:(f + 1) * P] if f < NF else wB("sh1")
                        pe.matmul(PS[:, n % 2, :], w, GH[:, c * CH:(c + 1) * CH], start=True, stop=True).then_inc(S["up_ps"], 1)

                    def go_down(n):
                        f, c = work[n]
                        pe.wait_ge(S["mult_out"], d["mult_out"] + n + 1)
                        w = wB("w2")[:, f * P:(f + 1) * P] if f < NF else wB("sh2")
                        pe.matmul(PS[:, 4 + c, :], w, HB[:, n % 4, :], start=f == 0, stop=f == n_all - 1
                                  ).then_inc(S["down_ps"], 1)

                    pe.wait_ge(S["act_mark"], d["act_mark"] + 2)
                    go_up(0)
                    go_up(1)
                    pe.wait_ge(S["act_mark"], d["act_mark"] + 3)
                    for f in range(NF):
                        last = pe.matmul(PS[:, 6, 0:1], wB("w2")[:, f * P:(f + 1) * P], gb1[:, f:f + 1],
                                         start=f == 0, stop=f == NF - 1)
                    last.then_inc(S["pe_mark"], 1)
                    for n in range(len(work)):
                        if n + 2 < len(work):
                            go_up(n + 2)
                        go_down(n)
                    pe.wait_ge(S["dve_mark"], d["dve_mark"] + 1)
                    pe.wait_ge(S["act_mark"], d["act_mark"] + 4)
                    for t in range(TT):
                        bank = PS[:, t % 4, 0:D]
                        if t >= 4:
                            pe.wait_ge(S["x_added"], d["x_added"] + t - 3)
                        pe.matmul(bank, MT[:, t * P:(t + 1) * P], wB("up"), start=True, stop=False)
                        for k in range(KD):
                            last = pe.matmul(bank, GX[:, k, t * P:(t + 1) * P], wB("core", KD)[:, k, :],
                                             start=False, stop=k == KD - 1)
                        last.then_inc(S["o_proj"], 1)

                @block.scalar
                def _(act):
                    for c in range(NCH):
                        act.wait_ge(S["proj"], d["proj"] + c + 1)
                        act.activation(GH[:, c * CH:(c + 1) * CH], PS[:, 2 + c, :], ACT.Gelu,
                                       bias=vv("b_down1")).then_inc(S["act_mark"], 1)
                    act.activation(gb1[:], vv("b1"), ACT.Gelu).then_inc(S["act_mark"], 1)
                    act.activation(GX, HT[:], ACT.Gelu).then_inc(S["act_mark"], 1)
                    for n, (f, c) in enumerate(work):
                        act.wait_ge(S["up_ps"], d["up_ps"] + n + 1)
                        if n >= 4:
                            act.wait_ge(S["mult_out"], d["mult_out"] + n - 3)
                        b = vv("b1")[:, f:f + 1] if f < NF else vv("b_sh1")
                        act.activation(HA[:, n % 4, :], PS[:, n % 2, :], ACT.Gelu, bias=b).then_inc(S["act_out"], 1)

                @block.gpsimd
                def _(pool):
                    for i, name in enumerate(("b_up1", "b_core")):
                        row = rv(name).rearrange("p (a n) -> p a n", a=1).to_broadcast([P, TT, D])
                        if i:
                            pool.wait_ge(S["pool_mark"], d["pool_mark"] + 1)
                        pool.tensor_tensor(X[:], X[:], row, ALU.add).then_inc(S["pool_mark"], 1)

                @block.vector
                def _(dve):
                    L = lambda ins: link(dve, ins, "dve_chain")
                    dve.wait_ge(S["act_mark"], d["act_mark"] + 3)
                    dve.wait_ge(S["gates_back"], d["gates_back"] + 16)
                    for n, (f, c) in enumerate(work):
                        dve.wait_ge(S["act_out"], d["act_out"] + n + 1)
                        if n >= 4:
                            dve.wait_ge(S["down_ps"], d["down_ps"] + n - 3)
                        if f < NF:
                            ins = dve.scalar_tensor_tensor(HB[:, n % 4, :], HA[:, n % 4, :], gb1[:, f:f + 1],
                                                           GB[:, owner[f], c * CH:(c + 1) * CH], ALU.subtract, ALU.mult)
                        else:
                            ins = dve.tensor_scalar(HB[:, n % 4, :], HA[:, n % 4, :], 0.1, None, ALU.mult)
                        ins.then_inc(S["mult_out"], 1)
                    L(dve.tensor_reduce(cc[:, 0:1], vv("b2"), AX, ALU.add))
                    L(dve.scalar_tensor_tensor(cc[:, 1:2], vv("b_sh2"), 0.1, cc[:, 0:1], ALU.mult, ALU.add))
                    dve.wait_ge(S["pe_mark"], d["pe_mark"] + 1)
                    L(dve.tensor_tensor(cc[:, 2:3], PS[:, 6, 0:1], cc[:, 1:2], ALU.add))
                    dve.wait_ge(S["down_ps"], d["down_ps"] + len(work))
                    dve.tensor_scalar(MT[:].rearrange("p (a n) -> p a n", a=2), PS[:, 4:6, :], cc[:, 2:3], None,
                                      ALU.add).then_inc(S["dve_mark"], 1)
                    dve.wait_ge(S["pool_mark"], d["pool_mark"] + 2)
                    for t in range(TT):
                        dve.wait_ge(S["o_proj"], d["o_proj"] + t + 1)
                        dve.tensor_tensor(X[:, t, :], X[:, t, :], PS[:, t % 4, 0:D], ALU.add).then_inc(S["x_added"], 1)
            for name, k in (("gates_sent", 16), ("gates_back", 16), ("proj", NCH), ("up_ps", len(work)),
                            ("act_out", len(work)), ("mult_out", len(work)), ("down_ps", len(work)), ("pe_mark", 1),
                            ("act_mark", 4), ("dve_mark", 1), ("pool_mark", 2), ("o_proj", TT), ("x_added", TT)):
                done[name] += k

    def experts2():
        tag = str(nc.next_id())
        with ExitStack() as st:
            def tmp(name, shape, dt=F32):
                return st.enter_context(nc.sbuf_tensor(name + tag, shape, dt))
            G = tmp("G", [P, TT, E2 + 1])
            GT = tmp("GT", [P, B * T])
            W2 = tmp("W2", [P, RING2, 3 * D])
            GR = tmp("GR", [P, RINGG, B * T])

            def logits_of(dve, L, LG, ps):
                L(dve.tensor_copy(LG[:], ps))

            def gates_of(dve, L, PRB, RK, LG, r1, r2, wide, d):
                L(dve.scalar_tensor_tensor(LG[:], RK[:], 4.0, PRB[:], ALU.is_lt, ALU.mult))
                L(dve.tensor_reduce(r2[:], LG[:], AX, ALU.add))
                L(dve.tensor_scalar(r2[:], r2[:], 1e-9, None, ALU.max))
                L(dve.reciprocal(r2[:], r2[:]))
                dve.wait_ge(S["act_mark"], d["act_mark"] + 2)
                dve.tensor_tensor(G[:, :, 0:E2], LG[:], wide(r2), ALU.mult).then_inc(S["gates"], 1)

            route(E2, 1, wL("router2", KD), logits_of, gates_of, G, GT)

            def load(sp, d):
                sp.dma_start(gate_rows[:, :], GT[0:E2 + 1, :]).then_inc(S["gates_sent"], 16)

                def weights(i):
                    if i >= RING2:
                        sp.wait_ge(S["down_ps"], d["down_ps"] + NCH * (i - RING2 + 1))
                    sp.dma_start(W2[:, i % RING2, :], w2f[i]).then_inc(S[f"w_slot{i % RING2}"], 16)

                def gates(i):
                    if i >= RINGG:
                        sp.wait_ge(S["pool_mark"], d["pool_mark"] + NCH * (i - RINGG + 1))
                    owner = [min((i * P + r) // I2, E2) for r in range(P)]
                    cut = next((r for r in range(P) if owner[r] != owner[0]), P // 2)
                    for lo, hi in ((0, cut), (cut, P)):
                        e = owner[lo]
                        sp.dma_start(GR[lo:hi, i % RINGG, :], gate_rows[e:e + 1, :].to_broadcast([hi - lo, B * T])
                                     ).then_inc(S[f"g_slot{i % RINGG}"], 16)

                for i in range(NI2):
                    weights(i)
                    if i == 0:
                        sp.wait_ge(S["gates_sent"], d["gates_sent"] + 16)
                    gates(i)

            chunk = lambda i, j: W2[:, i % RING2, j * D:(j + 1) * D]
            mlp(NI2, up=lambda i, k: chunk(i, 0)[:, k * P:(k + 1) * P], gate=lambda i, k: chunk(i, 1)[:, k * P:(k + 1) * P],
                down=lambda i: chunk(i, 2), mode="silu", load=load, gates=lambda i: GR[:, i % RINGG, :])
            done["gates_sent"] += 16

    def wkv_scan():
        NS = KD * B
        d = dict(done)
        tag = str(nc.next_id())
        with ExitStack() as st:
            def tmp(name, shape, dt=F32):
                return st.enter_context(nc.sbuf_tensor(name + tag, shape, dt))
            O, PN, QN = (tmp(x, [P, NS, T + 1]) for x in ("O", "PN", "QN"))
            A2, E2_, EV, A1 = (tmp(x, [P, NS, T]) for x in ("A2", "E2", "EV", "A1"))
            K = HT[:].rearrange("p k (b t) -> p (k b) t", t=T)
            V = CXT[:].rearrange("p k (b t) -> p (k b) t", t=T)
            w, u = vv("w3"), vv("u3")
            half = lambda a, k: a[:, k * B:(k + 1) * B]
            old, new = (lambda a: a[:, :, 0:T]), (lambda a: a[:, :, 1:T + 1])
            with nc.Block() as block:
                @block.vector
                def _(dve):
                    L = lambda ins: link(dve, ins, "dve_chain")
                    dve.memset(O[:, :, 0:1], -1e38)
                    dve.memset(PN[:, :, 0:1], 0.0)
                    L(dve.memset(QN[:, :, 0:1], 0.0))
                    for s in range(NS):
                        k = s // B
                        ins = dve.tensor_tensor_scan(O[:, s, 1:T + 1], w[:, k:k + 1].to_broadcast([P, T]), K[:, s, :], -1e38,
                                                     ALU.add, ALU.max)
                    L(ins)
                    dve.tensor_tensor(E2_[:], K, new(O), ALU.subtract).then_inc(S["dve_mark"], 1)
                    for k in range(KD):
                        ins = dve.scalar_tensor_tensor(half(A2, k), half(old(O), k), w[:, k:k + 1], half(new(O), k),
                                                       ALU.add, ALU.subtract)
                    ins.then_inc(S["dve_mark"], 1)
                    dve.wait_ge(S["act_mark"], d["act_mark"] + 1)
                    L(dve.tensor_tensor(EV[:], E2_[:], V, ALU.mult))
                    dve.wait_ge(S["act_mark"], d["act_mark"] + 2)
                    for s in range(NS):
                        dve.tensor_tensor_scan(PN[:, s, 1:T + 1], A2[:, s, :], EV[:, s, :], 0.0, ALU.mult, ALU.add)
                        ins = dve.tensor_tensor_scan(QN[:, s, 1:T + 1], A2[:, s, :], E2_[:, s, :], 0.0, ALU.mult, ALU.add)
                    L(ins)
                    for k in range(KD):
                        ins = dve.scalar_tensor_tensor(half(EV, k), half(K, k), u[:, k:k + 1], half(old(O), k), ALU.add, ALU.max)
                    L(ins)
                    dve.tensor_tensor(A1[:], old(O), EV[:], ALU.subtract).then_inc(S["dve_mark"], 1)
                    for k in range(KD):
                        ins = dve.scalar_tensor_tensor(half(E2_, k), half(K, k), u[:, k:k + 1], half(EV, k), ALU.add, ALU.subtract)
                    ins.then_inc(S["dve_mark"], 1)
                    dve.wait_ge(S["act_mark"], d["act_mark"] + 3)
                    L(dve.tensor_tensor(A2[:], A1[:], old(PN), ALU.mult))
                    L(dve.tensor_tensor(A1[:], A1[:], old(QN), ALU.mult))
                    dve.wait_ge(S["act_mark"], d["act_mark"] + 4)
                    L(dve.tensor_tensor(EV[:], E2_[:], V, ALU.mult))
                    L(dve.tensor_tensor(A2[:], A2[:], EV[:], ALU.add))
                    L(dve.tensor_tensor(A1[:], A1[:], E2_[:], ALU.add))
                    L(dve.reciprocal(A1[:], A1[:]))
                    dve.tensor_tensor(A2[:], A2[:], A1[:], ALU.mult).then_inc(S["dve_mark"], 1)
                    for g in range(TT // 2):
                        dve.wait_ge(S["turned"], d["turned"] + g + 1)
                        v = X[:, 2 * g:2 * g + 2, :].rearrange("p t d -> p (t d)")
                        dve.tensor_tensor(v, v, PS[:, g, :], ALU.add)

                @block.scalar
                def _(act):
                    for n, a in enumerate((E2_, A2, A1, E2_)):
                        act.wait_ge(S["dve_mark"], d["dve_mark"] + n + 1)
                        act.activation(a[:], a[:], ACT.Exp).then_inc(S["act_mark"], 1)

                @block.tensor
                def _(pe):
                    pe.wait_ge(S["dve_mark"], d["dve_mark"] + 5)
                    for g in range(TT // 2):
                        for j in range(2):
                            for k in range(KD):
                                last = pe.transpose(PS[:, g, j * D + k * P:j * D + (k + 1) * P],
                                                    A2[:, k * B + g, j * P:(j + 1) * P], ident)
                        last.then_inc(S["turned"], 1)
            done["dve_mark"] += 5
            done["act_mark"] += 4
            done["turned"] += TT // 2

    def ternary(SC):
        d = dict(done)
        tag = str(nc.next_id())
        with ExitStack() as st:
            def tmp(name, shape, dt=F32):
                return st.enter_context(nc.sbuf_tensor(name + tag, shape, dt))
            AB = tmp("AB", [P, 2, 2048])
            rs = tmp("rs", [P, 4])
            th = tmp("th", [P, 2, 4])
            mats = [wL(x) for x in ("up3", "gate3", "dn3")]
            with nc.Block() as block:
                @block.scalar
                def _(act):
                    for j, w in enumerate(mats):
                        if j == 0:
                            act.wait_ge(S["late_in"], 16)
                        if j == 2:
                            act.wait_ge(S["dve_mark"], d["dve_mark"] + 1)
                        act.activation(AB[:, j % 2], w, ACT.Abs).then_inc(S["act_mark"], 1)

                @block.tensor
                def _(pe):
                    pe.wait_ge(S["dve_mark"], d["dve_mark"] + 3)
                    pe.matmul(PS[:, 0, 0:3], cst("ones"), rs[:, 0:3], start=True, stop=True).then_inc(S["pe_mark"], 1)

                @block.vector
                def _(dve):
                    L = lambda ins: link(dve, ins, "dve_chain")
                    for j in range(3):
                        dve.wait_ge(S["act_mark"], d["act_mark"] + j + 1)
                        dve.tensor_reduce(rs[:, j:j + 1], AB[:, j % 2], AX, ALU.add).then_inc(S["dve_mark"], 1)
                    dve.wait_ge(S["dve_mark"], d["dve_mark"] + 3)
                    dve.wait_ge(S["pe_mark"], d["pe_mark"] + 1)
                    L(dve.tensor_scalar(SC[:, 0:3], PS[:, 0, 0:3], 1.0 / (F3 * D), 1e-8, ALU.mult, ALU.add))
                    L(dve.tensor_scalar(th[:, 0, 0:3], SC[:, 0:3], 0.5, None, ALU.mult))
                    L(dve.tensor_scalar(th[:, 1, 0:3], SC[:, 0:3], -0.5, None, ALU.mult))
                    for j, w in enumerate(mats):
                        L(dve.tensor_scalar(AB[:, 0], w, th[:, 1, j:j + 1], None, ALU.is_lt))
                        L(dve.scalar_tensor_tensor(w, w, th[:, 0, j:j + 1], AB[:, 0], ALU.is_gt, ALU.subtract))
            done["act_mark"] += 3
            done["dve_mark"] += 3
            done["pe_mark"] += 1

    load_all()

    def finish(st, pre, rows, **norm):
        layernorm(X, H, pre=pre, rows=rows, **norm)
        st.close()

    def cross16(left):
        hd = 16
        NR = 16 * NSTACK[hd]
        with ExitStack() as cs:
            SQ, SK = (cs.enter_context(nc.sbuf_tensor(x, [P, TT * P // hd, D], BF16)) for x in ("SQX", "SKX"))
            at0 = dict(done)

            def fetch(sp, g, dst, src, order):
                blk = slice(g * 2 * P // hd, (g + 1) * 2 * P // hd)
                fetch_parts(sp, hd, lambda _: dst[:, blk],
                            lambda which, _: src[which, g * 2 * P:(g + 1) * 2 * P, :].rearrange("(a d) c -> d a c", d=hd),
                            order, f"stacked{g}")

            with ExitStack() as ss:
                SPL = ss.enter_context(nc.sbuf_tensor("SPLX", [P, TT // 2, 3, 2, D], BF16))
                REST = CX[:].rearrange("p (g t) d -> p g t d", t=2)

                def send(sp, g, d):
                    if g == 0:
                        fetch(sp, 0, SK, xk_parts, PARTS_K)
                    sp.wait_ge(S["part_l"], d["part_l"] + g + 1)
                    for t in range(2):
                        sp.dma_start(xq_parts[:, (2 * g + t) * P:(2 * g + t + 1) * P, :].rearrange("a p c -> p a c"),
                                     SPL[:, g, :, t]).then_inc(S[f"chunk_out{g}"], 16)
                    if g == 1:
                        sp.wait_ge(S["chunk_out0"], d["chunk_out0"] + 32)
                        fetch(sp, 0, SQ, xq_parts, PARTS_Q)
                    if g == TT // 2 - 1:
                        for n in range(1, TT // 2):
                            sp.wait_ge(S[f"chunk_out{n}"], d[f"chunk_out{n}"] + 32)

                st, pre, rows = left
                layernorm(X, H, pre=pre, rows=rows, split=(SPL, REST, send))
                for g in range(TT // 2):
                    done[f"chunk_out{g}"] += 32
            st.close()

            def rest(sp):
                for g in range(1, TT // 2):
                    fetch(sp, g, SK, xk_parts, PARTS_K)
                    fetch(sp, g, SQ, xq_parts, PARTS_Q)

            def arrivals(bb):
                batches = [bb] if isinstance(bb, int) else range(2, B)
                return [(f"stacked{g}", at0[f"stacked{g}"] + 2 * NR) for g in batches]

            stacked_cross(hd, SQ, SK, (arrivals, rest))
            for g in range(TT // 2):
                done[f"stacked{g}"] += 2 * NR

    def context_parts():
        st = ExitStack()
        SPL = st.enter_context(nc.sbuf_tensor("SPLC", [P, 3, TT, D], BF16))
        REST = st.enter_context(nc.sbuf_tensor("RESTC", [P, TT, D], F32))

        def vector(dve):
            L = lambda ins: link(dve, ins, "dve_chain")
            L(dve.tensor_copy(SPL[:, 0], CX[:]))
            L(dve.tensor_tensor(REST[:], CX[:], SPL[:, 0], ALU.subtract))
            L(dve.tensor_copy(SPL[:, 1], REST[:]))
            dve.tensor_tensor(SPL[:, 2], REST[:], SPL[:, 1], ALU.subtract).then_inc(S["part_l"], 1)

        def sync(sp, d):
            sp.wait_ge(S["part_l"], d["part_l"] + 1)
            for k in range(3):
                sp.dma_start(xk_parts[k].rearrange("(t p) c -> p t c", p=P), SPL[:, k]).then_inc(S["parts_out"], 16)
            sp.wait_ge(S["parts_out"], d["parts_out"] + 48)

        return st, vector, sync

    def layers():
        layernorm(X, H, to_HT, first=True)
        left = self_attention(0, {"q": wA("q0", KD), "qp": wA("qp0", KD), "k": wA("k0", KD), "kp": wA("kp0", KD),
                                  "v": wA("v0", KD), "o": wA("o0", 4)}, 4, 32, D ** -0.5, softcap=50.0,
                              arrived=(S["a_in"], 16))
        finish(*left)
        turn_context()
        cross_attention(32)
        quantise_fp4()
        layernorm(X, H, to_HT)
        up0 = wA("up0", KD)
        dn0 = wA("dn0", 8)
        with nc.Block() as block:
            @block.gpsimd
            def _(pool):
                pool.wait_ge(S["b_in"], 64)
        st, vector, sync = context_parts()
        mlp(F0 // P, up=lambda i, k: up0[:, k, i * P:(i + 1) * P], gate=None, down=lambda i: dn0[:, i, :], mode="gelu",
            bias=vv("b_up0"), load=sync, beside=vector)
        st.close()
        done["part_l"] += 1
        done["parts_out"] += 48
        layernorm(X, H, pre=add_sums())
        finish(*mixing())
        with nc.Block() as block:
            @block.sync
            def _(sp):
                sp.dma_start(WA[:, 0:L_N], wl).then_inc(S["late_in"], 16)
        cross_attention(32, gamma=rv("gamma"))
        layernorm(X, H, to_HT)
        experts1()
        wb_store.close()
        layernorm(X, H, to_HT)
        left = stacked_attention(2, {"q": wL("q2", KD), "qp": wL("qp2", KD), "k": wL("k2", KD), "kp": wL("kp2", KD),
                                  "v": wL("v2", KD), "o": wL("o2", KD)}, 2, 8, 8 ** -0.5, arrived=(S["late_in"], 16))
        cross16(left)
        layernorm(X, H, to_HT)
        experts2()
        layernorm(X, H, to_HT, pre=add_sums())
        left = stacked_attention(3, {"q": wL("q3", KD), "qp": wL("qp3", KD), "k": wL("k3", KD), "kp": wL("kp3", KD),
                                  "v": wL("v3", KD), "o": wL("o3", KD)}, 2, 16, 0.25)
        finish(*left, dstT=to_HT)
        wkv_scan()
        SC = sb("SC", [P, 4])
        ternary(SC)
        layernorm(X, H, to_HT)
        up3, gate3, dn3 = wL("up3", KD), wL("gate3", KD), wL("dn3", 8)
        mlp(F3 // P, up=lambda i, k: up3[:, k, i * P:(i + 1) * P], gate=lambda i, k: gate3[:, k, i * P:(i + 1) * P],
            down=lambda i: dn3[:, i, :], mode="silu", scales=SC)
        with nc.Block() as block:
            @block.vector
            def _(dve):
                for g in range(TT // 2):
                    v = X[:, 2 * g:2 * g + 2, :]
                    ps = PS[:, 4 + g, :].rearrange("p (t n) -> p t n", t=2)
                    dve.scalar_tensor_tensor(v, ps, SC[:, 2:3], v, ALU.mult, ALU.add).then_inc(S["x_added"], 1)

            @block.sync
            def _(sp):
                half = TT // 2
                for h in range(2):
                    sp.wait_ge(S["x_added"], done["x_added"] + 2 * (h + 1))
                    sp.dma_start(tok(out)[:, h * half:(h + 1) * half, :], X[:, h * half:(h + 1) * half, :]
                                 ).then_inc(S["out_done"], 16)
                sp.wait_ge(S["out_done"], 32)

    layers()
    es.close()


def blocks(w):
    k = w.shape[0] // P
    return w.reshape(k, P, -1).transpose(1, 0, 2).reshape(P, -1)


def column_of(v):
    return v.reshape(-1, P).T


def swapped(w, hd, paired):
    i = np.arange(w.shape[1])
    h, dd = i // hd, i % hd
    other = dd ^ 1 if paired else (dd + hd // 2) % hd
    return w[:, h * hd + other]


def gqa(wq, wk, wv, wo, hd, group, paired):
    if hd == 32:
        order = [2 * (4 * kb + s) + r for kb in range(2) for r in range(2) for s in range(4)]
        cols = np.concatenate([np.arange(h * hd, (h + 1) * hd) for h in order])
        wq, wo = wq[:, cols], wo[cols]
    else:
        cols = np.concatenate([np.arange(h // group * hd, (h // group + 1) * hd) for h in range(D // hd)])
        wk, wv = wk[:, cols], wv[:, cols]
    return [blocks(a) for a in (wq, swapped(wq, hd, paired), wk, swapped(wk, hd, paired), wv, wo)]


def layout(i):
    n = {k: np.asarray(v) for k, v in i.items()}
    cat = lambda xs: np.ascontiguousarray(np.concatenate(xs, axis=1))
    g0 = gqa(n["L0_attn_Wq"], n["L0_attn_Wk"], n["L0_attn_Wv"], n["L0_attn_Wo"], 32, 2, False)
    wa = cat(g0 + [blocks(n["L0_ffn_up_kernel"].T), blocks(n["L0_ffn_down_kernel"].T)]
             + [blocks(n["L1_attn_" + k].T) for k in ("tm_Wr", "tm_Wk", "tm_Wv", "tm_Wout", "cm_Wr", "cm_Wk", "cm_Wv")])
    f = lambda k: n["L1_ffn_" + k]
    wb = cat([blocks(f("down_w")), blocks(f("up_w")), blocks(f("router_w")), f("shared_w1"), f("shared_w2"),
              blocks(f("core_w"))] + [f(f"e{e}_w1") for e in range(E1)] + [blocks(f(f"e{e}_w2")) for e in range(E1)])
    g2 = gqa(n["L2_attn_wq"], n["L2_attn_wk"], n["L2_attn_wv"], n["L2_attn_wo"], 8, 4, True)
    g3 = gqa(n["L3_attn_wq"], n["L3_attn_wk"], n["L3_attn_wv"], n["L3_attn_wo"], 16, 4, False)
    router2 = np.concatenate([n["L2_ffn_router_w"].T, n["L2_ffn_sh_gate_w"]], axis=1)
    wl = cat(g2 + g3 + [blocks(n["L3_ffn_W_up"].T), blocks(n["L3_ffn_W_gate"].T), blocks(n["L3_ffn_W_down"].T),
                        blocks(router2)])
    pad = NI2 * P - E2 * I2 - ISH
    wide = lambda w, s: np.concatenate([w.transpose(1, 0, 2).reshape(D, -1), s, np.zeros((D, pad), np.float32)], axis=1)
    gate, up = wide(n["L2_ffn_w_gate"], n["L2_ffn_sh_gate"]), wide(n["L2_ffn_w_up"], n["L2_ffn_sh_up"])
    down = np.concatenate([n["L2_ffn_w_down"].reshape(-1, D), n["L2_ffn_sh_down"], np.zeros((pad, D), np.float32)])
    halves = lambda w: w.reshape(KD, P, NI2, P).transpose(2, 1, 0, 3).reshape(NI2, P, KD * P)
    w2f = np.ascontiguousarray(np.concatenate([halves(gate), halves(up), down.reshape(NI2, P, D)], axis=2))
    a = lambda k: column_of(n["L1_attn_" + k])
    vec = cat([column_of(n["L0_ffn_up_bias"])] + [a(k) for k in ("ln1_g", "ln1_b", "ln2_g", "ln2_b", "tm_u", "tm_mu_r",
              "tm_mu_k", "tm_mu_v", "cm_mu_r", "cm_mu_k")]
              + [column_of(f(k)) for k in ("down_b", "shared_b1", "shared_b2")] + [column_of(f(f"e{e}_b1")) for e in range(E1)]
              + [column_of(f(f"e{e}_b2")) for e in range(E1)] + [column_of(n["L3_xattn_w"]), column_of(n["L3_xattn_u"])])
    rowv = cat([n["L0_ffn_down_bias"][None], f("up_b")[None], f("core_b")[None], f("router_b")[None],
                n["L1_xattn_gamma"].reshape(1, 1)])
    return {"x": n["x"], "ctx": n["ctx_2048"], "wa": wa, "wb": wb, "wl": wl, "w2f": w2f, "vec": vec, "rowv": rowv,
            "const": shape_constants()}


def kernel(**inputs):
    import concourse.bacc as bacc
    from concourse.bass_utils import run_bass_kernel_spmd

    nc = bacc.Bacc("TRN2", target_bir_lowering=False, num_devices=1)
    arrays = layout(inputs)
    aps = {k: nc.dram_tensor(k + "_in", a.shape, mybir.dt.from_np(a.dtype), kind="ExternalInput").ap()
           for k, a in arrays.items()}
    out = nc.dram_tensor("out", (B, T, D), F32, kind="ExternalOutput").ap()
    build_decoder(nc, out=out, **aps)
    r = run_bass_kernel_spmd(nc, [{k + "_in": a for k, a in arrays.items()}], core_ids=[0])
    return r.results[0]["out"]
```

```python
from contextlib import ExitStack

import numpy as np

import concourse.bass as bass
from concourse import mybir

F32 = mybir.dt.float32
BF16 = mybir.dt.bfloat16
U32 = mybir.dt.uint32
ALU = mybir.AluOpType
ACT = mybir.ActivationFunctionType
AX = mybir.AxisListType.X

P = 128
B, T, D = 4, 256, 256
TT = B * T // P
KD = D // P
CH = 512
NCH = B * T // CH
TPC = CH // P
EPS = 1e-5
NEG = -1e30

HID = [128, 256, 384, 512, 128, 256, 384, 512]
E1 = len(HID)
FB1 = [h // P for h in HID]
E2, I2, ISH = 16, 176, 704
NI2 = -(-(E2 * I2 + ISH) // P)
F3 = 1024
F0 = 1024

A_SIZES = {
    "q0": 2 * 512, "qp0": 2 * 512, "k0": 512, "kp0": 512, "v0": 512, "o0": 4 * 256,
    "upT0": 2048, "dnT0": 2048, "up0": 2048, "dn0": 2048,
    "wr": 512, "wk": 512, "wv": 512, "wout": 512, "cr": 512, "ck": 512, "cv": 512,
}
B_SIZES = {"down": KD * P, "up": D, "router": KD * E1, "sh1": P, "sh2": P, "core": KD * D,
           "w1": sum(HID), "w2": sum(FB1) * P}
L_SIZES = {"q2": 512, "qp2": 512, "k2": 512, "kp2": 512, "v2": 512, "o2": 512,
           "q3": 512, "qp3": 512, "k3": 512, "kp3": 512, "v3": 512, "o3": 512,
           "up3": 2048, "gate3": 2048, "dn3": 2048,
           "router2": KD * (E2 + 1)}
V_SIZES = {"b_up0": 8, "ln1_g": 2, "ln1_b": 2, "ln2_g": 2, "ln2_b": 2, "u": 2,
           "mu_r": 2, "mu_k": 2, "mu_v": 2, "cmu_r": 2, "cmu_k": 2,
           "b_down1": 1, "b_sh1": 1, "b_sh2": 1, "b1": sum(FB1), "b2": E1, "w3": 2, "u3": 2}
R_SIZES = {"b_dn0": D, "b_up1": D, "b_core": D, "b_router": E1, "gamma": 1}

PARTS_Q = (0, 0, 1, 0, 1, 2, 1, 2)
PARTS_K = (0, 1, 0, 2, 1, 0, 2, 1)
NSTACK = {8: 8, 16: 6}


def columns(sizes):
    at, n = {}, 0
    for name, size in sizes.items():
        at[name] = (n, size)
        n += size
    return at, n


A_AT, A_N = columns(A_SIZES)
B_AT, B_N = columns(B_SIZES)
L_AT, L_N = columns(L_SIZES)
V_AT, V_N = columns(V_SIZES)
R_AT, R_N = columns(R_SIZES)
RING2 = 4
RINGG = 2
RAW_A = ["q0", "qp0", "k0", "kp0", "v0", "o0", "upT0", "dnT0"]

C_SIZES = {"ident": P, "ones": P, "cos32": T, "sin32": T, "cos8": T, "sin8": T, "cos16": T, "sin16": T,
           "tril": P, "lower8": E1 * E1, "lower16": E2 * E2, "cost": E1, "eps": 1,
           "rows32": 4, "rows8": 16, "rows16": 8, "cols32": 32, "cols8": 4 * 32, "cols16": 2 * 32}
C_AT, C_N = columns(C_SIZES)


def shape_constants():
    c = np.zeros((P, C_N), np.float32)

    def put(name, a):
        at, n = C_AT[name]
        c[:, at:at + n] = np.asarray(a, np.float32).reshape(P, n)

    put("ident", np.eye(P))
    put("ones", np.ones((P, P)))
    pos = np.arange(T, dtype=np.float32)
    row = np.arange(P)
    for hd, paired in ((32, False), (8, True), (16, False)):
        inv = (np.float32(1.0) / np.float32(10000.0) ** (np.arange(0, hd, 2).astype(np.float32) / np.float32(hd))).astype(np.float32)
        ang = pos[None, :] * inv[:, None]
        d = row % hd
        freq = d // 2 if paired else d % (hd // 2)
        first = d % 2 == 0 if paired else d < hd // 2
        put(f"cos{hd}", np.cos(ang)[freq])
        put(f"sin{hd}", np.sin(ang)[freq] * np.where(first, -1.0, 1.0)[:, None])
        r = 32 // hd
        rows = np.zeros((P, r, 4))
        for s in range(4):
            for v in range(r):
                rows[32 * s + v * hd:32 * s + (v + 1) * hd, v, s] = 1.0
        put(f"rows{hd}", rows)
        cols = np.zeros((P, r, 32))
        for v in range(r):
            cols[:, v, v * hd:(v + 1) * hd] = 1.0
        put(f"cols{hd}", cols)
    put("tril", np.tril(np.ones((P, P))))
    for e in (E1, E2):
        put(f"lower{e}", np.broadcast_to(np.tril(np.ones((e, e)), -1), (P, e, e)))
    cost = np.float32(1e-07) * np.array([2 * P * h for h in HID], np.float32)
    put("cost", np.broadcast_to(cost, (P, E1)))
    put("eps", np.full((P, 1), EPS))
    return c


def build_decoder(nc, x, ctx, wa, wb, wl, w2f, vec, rowv, const, out):
    es = ExitStack()

    def sb(name, shape, dt=F32):
        return es.enter_context(nc.sbuf_tensor(name, shape, dt))

    def sem(name):
        return es.enter_context(nc.semaphore(name))

    X = sb("X", [P, TT, D])
    H = sb("H", [P, TT, D])
    HT = sb("HT", [P, KD, B * T])
    CX = sb("CX", [P, TT, D])
    CXT = sb("CXT", [P, KD, B * T])
    WA = sb("WA", [P, A_N])
    VEC = sb("VEC", [P, V_N])
    ROW = sb("ROW", [P, R_N])
    CST = sb("CST", [P, C_N])
    identb = sb("identb", [P, P], BF16)
    maskb = sb("maskb", [P, P], BF16)
    wb_store = ExitStack()
    WB = wb_store.enter_context(nc.sbuf_tensor("WB", [P, B_N], F32))
    PS = es.enter_context(nc.psum_tensor("PS", [P, 8, 512], F32))
    gate_rows = nc.dram_tensor("gate_rows", [E2 + 1, B * T], F32, kind="Internal").ap()
    q_parts, k_parts = (nc.dram_tensor(x, [3, D, B * T], BF16, kind="Internal").ap() for x in ("q_parts", "k_parts"))
    xq_parts, xk_parts = (nc.dram_tensor(x, [3, TT * P, D], BF16, kind="Internal").ap() for x in ("xq_parts", "xk_parts"))

    def part(store, at, name, k=None):
        a, n = at[name]
        v = store[:, a:a + n]
        return v if k is None else v.rearrange("p (k n) -> p k n", k=k)

    wA = lambda name, k=None: part(WA, A_AT, name, k)
    wB = lambda name, k=None: part(WB, B_AT, name, k)
    wL = lambda name, k=None: part(WA, L_AT, name, k)
    vv = lambda name: part(VEC, V_AT, name)
    rv = lambda name: part(ROW, R_AT, name)
    cst = lambda name, k=None: part(CST, C_AT, name, k)
    ident = cst("ident")

    def tok(a):
        return a.rearrange("b (h p) d -> p (b h) d", p=P)

    names = ["x_in0", "x_in1", "ctx_in", "const_in", "a_in", "kernels_in", "b_in", "late_in", "ctx_copied", "quantised",
             "abs_sums", "abs_total",
             "stats", "moments", "std", "rstd", "normed", "turned",
             "q_staged", "k_staged", "v_staged", "scores", "row_max", "bias", "exps", "turn_a", "turn_b",
             "copied_a", "copied_b", "pv", "den_inv", "heads_out", "masked",
             "proj", "rope_cos", "rope_sin", "rope_sum", "v_proj", "v_out", "o_proj", "x_added",
             "up_ps", "act_out", "down_ps", "mult_out", "dve_chain", "pe_mark",
             "dve_mark", "act_mark", "pool_mark", "first_bias", "narrow", "bias_gelu", "gates", "gates_sent", *(f"gates_back{e}" for e in range(E1)),
             "part_h", "rest", "part_m", "part_l", "parts_out", "chunk_out0", "chunk_out1", "chunk_out2", "chunk_out3",
             "stacked0", "stacked1", "stacked2", "stacked3",
             "maxima", "keep", "top", "new", "keys", "old", "keep_exp", "key_exp", "new_exp", "old_exp", "key_values",
             "new_values", "old_values", "numerators", "inverse", "outputs", "quotients",
             "out_done"] + [f"w_slot{j}" for j in range(RING2)] + [f"g_slot{j}" for j in range(RINGG)]
    S = {n: sem(n) for n in names}
    done = dict.fromkeys(names, 0)

    def link(eng, ins, name):
        done[name] += 1
        ins.then_inc(S[name], 1)
        eng.wait_ge(S[name], done[name])

    def load_all():
        with nc.Block() as block:
            @block.sync
            def _(sp):
                half = TT // 2
                sp.dma_start(X[:, 0:half, :], tok(x)[:, 0:half, :]).then_inc(S["x_in0"], 16)
                sp.dma_start(X[:, half:TT, :], tok(x)[:, half:TT, :]).then_inc(S["x_in1"], 16)
                sp.dma_start(CST[:], const).then_inc(S["const_in"], 16)
                raw = sum(A_SIZES[n] for n in RAW_A)
                last = A_AT["wr"][0]
                first = A_AT["o0"][0]
                sp.dma_start(WA[:, 0:first], wa[:, 0:first]).then_inc(S["a_in"], 16)
                sp.dma_start(WA[:, first:raw], wa[:, first:raw]).then_inc(S["kernels_in"], 16)
                sp.dma_start(CX[:], tok(ctx)).then_inc(S["ctx_in"], 16)
                sp.dma_start(VEC[:], vec).then_inc(S["b_in"], 16)
                sp.dma_start(ROW[:], rowv.to_broadcast([P, R_N])).then_inc(S["b_in"], 16)
                sp.dma_start(WA[:, last:A_N], wa[:, raw:]).then_inc(S["b_in"], 16)
                sp.dma_start(WB[:], wb).then_inc(S["b_in"], 16)

    def masks(dve):
        dve.wait_ge(S["const_in"], 16)
        dve.tensor_copy(identb[:], ident)
        dve.tensor_scalar(maskb[:], cst("tril"), -1.0, -NEG, ALU.add, ALU.mult)

    def layernorm(src, dst, dstT=None, gain=None, shift=None, first=False, rows=None, pre=None, split=None):
        with ExitStack() as st:
            tag = str(nc.next_id())
            stats = st.enter_context(nc.sbuf_tensor("stats" + tag, [P, TT, 6], F32))
            mom = st.enter_context(nc.sbuf_tensor("mom" + tag, [P, TT, 2], F32))
            std = st.enter_context(nc.sbuf_tensor("std" + tag, [P, TT], F32))
            rstd = st.enter_context(nc.sbuf_tensor("rstd" + tag, [P, TT], F32))
            NG = TT // 2
            d = dict(done)
            tbank = (lambda g: 2 * g) if rows is not None else (lambda g: g)

            with nc.Block() as block:
                @block.vector
                def _(dve):
                    def measure(g):
                        if first:
                            dve.wait_ge(S[f"x_in{g // 2}"], 16)
                        if rows is not None:
                            dve.wait_ge(S["o_proj"], d["o_proj"] + 2 * g + 2)
                        if pre is not None:
                            pre(dve, g)
                        for t in (2 * g, 2 * g + 1):
                            dve.bn_stats(stats[:, t, :], src[:, t, :]).then_inc(S["stats"], 1)
                        for t in (2 * g, 2 * g + 1):
                            dve.wait_ge(S["stats"], d["stats"] + t + 1)
                            dve.bn_aggr(mom[:, t, :], stats[:, t, :]).then_inc(S["moments"], 1)

                    def apply(g):
                        dve.wait_ge(S["std"], d["std"] + g + 1)
                        dve.reciprocal(rstd[:, 2 * g:2 * g + 2], std[:, 2 * g:2 * g + 2]).then_inc(S["rstd"], 1)
                        dve.wait_ge(S["rstd"], d["rstd"] + g + 1)
                        for t in (2 * g, 2 * g + 1):
                            dve.tensor_scalar(dst[:, t, :], src[:, t, :], mom[:, t, 0:1], rstd[:, t:t + 1],
                                              ALU.subtract, ALU.mult).then_inc(S["normed"], 1)

                    for g in range(NG + 1):
                        if g < NG:
                            measure(g)
                        if g:
                            apply(g - 1)

                @block.scalar
                def _(act):
                    def root(g):
                        if first and g == 0:
                            act.wait_ge(S["const_in"], 16)
                        act.wait_ge(S["moments"], d["moments"] + 2 * g + 2)
                        act.activation(std[:, 2 * g:2 * g + 2], mom[:, 2 * g:2 * g + 2, 1], ACT.Sqrt,
                                       bias=cst("eps")).then_inc(S["std"], 1)

                    def copy(g):
                        act.wait_ge(S["turned"], d["turned"] + g + 1)
                        src_ps = PS[:, tbank(g), :].rearrange("p (k n) -> p k n", k=KD)
                        if gain is None:
                            act.activation(dstT(slice(0, KD), g), src_ps, ACT.Copy)
                        else:
                            for k in range(KD):
                                act.activation(dstT(k, g), src_ps[:, k, :], ACT.Identity,
                                               bias=shift[:, k:k + 1], scale=gain[:, k:k + 1])

                    def high(g):
                        act.wait_ge(S["normed"], d["normed"] + 2 * g + 2)
                        act.activation(split[0][:, g, 0], dst[:, 2 * g:2 * g + 2, :], ACT.Copy).then_inc(S["part_h"], 1)

                    def middle(g):
                        act.wait_ge(S["rest"], d["rest"] + g + 1)
                        act.activation(split[0][:, g, 1], split[1][:, g], ACT.Copy).then_inc(S["part_m"], 1)

                    for g in range(NG + 2):
                        if g < NG:
                            root(g)
                        if split is not None and 1 <= g <= NG:
                            high(g - 1)
                        if split is not None and g >= 2:
                            middle(g - 2)
                        if g >= 2 and dstT is not None:
                            copy(g - 2)

                if split is not None:
                    @block.gpsimd
                    def _(pool):
                        def low(g):
                            pool.wait_ge(S["part_m"], d["part_m"] + g + 1)
                            pool.tensor_tensor(split[0][:, g, 2], split[1][:, g], split[0][:, g, 1], ALU.subtract
                                               ).then_inc(S["part_l"], 1)

                        for g in range(NG + 1):
                            if g < NG:
                                pool.wait_ge(S["part_h"], d["part_h"] + g + 1)
                                pool.tensor_tensor(split[1][:, g], dst[:, 2 * g:2 * g + 2, :], split[0][:, g, 0], ALU.subtract
                                                   ).then_inc(S["rest"], 1)
                            if g:
                                low(g - 1)

                    @block.sync
                    def _(sp):
                        for g in range(NG):
                            split[2](sp, g, d)

                if dstT is not None or rows is not None:
                    @block.tensor
                    def _(pe):
                        def product(g):
                            lhs, rhs, nk = rows
                            for t in (2 * g, 2 * g + 1):
                                for k in range(nk):
                                    last = pe.matmul(PS[:, t, 0:D], lhs(k, t), rhs(k), start=k == 0, stop=k == nk - 1)
                                last.then_inc(S["o_proj"], 1)

                        def turn(g):
                            if first and g == 0:
                                pe.wait_ge(S["const_in"], 16)
                            pe.wait_ge(S["normed"], d["normed"] + 2 * g + 2)
                            for k in range(KD):
                                for j in range(2):
                                    last = pe.transpose(PS[:, tbank(g), k * 256 + j * P:k * 256 + (j + 1) * P],
                                                        dst[:, 2 * g + j, k * P:(k + 1) * P], ident)
                            last.then_inc(S["turned"], 1)

                        for g in range(NG + 2):
                            if rows is not None and g < NG:
                                product(g)
                            if g >= 2 and dstT is not None:
                                turn(g - 2)
            for n, k in (("stats", TT), ("moments", TT), ("std", NG), ("rstd", NG), ("normed", TT),
                         ("turned", NG if dstT is not None else 0), ("o_proj", TT if rows is not None else 0),
                         *((n, NG if split is not None else 0) for n in ("part_h", "rest", "part_m", "part_l"))):
                done[n] += k

    def add_product(dst):
        def pre(dve, g):
            v = dst[:, 2 * g:2 * g + 2, :]
            link(dve, dve.tensor_tensor(v, v, PS[:, 2 * g:2 * g + 2, 0:D], ALU.add), "dve_chain")
        return pre

    def add_sums():
        def pre(dve, g):
            v = X[:, 2 * g:2 * g + 2, :]
            ps = PS[:, 4 + g, :].rearrange("p (t n) -> p t n", t=2)
            link(dve, dve.tensor_tensor(v, ps, v, ALU.add), "dve_chain")
        return pre

    def to_HT(k, g):
        return HT[:, k, g * 256:(g + 1) * 256]

    def attention(hd, units, causal, scale, q_of, k_of, v_of, out_of, softcap=None, gamma=None,
                  stack=None, beside=None):
        r = 32 // hd
        npair = 2 * r
        width = 384 if causal else 512
        d = dict(done)
        tag = str(nc.next_id())
        with ExitStack() as st:
            def tmp(name, shape, dt=F32):
                return st.enter_context(nc.sbuf_tensor(name + tag, shape, dt))

            if stack is None:
                QS = tmp("QS", [P, 2, T])
                KM = tmp("KM", [P, 2, 4, T])
            VM = tmp("VM", [P, 2, 2, r, P])
            PR = tmp("PR", [P, 2, 2, 512])
            PT = tmp("PT", [P, 2, 2, 512])
            MX = tmp("MX", [P, 2, 4])
            NB = tmp("NB", [P, 2, 4])
            DI = tmp("DI", [P, 2, T])
            if not causal:
                OU = tmp("OU", [P, 2, T])
            rows = cst(f"rows{hd}", r)
            cols = cst(f"cols{hd}", r)

            def where(u, p):
                quad = p // 2
                slots = (2 * (p % 2), 2 * (p % 2) + 1)
                return quad, slots, (u * r + quad) % 2

            def steps():
                return [(u, p) for u in range(units) for p in range(npair)]

            NU = units * npair

            def ahead(bb, i, last):
                if i + 2 < NU:
                    return bb, i + 2
                return None if last else (bb + 1, i + 2 - NU)

            def batches(eng, body):
                body(0, False, True)
                with eng.Fori(1, B - 1) as bb:
                    body(bb, False)
                body(B - 1, True)

            with nc.Block() as block:
                if stack is not None:
                    @block.sync
                    def _(sp):
                        stack[3](sp)

                @block.gpsimd
                def _(pool):
                    def values(bb, u, U):
                        pool.wait_ge(S["pv"], (U + 1) * npair + d["pv"])
                        for n2 in range(2):
                            pool.tensor_tensor(
                                VM[:, u % 2, n2].rearrange("p r (s c) -> p r s c", s=4),
                                v_of(bb, u, n2).rearrange("p (a s c) -> p a s c", a=1, s=4).to_broadcast([P, r, 4, 32]),
                                cols.rearrange("p r (a c) -> p r a c", a=1).to_broadcast([P, r, 4, 32]),
                                ALU.mult).then_inc(S["v_staged"], 1)

                    def batch(bb, last):
                        for u in range(units):
                            U = bb * units + u
                            if stack is not None:
                                values(bb, u, U)
                                continue
                            pool.wait_ge(S["scores"], (U + 1) * npair + d["scores"])
                            pool.tensor_copy(QS[:, u % 2, :], q_of(bb, u)).then_inc(S["q_staged"], 1)
                            for q in range(r):
                                n = u * r + q
                                Q = bb * (units * r) + n
                                pool.wait_ge(S["scores"], Q * 2 + (2 * npair - 2 + d["scores"]))
                                pool.tensor_tensor(
                                    KM[:, n % 2], k_of(bb, u).rearrange("p (a t) -> p a t", a=1).to_broadcast([P, 4, T]),
                                    rows[:, q, :].rearrange("p (s a) -> p s a", a=1).to_broadcast([P, 4, T]),
                                    ALU.mult).then_inc(S["k_staged"], 1)
                                if q == 0:
                                    values(bb, u, U)

                    for bb in range(B):
                        batch(bb, bb == B - 1)

                @block.tensor
                def _(pe):
                    pe.nop().then_inc(S["scores"], 2 * npair)
                    pe.nop().then_inc(S["pv"], 2 * npair)
                    pe.nop().then_inc(S["turn_b"], 2)

                    def score(bb, i):
                        u, p = i // npair, i % npair
                        quad, slots, kb = where(u, p)
                        G = bb * NU + i
                        if stack is not None and i == 0:
                            for name, count in stack[2](bb):
                                pe.wait_ge(S[name], count)
                        if p == 0 and stack is None:
                            pe.wait_ge(S["q_staged"], bb * units + (u + 1 + d["q_staged"]))
                        if p % 2 == 0 and stack is None:
                            pe.wait_ge(S["k_staged"], bb * (units * r) + (u * r + quad + 1 + d["k_staged"]))
                        pe.wait_ge(S["exps"], G + (1 + d["exps"]))
                        for h in range(2):
                            bank = PS[:, 2 * (i % 2) + h, :]
                            for m in range(2):
                                n = P * (m + 1) if causal else T
                                if stack is None:
                                    q, k = QS[:, u % 2, m * P:(m + 1) * P], KM[:, kb, slots[h], 0:n]
                                else:
                                    q, k = stack[0](bb, u, slots[h], quad, m * P, P), stack[1](bb, u, slots[h], quad, 0, n)
                                last = pe.matmul(bank[:, m * T:m * T + n], q, k, start=True, stop=softcap is not None or not causal,
                                                 skip_group_check=True)
                                if causal and softcap is None:
                                    last = pe.matmul(bank[:, m * T + m * P:m * T + (m + 1) * P], identb[:], maskb[:],
                                                     start=False, stop=True, skip_group_check=True)
                        last.then_inc(S["scores"], 1)

                    def turn(bb, i):
                        G = bb * NU + i
                        ready = "masked" if softcap is not None else "exps"
                        pe.wait_ge(S[ready], G + ((1 if softcap is not None else 3) + d[ready]))
                        for h in range(2):
                            pe.wait_ge(S["copied_a" if h == 0 else "copied_b"], G + (1 + d["copied_a" if h == 0 else "copied_b"]))
                            for n in range(2):
                                for m in range(n if causal else 0, 2):
                                    col = n * T + m * P - (P if causal and n else 0)
                                    last = pe.transpose(PS[:, 4 + h, col:col + P],
                                                        PR[:, i % 2, h, m * T + n * P:m * T + (n + 1) * P], ident)
                            last.then_inc(S["turn_a" if h == 0 else "turn_b"], 1)

                    def product(bb, i):
                        u, p = i // npair, i % npair
                        quad, slots, _ = where(u, p)
                        G = bb * NU + i
                        pe.wait_ge(S["copied_a"], G + (2 + d["copied_a"]))
                        pe.wait_ge(S["copied_b"], G + (2 + d["copied_b"]))
                        if p == 0:
                            pe.wait_ge(S["v_staged"], bb * (2 * units) + (2 * u + 2 + d["v_staged"]))
                            pe.wait_ge(S["heads_out"], bb * units + (u + 1 + d["heads_out"]))
                        bank = PS[:, 6 + u % 2, :]
                        for n in range(2):
                            for what in range(2):
                                for h in range(2):
                                    s = slots[h]
                                    at = 32 * (s if what == 0 else (s + 2) % 4)
                                    lo = P if causal and n else 0
                                    src = PT[:, i % 2, h, T:width] if n else PT[:, i % 2, h, 0:T]
                                    lhs = VM[:, u % 2, n, quad, 32 * s:32 * s + 32] if what == 0 else cols[:, quad, :]
                                    last = pe.matmul(bank[at:at + 32, what * T + lo:what * T + T], lhs, src,
                                                     start=p == 0 and n == 0, stop=p == npair - 1 and n == 1,
                                                     skip_group_check=True, tile_position=(0, at))
                        last.then_inc(S["pv"], 1)

                    score(0, 0)
                    score(0, 1)

                    def batch(bb, last, first=False):
                        for i in range(NU):
                            nxt = ahead(bb, i, last)
                            if nxt is not None:
                                score(*nxt)
                            turn(bb, i)
                            if i:
                                product(bb, i - 1)
                            elif not first:
                                product(bb - 1, NU - 1)
                        if last:
                            product(bb, NU - 1)

                    batches(pe, batch)

                @block.vector
                def _(dve):
                    dve.nop().then_inc(S["copied_a"], 1)
                    dve.nop().then_inc(S["heads_out"], 2)

                    def maxima(bb, i):
                        G = bb * NU + i
                        pr = i % 2
                        if softcap is not None:
                            dve.wait_ge(S["bias"], G + (1 + d["bias"]))
                            v = PR[:, pr].rearrange("p h (a n) -> p h a n", a=4)[:, :, 0:4:3, :]
                            tri = cst("tril", 1).rearrange("p a (b n) -> p a b n", b=1).to_broadcast([P, 2, 2, P])
                            dve.tensor_tensor(v, v, tri, ALU.mult).then_inc(S["masked"], 1)
                            return
                        dve.wait_ge(S["scores"], G + (1 + 2 * npair + d["scores"]))
                        mx = MX[:, pr].rearrange("p (h m) -> p h m", h=2)
                        if causal:
                            v = PS[:, 2 * pr:2 * pr + 2, :]
                            dve.tensor_reduce(mx[:, :, 0], v[:, :, 0:P], AX, ALU.max).then_inc(S["row_max"], 1)
                            dve.tensor_reduce(mx[:, :, 1], v[:, :, T:2 * T], AX, ALU.max).then_inc(S["row_max"], 1)
                        else:
                            v = PS[:, 2 * pr:2 * pr + 2, :].rearrange("p h (m n) -> p (h m) n", m=2)
                            dve.tensor_reduce(MX[:, pr], v, AX, ALU.max).then_inc(S["row_max"], 2)
                        dve.wait_ge(S["row_max"], 2 * G + (2 + d["row_max"]))
                        dve.tensor_scalar(NB[:, pr], MX[:, pr], -scale, None, ALU.mult).then_inc(S["bias"], 1)

                    def copy(bb, i):
                        G = bb * NU + i
                        dve.wait_ge(S["turn_a"], G + (1 + d["turn_a"]))
                        dve.wait_ge(S["pv"], G + (2 * npair - 1 + d["pv"]))
                        dve.tensor_copy(PT[:, i % 2, 0, 0:width], PS[:, 4, 0:width]).then_inc(S["copied_a"], 1)

                    def invert(bb, u, half):
                        U = bb * units + u
                        if half == 0:
                            dve.wait_ge(S["pv"], (U + 3) * npair + d["pv"])
                        c = slice(half * P, (half + 1) * P)
                        dve.reciprocal(DI[:, u % 2, c], PS[:, 6 + u % 2, T + half * P:T + (half + 1) * P]
                                       ).then_inc(S["den_inv"], 1)

                    def normalise(bb, u):
                        U = bb * units + u
                        bank = PS[:, 6 + u % 2, :]
                        dve.wait_ge(S["den_inv"], 2 * U + (2 + d["den_inv"]))
                        dst, add = out_of(bb, u)
                        to = dst if add is None else OU[:, u % 2, :]
                        for lo in (0, P // 2):
                            hi = P // 2 - lo
                            ins = dve.tensor_tensor(to[lo:lo + P // 2], bank[lo:lo + P // 2, 0:T],
                                                    DI[hi:hi + P // 2, u % 2, :], ALU.mult)
                        ins.then_inc(S["heads_out"], 1)
                        if add is not None:
                            dve.wait_ge(S["heads_out"], U + (3 + d["heads_out"]))
                            dve.scalar_tensor_tensor(dst, OU[:, u % 2, :], 1.0 if gamma is None else gamma, dst,
                                                     ALU.mult, ALU.add)

                    late = 2 if npair == 2 else 3
                    after = [(2, lambda b, u: invert(b, u, 0)), (late, lambda b, u: invert(b, u, 1)), (late + 1, normalise)]

                    def finish_units(bb, i, first):
                        for delay, what in after:
                            if (i - delay + 1) % npair == 0:
                                u = (i - delay) // npair
                                if 0 <= u < units:
                                    what(bb, u)
                                elif u < 0 and not first:
                                    what(bb - 1, u + units)

                    maxima(0, 0)
                    maxima(0, 1)

                    def batch(bb, last, first=False):
                        for i in range(NU):
                            if softcap is not None:
                                copy(bb, i)
                            nxt = ahead(bb, i, last)
                            if nxt is not None:
                                maxima(*nxt)
                            if softcap is None:
                                copy(bb, i)
                            finish_units(bb, i, first)
                            if beside is not None:
                                beside(dve, bb, i, NU)
                        if last:
                            for i in range(NU, NU + late + 1):
                                finish_units(bb, i, False)

                    batches(dve, batch)

                @block.scalar
                def _(act):
                    act.nop().then_inc(S["copied_b"], 1)
                    act.nop().then_inc(S["exps"], 2)

                    def exps(bb, i):
                        G = bb * NU + i
                        pr = i % 2
                        act.wait_ge(S["turn_b"], G + (1 + d["turn_b"]))
                        if softcap is not None:
                            act.wait_ge(S["scores"], G + (1 + 2 * npair + d["scores"]))
                            for m in range(2):
                                n = P * (m + 1) if causal else T
                                v = PR[:, pr, :, m * T:m * T + n]
                                ins = act.activation(v, PS[:, 2 * pr:2 * pr + 2, m * T:m * T + n], ACT.Tanh, scale=scale / softcap)
                                if m == 1:
                                    ins.then_inc(S["exps"], 1)
                            act.wait_ge(S["exps"], G + (3 + d["exps"]))
                            for m in range(2):
                                n = P * (m + 1) if causal else T
                                v = PR[:, pr, :, m * T:m * T + n]
                                ins = act.activation(v, v, ACT.Exp, scale=softcap)
                            ins.then_inc(S["bias"], 1)
                            return
                        act.wait_ge(S["bias"], G + (1 + d["bias"]))
                        for h in range(2):
                            for m in range(2):
                                n = P * (m + 1) if causal else T
                                ins = act.activation(PR[:, pr, h, m * T:m * T + n], PS[:, 2 * pr + h, m * T:m * T + n],
                                                     ACT.Exp, bias=NB[:, pr, 2 * h + m:2 * h + m + 1], scale=scale)
                        ins.then_inc(S["exps"], 1)

                    def copy(bb, i):
                        G = bb * NU + i
                        act.wait_ge(S["turn_b"], G + (3 + d["turn_b"]))
                        act.wait_ge(S["pv"], G + (2 * npair - 1 + d["pv"]))
                        act.activation(PT[:, i % 2, 1, 0:width], PS[:, 5, 0:width], ACT.Copy).then_inc(S["copied_b"], 1)

                    exps(0, 0)
                    exps(0, 1)

                    def batch(bb, last, first=False):
                        for i in range(NU):
                            copy(bb, i)
                            nxt = ahead(bb, i, last)
                            if nxt is not None:
                                exps(*nxt)

                    batches(act, batch)

            n = B * NU
            for name, k in (("q_staged", B * units if stack is None else 0),
                            ("k_staged", B * units * r if stack is None else 0), ("v_staged", 2 * B * units),
                            ("scores", n + 2 * npair), ("row_max", 0 if softcap is not None else 2 * n), ("bias", n),
                            ("exps", n + 2), ("turn_a", n), ("turn_b", n + 2), ("copied_a", n + 1),
                            ("copied_b", n + 1), ("pv", n + 2 * npair), ("den_inv", 2 * B * units),
                            ("heads_out", B * units + 2), ("masked", n if softcap is not None else 0)):
                done[name] += k

    def project(w, nq, hd, QT, KT, V, arrived=None, split=None, first=None, beside=None,
                extra=None):
        d = dict(done)
        cos = cst(f"cos{hd}", 1)
        sin = cst(f"sin{hd}", 1)
        nchunk = CH // T
        work = [(w["q"], w["qp"], QT, j, c) for j in range(nq) for c in range(NCH)]
        work += [(w["k"], w["kp"], KT, j, c) for j in range(2) for c in range(NCH)]
        if split is not None:
            work = [(a, ap, to, j, c) for c in range(NCH) for (a, ap, to, j, c2) in work if c2 == c]
        with ExitStack() as st:
            tag = str(nc.next_id())
            if split is not None:
                SPL = st.enter_context(nc.sbuf_tensor("SPL" + tag, [P, len(work), 3, CH], BF16))
            RC = st.enter_context(nc.sbuf_tensor("RC" + tag, [P, 2, CH], F32))
            RS = st.enter_context(nc.sbuf_tensor("RS" + tag, [P, 2, CH], F32))
            ROT = RC
            REST = H[:].rearrange("p (s t) d -> p s (t d)", t=2)
            NREST = TT // 2
            def values_out(eng):
                for t in range(TT):
                    eng.wait_ge(S["v_proj"], d["v_proj"] + t + 1)
                    dst, src = V[:, t, :], PS[:, 4 + t % 2, 0:D]
                    ins = eng.tensor_copy(dst, src) if split is not None else eng.activation(dst, src, ACT.Copy)
                    ins.then_inc(S["v_out"], 1)

            with nc.Block() as block:
                @block.tensor
                def _(pe):
                    if arrived is not None:
                        pe.wait_ge(*arrived)
                    for n, (a, ap, _, j, c) in enumerate(work):
                        if n >= 2:
                            pe.wait_ge(S["rope_sin"], d["rope_sin"] + n - 1)
                        for half, wt in enumerate((a, ap)):
                            for k in range(KD):
                                last = pe.matmul(PS[:, 2 * (n % 2) + half, :], wt[:, k, j * P:(j + 1) * P],
                                                 HT[:, k, c * CH:(c + 1) * CH], start=k == 0, stop=k == KD - 1)
                        last.then_inc(S["proj"], 1)
                    for t in range(TT):
                        if t >= 2:
                            pe.wait_ge(S["v_out"], d["v_out"] + t - 1)
                        for k in range(KD):
                            last = pe.matmul(PS[:, 4 + t % 2, 0:D], HT[:, k, t * P:(t + 1) * P], w["v"][:, k, :],
                                             start=k == 0, stop=k == KD - 1)
                        last.then_inc(S["v_proj"], 1)
                    if extra is not None:
                        extra[1](pe)

                @block.vector
                def _(dve):
                    if first is not None:
                        first(dve)
                    for n, (_, _, dst, j, c) in enumerate(work):
                        dve.wait_ge(S["proj"], d["proj"] + n + 1)
                        if n >= 2:
                            name = "rest" if split is not None else "rope_sum"
                            dve.wait_ge(S[name], d[name] + n - 1)
                        ps = lambda half: PS[:, 2 * (n % 2) + half, :].rearrange("p (b t) -> p b t", t=T)
                        tm = lambda a: a[:, n % 2].rearrange("p (b t) -> p b t", t=T)
                        dve.tensor_tensor(tm(RC), ps(0), cos.to_broadcast([P, nchunk, T]), ALU.mult).then_inc(S["rope_cos"], 1)
                        dve.tensor_tensor(tm(RS), ps(1), sin.to_broadcast([P, nchunk, T]), ALU.mult).then_inc(S["rope_sin"], 1)
                        if split is None:
                            if beside is not None:
                                beside(dve, n, len(work))
                        else:
                            dve.wait_ge(S["rope_cos"], d["rope_cos"] + n + 1)
                            dve.wait_ge(S["rope_sin"], d["rope_sin"] + n + 1)
                            dve.tensor_tensor(ROT[:, n % 2], RC[:, n % 2], RS[:, n % 2], ALU.add).then_inc(S["rope_sum"], 1)
                    if split is not None:
                        values_out(dve)
                    if extra is not None:
                        extra[2](dve)

                if split is None:
                    @block.gpsimd
                    def _(pool):
                        for n, (_, _, dst, j, c) in enumerate(work):
                            pool.wait_ge(S["rope_cos"], d["rope_cos"] + n + 1)
                            pool.wait_ge(S["rope_sin"], d["rope_sin"] + n + 1)
                            pool.tensor_tensor(dst[:, j, c * CH:(c + 1) * CH], RC[:, n % 2], RS[:, n % 2], ALU.add
                                               ).then_inc(S["rope_sum"], 1)

                if split is not None:
                    @block.gpsimd
                    def _(pool):
                        for n in range(len(work) + 1):
                            if n < len(work):
                                pool.wait_ge(S["rope_sum"], d["rope_sum"] + n + 1)
                                pool.wait_ge(S["part_h"], d["part_h"] + n + 1)
                                pool.tensor_tensor(REST[:, n % NREST], ROT[:, n % 2], SPL[:, n, 0], ALU.subtract
                                                   ).then_inc(S["rest"], 1)
                            if n:
                                m = n - 1
                                pool.wait_ge(S["part_m"], d["part_m"] + m + 1)
                                pool.tensor_tensor(SPL[:, m, 2], REST[:, m % NREST], SPL[:, m, 1], ALU.subtract
                                                   ).then_inc(S["part_l"], 1)

                    @block.sync
                    def _(sp):
                        split[1](sp, d)

                @block.scalar
                def _(act):
                    if split is None:
                        values_out(act)
                        return
                    if extra is not None:
                        extra[0](act)
                    for n in range(len(work) + 2):
                        if n < len(work):
                            act.wait_ge(S["rope_sum"], d["rope_sum"] + n + 1)
                            act.activation(SPL[:, n, 0], ROT[:, n % 2], ACT.Copy).then_inc(S["part_h"], 1)
                        if 1 <= n <= len(work):
                            act.wait_ge(S["rest"], d["rest"] + n)
                            act.activation(SPL[:, n - 1, 1], REST[:, (n - 1) % NREST], ACT.Copy).then_inc(S["part_m"], 1)
                        if n >= 2:
                            split[0](act, SPL, d, n - 2)
        done["proj"] += len(work)
        done["rope_cos"] += len(work)
        done["rope_sin"] += len(work)
        done["v_proj"] += TT
        done["v_out"] += TT
        done["rope_sum"] += len(work)
        if split is not None:
            for name in ("part_h", "rest", "part_m", "part_l"):
                done[name] += len(work)

    def fetch_parts(sp, hd, dst, src, order, name):
        for base in range(2 if hd == 8 else 1):
            for j in range(NSTACK[hd]):
                at = 64 * base + hd * j
                sp.dma_start(dst(base)[at:at + hd], src(order[j], base)).then_inc(S[name], 16)

    def stacked_attention(layer, w, nq, hd, scale, arrived=None, extra=None):
        QT = HT
        with ExitStack() as s2:
            V = s2.enter_context(nc.sbuf_tensor(f"V{layer}", [P, TT, D], F32))
            r = 32 // hd
            nbase = 2 if hd == 8 else 1
            SQ = s2.enter_context(nc.sbuf_tensor(f"SQ{layer}", [P, D // hd // nbase, B * T], BF16))
            SK = s2.enter_context(nc.sbuf_tensor(f"SK{layer}", [P, nbase, 4, B * T], BF16))
            rows = nbase * NSTACK[hd] * hd
            at0 = dict(done)
            NR = nbase * NSTACK[hd] * 2 * 16

            def fetch(sp, c):
                cs = slice(c * CH, (c + 1) * CH)
                if hd == 8:
                    half = lambda a, which, u: a[which, u * P:(u + 1) * P, cs]
                    q_src = lambda which, u: half(q_parts, which, u).rearrange("(a d) t -> d a t", d=hd)
                    k_src = lambda which, u: half(k_parts, which, u).rearrange("(s r d) t -> d s r t", r=r, d=hd)[:, :, 0]
                else:
                    q_src = lambda which, base: q_parts[which, :, cs].rearrange("(a d) t -> d a t", d=hd)
                    k_src = lambda which, base: k_parts[which, :, cs].rearrange("(a b d) t -> d a b t", a=4, d=hd)[:, :, 0]
                fetch_parts(sp, hd, lambda u: SK[:, u, :, cs], k_src, PARTS_K, f"stacked{c}")
                fetch_parts(sp, hd, lambda u: SQ[:, :, cs], q_src, PARTS_Q, f"stacked{c}")

            NW = nq + 2

            def send(act, SPL, d, n):
                c, j = n // NW, n % NW
                dst, j2 = (q_parts, j) if j < nq else (k_parts, j - nq)
                act.wait_ge(S["part_l"], d["part_l"] + n + 1)
                act.dma_start(dst[:, j2 * P:(j2 + 1) * P, c * CH:(c + 1) * CH].rearrange("a p t -> p a t"), SPL[:, n]
                              ).then_inc(S[f"chunk_out{c}"], 16)

            def split(sp, d):
                sp.wait_ge(S["chunk_out0"], d["chunk_out0"] + 16 * NW)
                fetch(sp, 0)
                sp.wait_ge(S["chunk_out1"], d["chunk_out1"] + 16 * NW)

            def zeros(dve):
                dve.memset(SK[64:128, 0], 0.0)
                dve.memset(SK[0:64, 1], 0.0)

            project(w, nq, hd, None, None, V, arrived, (send, split), zeros if hd == 8 else None, extra=extra)
            for c in range(NCH):
                done[f"chunk_out{c}"] += 16 * NW

            def rest(sp):
                fetch(sp, 1)

            def arrivals(bb):
                c = bb * T // CH if isinstance(bb, int) else 1
                return [(f"stacked{c}", at0[f"stacked{c}"] + NR)]

            per = nq // 2

            def queries(b, u, s, quad, lo, n):
                blk = s * r + quad if hd == 8 else (4 * u + s) * r + quad
                return SQ[0:rows, blk, bass.ds(b * T + lo, n)]

            def keys(b, u, s, quad, lo, n):
                a = SK[0:rows, u, s] if hd == 8 else SK[0:rows, 0, 2 * u + s // 2]
                return a[:, bass.ds(b * T + lo, n)]

            attention(hd, nq, True, scale, q_of=None, k_of=None,
                      v_of=lambda b, u, n: V[:, 2 * b + n, (u // per) * P:(u // per + 1) * P],
                      out_of=lambda b, u: (QT[:, u, bass.ds(b * T, T)], None),
                      stack=(queries, keys, arrivals, rest))
            for c in range(NCH):
                done[f"stacked{c}"] += NR
        return ExitStack(), add_product(X), (lambda k, t: QT[:, k, t * P:(t + 1) * P], lambda k: w["o"][:, k, :], nq)

    def self_attention(layer, w, nq, hd, scale, softcap=None, arrived=None,
                       beside=(None, None)):
        st = ExitStack()
        QT = st.enter_context(nc.sbuf_tensor(f"QT{layer}", [P, nq, B * T], F32))
        KT = st.enter_context(nc.sbuf_tensor(f"KT{layer}", [P, 2, B * T], F32))
        V = st.enter_context(nc.sbuf_tensor(f"V{layer}", [P, TT, D], F32))
        project(w, nq, hd, QT, KT, V, arrived, first=masks if layer == 0 else None, beside=beside[0])
        per = nq // 2
        attention(hd, nq, True, scale,
                  q_of=lambda b, u: QT[:, u, bass.ds(b * T, T)],
                  k_of=lambda b, u: KT[:, u // per, bass.ds(b * T, T)],
                  v_of=lambda b, u, n: V[:, 2 * b + n, (u // per) * P:(u // per + 1) * P],
                  out_of=lambda b, u: (QT[:, u, bass.ds(b * T, T)], None), softcap=softcap, beside=beside[1])
        return st, add_product(X), (lambda k, t: QT[:, k, t * P:(t + 1) * P], lambda k: w["o"][:, k, :], nq)

    def stacked_cross(hd, SQ, SK, after):
        r = 32 // hd
        rows = NSTACK[hd] * hd
        at = lambda a: a[0:rows].rearrange("p n c -> p (n c)")
        head = lambda b, u, s, q, lo, n: bass.ds(((2 * b + u) * 8 + s * r + q) * D + lo, n)
        attention(hd, 2, False, float(hd) ** -0.5, q_of=None, k_of=None,
                  v_of=lambda b, u, n: CXT[:, n, bass.ds((2 * b + u) * P, P)],
                  out_of=lambda b, u: (X[:, 2 * b + u, :], True),
                  stack=(lambda *a: at(SQ)[:, head(*a)], lambda *a: at(SK)[:, head(*a)], *after))

    def cross_attention(hd, gamma=None):
        attention(hd, 2, False, float(hd) ** -0.5,
                  q_of=lambda b, u: H[:, 2 * b + u, :],
                  k_of=lambda b, u: CX[:, 2 * b + u, :],
                  v_of=lambda b, u, n: CXT[:, n, bass.ds((2 * b + u) * P, P)],
                  out_of=lambda b, u: (X[:, 2 * b + u, :], True), gamma=gamma)

    def quantise_fp4():
        raw = WA[:, A_AT["upT0"][0]:A_AT["upT0"][0] + 4096]
        NP = 4096 // CH
        early = NP - B
        AB, HI, LO, small = (H[:, 2 * j:2 * j + 2, :].rearrange("p t d -> p (t d)") for j in range(4))
        NG = CH // 32
        am, pw, iv = (small[:, j * NG:(j + 1) * NG] for j in range(3))
        grp = lambda a: a.rearrange("p (g w) -> p g w", w=32)
        wide = lambda a: a.rearrange("p (g w) -> p g w", w=1).to_broadcast([P, NG, 32])
        u32 = lambda a: a.bitcast(U32)

        def piece(n):
            return raw[:, bass.ds(n * CH, CH)]

        def steps(dve, n):
            src = piece(n)
            return [
                lambda: dve.tensor_scalar(u32(AB), u32(src), 0x7FFFFFFF, None, ALU.bitwise_and),
                lambda: dve.tensor_reduce(am, grp(AB), AX, ALU.max),
                lambda: dve.tensor_scalar(am, am, 1e-30, None, ALU.max),
                lambda: dve.tensor_scalar(u32(pw), u32(am), 0x7F800000, None, ALU.bitwise_and),
                lambda: dve.tensor_scalar(pw, pw, 0.25, None, ALU.mult),
                lambda: dve.reciprocal(iv, pw),
                lambda: dve.tensor_tensor(grp(AB), grp(AB), wide(iv), ALU.mult),
                lambda: dve.tensor_scalar(HI, AB, 5.0, 2.0, ALU.is_ge, ALU.mult),
                *[lambda mid=mid: dve.scalar_tensor_tensor(HI, AB, mid, HI, ALU.is_ge, ALU.add) for mid in (3.5, 2.5)],
                lambda: dve.tensor_scalar(LO, AB, 1.75, None, ALU.is_ge),
                *[lambda mid=mid: dve.scalar_tensor_tensor(LO, AB, mid, LO, ALU.is_ge, ALU.add)
                  for mid in (1.25, 0.75, 0.25)],
                lambda: dve.scalar_tensor_tensor(HI, LO, 0.5, HI, ALU.mult, ALU.add),
                lambda: dve.scalar_tensor_tensor(u32(HI), u32(src), 0x80000000, u32(HI), ALU.bitwise_and, ALU.bitwise_or),
                lambda: dve.tensor_tensor(grp(src), grp(HI), wide(pw), ALU.mult),
            ]

        NS = len(steps(None, 0))
        at0 = done["quantised"]

        def do(dve, n, lo, hi):
            todo = steps(dve, n)
            for k in range(lo, hi):
                if not (isinstance(n, int) and n == 0 and k == 0):
                    dve.wait_ge(S["quantised"], n * NS + (k + at0))
                todo[k]().then_inc(S["quantised"], 1)

        def beside_projection(dve, i, n):
            if i < 2:
                return
            if i == 2:
                dve.wait_ge(S["kernels_in"], 16)
            lo, hi = (early * NS * (j - 2) // (n - 2) for j in (i, i + 1))
            for m in range(early):
                a, b = max(lo, m * NS), min(hi, (m + 1) * NS)
                if a < b:
                    do(dve, m, a - m * NS, b - m * NS)

        def beside_attention(dve, bb, i, n):
            do(dve, bb + early, NS * i // n, NS * (i + 1) // n)

        done["quantised"] += NP * NS
        return beside_projection, beside_attention

    def turn_context_and_weights():
        CTX = TT // 2
        d = dict(done)
        with nc.Block() as block:
            @block.gpsimd
            def _(pool):
                pool.wait_ge(S["b_in"], 64)

            @block.tensor
            def _(pe):
                pe.wait_ge(S["ctx_in"], 16)
                for g in range(CTX):
                    for k in range(KD):
                        for j in range(2):
                            last = pe.transpose(PS[:, g, k * 256 + j * P:k * 256 + (j + 1) * P],
                                                CX[:, 2 * g + j, k * P:(k + 1) * P], ident)
                    last.then_inc(S["turned"], 1)
                upT, dnT = wA("upT0", 8), wA("dnT0", KD)
                for g in range(8):
                    if g >= 4:
                        pe.wait_ge(S["ctx_copied"], g - 3)
                    for j in range(4):
                        if g < 4:
                            src = upT[:, 4 * (g % 2) + j, (g // 2) * P:(g // 2 + 1) * P]
                        else:
                            f = 2 * (g - 4) + j // 2
                            src = dnT[:, j % 2, f * P:(f + 1) * P]
                        last = pe.transpose(PS[:, (4 + g) % 8, j * P:(j + 1) * P], src, ident)
                    last.then_inc(S["turned"], 1)

            def kernel_out(g):
                if g < 4:
                    k, f = g // 2, 4 * (g % 2)
                    return wA("up0", KD)[:, k, f * P:(f + 4) * P]
                f = 2 * (g - 4)
                return wA("dn0")[:, f * D:(f + 2) * D]

            @block.scalar
            def _(act):
                for g in range(CTX):
                    act.wait_ge(S["turned"], d["turned"] + g + 1)
                    act.activation(CXT[:, :, g * 256:(g + 1) * 256],
                                   PS[:, g, :].rearrange("p (k n) -> p k n", k=KD), ACT.Copy).then_inc(S["ctx_copied"], 1)
                for g in range(4, 8):
                    act.wait_ge(S["turned"], d["turned"] + CTX + g + 1)
                    act.activation(kernel_out(g), PS[:, (4 + g) % 8, :], ACT.Copy)

            @block.vector
            def _(dve):
                for g in range(4):
                    dve.wait_ge(S["turned"], d["turned"] + CTX + g + 1)
                    dve.tensor_copy(kernel_out(g), PS[:, 4 + g, :])
        done["turned"] += CTX + 8

    def mlp(n, up, gate, down, mode, bias=None, scales=None, load=None, gates=None, beside=None):
        two = mode == "silu"
        d = dict(done)
        tag = str(nc.next_id())
        with ExitStack() as st:
            def tmp(name, shape, dt=F32):
                return st.enter_context(nc.sbuf_tensor(name + tag, shape, dt))
            AO = tmp("AO", [P, NCH, CH])
            MO = tmp("MO", [P, NCH, CH])
            HO = tmp("HO", [P, NCH, CH])
            with nc.Block() as block:
                if load is not None:
                    @block.sync
                    def _(sp):
                        load(sp, d)

                @block.tensor
                def _(pe):
                    def go_up(i, c):
                        if gates is not None and c == 0:
                            pe.wait_ge(S[f"w_slot{i % RING2}"], 16 * (i // RING2 + 1))
                        if i >= 1:
                            name = "mult_out" if two else "act_out"
                            pe.wait_ge(S[name], d[name] + NCH * (i - 1) + c + 1)
                        for half, w in enumerate((up, gate) if two else (up,)):
                            for k in range(KD):
                                last = pe.matmul(PS[:, 2 * c + half, :], w(i, k), HT[:, k, c * CH:(c + 1) * CH],
                                                 start=k == 0, stop=k == KD - 1)
                        last.then_inc(S["up_ps"], 1)

                    def go_down(i, c):
                        src, name = (HO, "pool_mark") if gates is not None else (MO, "mult_out") if two else (AO, "act_out")
                        pe.wait_ge(S[name], d[name] + NCH * i + c + 1)
                        for j in range(TPC):
                            t = c * TPC + j
                            last = pe.matmul(PS[:, 4 + t // 2, (t % 2) * D:(t % 2 + 1) * D], src[:, c, j * P:(j + 1) * P],
                                             down(i), start=i == 0 and t % 2 == 0, stop=i == n - 1,
                                             skip_group_check=True)
                        last.then_inc(S["down_ps"], 1)

                    for c in range(NCH):
                        go_up(0, c)
                    for i in range(n):
                        for c in range(NCH):
                            if i + 1 < n:
                                go_up(i + 1, c)
                            go_down(i, c)

                @block.scalar
                def _(act):
                    for i in range(n):
                        for c in range(NCH):
                            act.wait_ge(S["up_ps"], d["up_ps"] + NCH * i + c + 1)
                            if i >= 1:
                                name = "mult_out" if two else "down_ps"
                                act.wait_ge(S[name], d[name] + NCH * (i - 1) + c + 1)
                            if two:
                                ins = act.activation(AO[:, c], PS[:, 2 * c, :], ACT.Silu,
                                                     scale=1.0 if scales is None else scales[:, 0:1])
                            else:
                                ins = act.activation(AO[:, c], PS[:, 2 * c, :], ACT.Gelu_apprx_tanh, bias=bias[:, i:i + 1])
                            ins.then_inc(S["act_out"], 1)

                if two:
                    @block.vector
                    def _(dve):
                        for i in range(n):
                            for c in range(NCH):
                                dve.wait_ge(S["act_out"], d["act_out"] + NCH * i + c + 1)
                                if i >= 1:
                                    name = "pool_mark" if gates is not None else "down_ps"
                                    dve.wait_ge(S[name], d[name] + NCH * (i - 1) + c + 1)
                                if scales is None:
                                    ins = dve.tensor_tensor(MO[:, c], PS[:, 2 * c + 1, :], AO[:, c], ALU.mult)
                                else:
                                    ins = dve.scalar_tensor_tensor(MO[:, c], PS[:, 2 * c + 1, :], scales[:, 1:2],
                                                                   AO[:, c], ALU.mult, ALU.mult)
                                ins.then_inc(S["mult_out"], 1)
                                if beside is not None:
                                    beside(dve, NCH * i + c)

                if beside is not None and not two:
                    @block.vector
                    def _(dve):
                        beside(dve)

                if bias is not None:
                    @block.gpsimd
                    def _(pool):
                        row = rv("b_dn0").rearrange("p (a n) -> p a n", a=1).to_broadcast([P, TT, D])
                        pool.tensor_tensor(X[:], X[:], row, ALU.add).then_inc(S["pool_mark"], 1)

                if gates is not None:
                    @block.gpsimd
                    def _(pool):
                        for i in range(n):
                            for c in range(NCH):
                                pool.wait_ge(S["mult_out"], d["mult_out"] + NCH * i + c + 1)
                                if c == 0:
                                    pool.wait_ge(S[f"g_slot{i % RINGG}"], 32 * (i // RINGG + 1))
                                if i >= 1:
                                    pool.wait_ge(S["down_ps"], d["down_ps"] + NCH * (i - 1) + c + 1)
                                pool.tensor_tensor(HO[:, c], MO[:, c], gates(i)[:, c * CH:(c + 1) * CH],
                                                   ALU.mult).then_inc(S["pool_mark"], 1)
            for name, k in (("up_ps", NCH * n), ("down_ps", NCH * n), ("act_out", NCH * n),
                            ("mult_out", NCH * n if two else 0),
                            ("pool_mark", NCH * n if gates is not None else 1 if bias is not None else 0)):
                done[name] += k

    def mixing():
        tag = str(nc.next_id())
        st = ExitStack()

        def tmp(name, shape, dt=F32):
            return st.enter_context(nc.sbuf_tensor(name + tag, shape, dt))

        N = tmp("N", [P, TT, D])
        AP_ = tmp("AP", [P, KD, B, T + 1])
        DF = tmp("DF", [P, KD, B, T])
        XM = tmp("XM", [P, 3, KD, B, T])
        RR = tmp("RR", [P, KD, B * T])
        EK = tmp("EK", [P, KD, B * T])
        us = tmp("us", [P, KD])
        cur = AP_[:, :, :, 1:T + 1]
        prev = AP_[:, :, :, 0:T]
        flat = lambda a: a.rearrange("p b t -> p (b t)")
        halves = [(j, c) for c in range(NCH) for j in range(KD)]
        NHV = len(halves)
        piece = lambda a, j, c: a[:, j, c * CH:(c + 1) * CH]

        def to_padded(k, g):
            return AP_[:, k, g, 1:T + 1]

        def mix(dve, d, n, mu):
            for k in range(KD):
                dve.scalar_tensor_tensor(XM[:, n, k], DF[:, k], vv(mu)[:, k:k + 1], prev[:, k], ALU.mult,
                                         ALU.add).then_inc(S["dve_mark"], 1)

        def products(pe, d, n, w, bank, wait=None):
            pe.wait_ge(S["dve_mark"], d["dve_mark"] + KD * (n + 1))
            for m, (j, c) in enumerate(halves):
                if wait is not None:
                    pe.wait_ge(S[wait], d[wait] + m + 1)
                for k in range(KD):
                    last = pe.matmul(PS[:, bank + m, :], w[:, k, j * P:(j + 1) * P],
                                     flat(XM[:, n, k])[:, c * CH:(c + 1) * CH], start=k == 0, stop=k == KD - 1)
                last.then_inc(S["up_ps"], 1)

        with nc.Block() as block:
            @block.vector
            def _(dve):
                dve.memset(AP_[:, :, :, 0:1], 0.0)
                dve.tensor_scalar(us[:], vv("u"), -float(np.log(1e-8)), None, ALU.add)
        layernorm(H, N, to_padded, vv("ln1_g"), vv("ln1_b"))
        d = dict(done)
        with nc.Block() as block:
            @block.vector
            def _(dve):
                link(dve, dve.tensor_tensor(DF[:], cur, prev, ALU.subtract), "dve_chain")
                for n, mu in enumerate(("mu_r", "mu_k", "mu_v")):
                    mix(dve, d, n, mu)
                for m, (j, c) in enumerate(halves):
                    dve.wait_ge(S["act_out"], d["act_out"] + NHV + m + 1)
                    link(dve, dve.tensor_tensor(piece(RR, j, c), piece(RR, j, c), piece(EK, j, c), ALU.mult), "dve_chain")
                for m, (j, c) in enumerate(halves):
                    dve.wait_ge(S["up_ps"], d["up_ps"] + 2 * NHV + m + 1)
                    dve.tensor_tensor(piece(RR, j, c), piece(RR, j, c), PS[:, m, :], ALU.mult)

            @block.tensor
            def _(pe):
                products(pe, d, 0, wA("wr", KD), 0)
                products(pe, d, 1, wA("wk", KD), 4)
                products(pe, d, 2, wA("wv", KD), 0, "act_out")

            @block.scalar
            def _(act):
                for n in range(2):
                    for m, (j, c) in enumerate(halves):
                        act.wait_ge(S["up_ps"], d["up_ps"] + n * NHV + m + 1)
                        act.activation(piece((RR, EK)[n], j, c), PS[:, 4 * n + m, :], ACT.Sigmoid,
                                       **({"bias": us[:, j:j + 1]} if n else {})).then_inc(S["act_out"], 1)
        done["dve_mark"] += 3 * KD
        done["up_ps"] += 3 * NHV
        done["act_out"] += 2 * NHV
        layernorm(H, N, to_padded, vv("ln2_g"), vv("ln2_b"), pre=add_product(H),
                  rows=(lambda k, t: RR[:, k, t * P:(t + 1) * P], lambda k: wA("wout", KD)[:, k, :], KD))
        d = dict(done)
        with nc.Block() as block:
            @block.vector
            def _(dve):
                link(dve, dve.tensor_tensor(DF[:], cur, prev, ALU.subtract), "dve_chain")
                for n, mu in enumerate(("cmu_k", "cmu_r")):
                    mix(dve, d, n, mu)
                for m, (j, c) in enumerate(halves):
                    dve.wait_ge(S["act_out"], d["act_out"] + m + 1)
                    dve.tensor_tensor(piece(EK, j, c), piece(EK, j, c), PS[:, m, :], ALU.mult)

            @block.tensor
            def _(pe):
                products(pe, d, 0, wA("ck", KD), 0)
                pe.wait_ge(S["dve_mark"], d["dve_mark"] + 2 * KD)
                for t in range(TT):
                    for k in range(KD):
                        last = pe.matmul(PS[:, 4 + t // 2, (t % 2) * D:(t % 2 + 1) * D], flat(XM[:, 1, k])[:, t * P:(t + 1) * P],
                                         wA("cr", KD)[:, k, :], start=k == 0, stop=k == KD - 1)
                    if t % 2:
                        last.then_inc(S["up_ps"], 1)

            @block.scalar
            def _(act):
                for m, (j, c) in enumerate(halves):
                    act.wait_ge(S["up_ps"], d["up_ps"] + m + 1)
                    act.activation(piece(EK, j, c), PS[:, m, :], ACT.Relu).then_inc(S["act_out"], 1)
                for g in range(TT // 2):
                    act.wait_ge(S["up_ps"], d["up_ps"] + NHV + g + 1)
                    act.activation(N[:, 2 * g:2 * g + 2, :], PS[:, 4 + g, :].rearrange("p (t n) -> p t n", t=2), ACT.Sigmoid)
        done["dve_mark"] += 2 * KD
        done["up_ps"] += NHV + TT // 2
        done["act_out"] += NHV

        def pre(dve, g):
            L = lambda ins: link(dve, ins, "dve_chain")
            v = slice(2 * g, 2 * g + 2)
            L(dve.tensor_tensor(N[:, v, :], N[:, v, :], PS[:, v, 0:D], ALU.mult))
            L(dve.tensor_tensor(H[:, v, :], H[:, v, :], N[:, v, :], ALU.add))
            L(dve.tensor_tensor(X[:, v, :], X[:, v, :], H[:, v, :], ALU.add))

        return st, pre, (lambda k, t: EK[:, k, t * P:(t + 1) * P], lambda k: wA("cv", KD)[:, k, :], KD)

    def route(E, extra, weights, logits_of, gates_of, G, GT, beside=None):
        EW = E + extra
        tag = str(nc.next_id())
        d = dict(done)
        with ExitStack() as st:
            def tmp(name, shape, dt=F32):
                return st.enter_context(nc.sbuf_tensor(name + tag, shape, dt))
            LG, PRB, RK = (tmp(x, [P, TT, E]) for x in ("LG", "PRB", "RK"))
            C1, C2 = (tmp(x, [P, TT, E, E]) for x in ("CA", "CB"))
            r1, r2 = (tmp(x, [P, TT]) for x in ("ra", "rb"))
            wide = lambda a: a[:].rearrange("p (t e) -> p t e", e=1).to_broadcast([P, TT, E])
            with nc.Block() as block:
                @block.tensor
                def _(pe):
                    for t in range(TT):
                        for k in range(KD):
                            last = pe.matmul(PS[:, 0, t * EW:(t + 1) * EW], HT[:, k, t * P:(t + 1) * P], weights[:, k, :],
                                             start=k == 0, stop=k == KD - 1)
                    last.then_inc(S["pe_mark"], 1)
                    if beside is not None:
                        beside[1](pe)
                    pe.wait_ge(S["gates"], d["gates"] + 1)
                    for t in range(TT):
                        last = pe.transpose(PS[0:EW, 1 + t // 4, (t % 4) * P:(t % 4 + 1) * P], G[:, t, :], ident)
                    last.then_inc(S["turned"], 1)

                if beside is not None:
                    @block.gpsimd
                    def _(pool):
                        beside[0](pool)

                @block.scalar
                def _(act):
                    act.wait_ge(S["dve_mark"], d["dve_mark"] + 1)
                    act.activation(PRB[:], PRB[:], ACT.Exp).then_inc(S["act_mark"], 1)
                    if beside is not None:
                        beside[2](act)
                    if extra:
                        ps = PS[:, 0, 0:TT * EW].rearrange("p (t e) -> p t e", e=EW)
                        act.activation(G[:, :, E:EW], ps[:, :, E:EW], ACT.Sigmoid).then_inc(S["act_mark"], 1)
                    else:
                        act.wait_ge(S["dve_mark"], d["dve_mark"] + 2)
                        act.activation(LG[:], LG[:], ACT.Exp).then_inc(S["act_mark"], 1)

                @block.vector
                def _(dve):
                    L = lambda ins: link(dve, ins, "dve_chain")
                    dve.wait_ge(S["pe_mark"], d["pe_mark"] + 1)
                    ps = PS[:, 0, 0:TT * EW].rearrange("p (t e) -> p t e", e=EW)
                    logits_of(dve, L, LG, ps[:, :, 0:E])
                    L(dve.tensor_reduce(r1[:], LG[:], AX, ALU.max))
                    dve.tensor_tensor(PRB[:], LG[:], wide(r1), ALU.subtract).then_inc(S["dve_mark"], 1)
                    dve.wait_ge(S["act_mark"], d["act_mark"] + 1)
                    L(dve.tensor_reduce(r1[:], PRB[:], AX, ALU.add))
                    L(dve.reciprocal(r1[:], r1[:]))
                    L(dve.tensor_tensor(PRB[:], PRB[:], wide(r1), ALU.mult))
                    mine = PRB[:].rearrange("p t (e a) -> p t e a", a=1).to_broadcast([P, TT, E, E])
                    theirs = PRB[:].rearrange("p t (a e) -> p t a e", a=1).to_broadcast([P, TT, E, E])
                    low = cst(f"lower{E}").rearrange("p (a e f) -> p a (e f)", a=1, e=E).to_broadcast([P, TT, E * E])
                    L(dve.tensor_tensor(C1[:], theirs, mine, ALU.is_gt))
                    L(dve.tensor_tensor(C2[:], theirs, mine, ALU.is_equal))
                    c2 = C2[:].rearrange("p t e f -> p t (e f)")
                    L(dve.tensor_tensor(c2, c2, low, ALU.mult))
                    L(dve.tensor_tensor(C1[:], C1[:], C2[:], ALU.add))
                    L(dve.tensor_reduce(RK[:], C1[:], AX, ALU.add))
                    gates_of(dve, L, PRB, RK, LG, r1, r2, wide, d)
                    dve.wait_ge(S["turned"], d["turned"] + 1)
                    L(dve.tensor_copy(GT[0:EW, :].rearrange("p (a n) -> p a n", a=2), PS[0:EW, 1:3, :]))
            done["pe_mark"] += 1
            done["gates"] += 1
            done["turned"] += 1
            done["act_mark"] += 2
            done["dve_mark"] += 1 if extra else 2

    def experts1():
        NF = sum(FB1)
        tag = str(nc.next_id())
        owner = [e for e in range(E1) for _ in range(FB1[e])]
        with ExitStack() as st:
            def tmp(name, shape, dt=F32):
                return st.enter_context(nc.sbuf_tensor(name + tag, shape, dt))
            G = tmp("G", [P, TT, E1])
            GT = tmp("GT", [P, B * T])
            GH = tmp("GH", [P, B * T])
            GX = H[:].rearrange("p t d -> p (t d)").rearrange("p (k n) -> p k n", k=KD)
            GB = tmp("GB", [P, E1, B * T])
            gb1 = tmp("gb1", [P, NF])
            cc = tmp("cc", [P, 4])
            HA = tmp("HA", [P, 4, CH])
            HB = tmp("HB", [P, 4, CH])
            MT = tmp("MT", [P, B * T])

            def logits_of(dve, L, LG, ps):
                row = rv("b_router").rearrange("p (a e) -> p a e", a=1).to_broadcast([P, TT, E1])
                cost = cst("cost").rearrange("p (a e) -> p a e", a=1).to_broadcast([P, TT, E1])
                L(dve.tensor_tensor(LG[:], ps, row, ALU.add))
                L(dve.tensor_tensor(LG[:], LG[:], cost, ALU.subtract))

            def gates_of(dve, L, PRB, RK, LG, r1, r2, wide, d):
                L(dve.tensor_reduce(r2[:], PRB[:], AX, ALU.max))
                dve.tensor_tensor(LG[:], PRB[:], wide(r2), ALU.subtract).then_inc(S["dve_mark"], 1)
                dve.wait_ge(S["act_mark"], d["act_mark"] + 2)
                L(dve.scalar_tensor_tensor(LG[:], RK[:], 2.0, LG[:], ALU.is_lt, ALU.mult))
                L(dve.tensor_reduce(r2[:], LG[:], AX, ALU.add))
                L(dve.reciprocal(r2[:], r2[:]))
                dve.tensor_tensor(G[:], LG[:], wide(r2), ALU.mult).then_inc(S["gates"], 1)

            def biases(pool):
                for i, name in enumerate(("b_up1", "b_core")):
                    row = rv(name).rearrange("p (a n) -> p a n", a=1).to_broadcast([P, TT, D])
                    if i:
                        pool.wait_ge(S["first_bias"], 1)
                    pool.tensor_tensor(X[:], X[:], row, ALU.add).then_inc(S["first_bias"], 1)

            def narrow(pe):
                for c in range(NCH):
                    for k in range(KD):
                        last = pe.matmul(PS[:, 3 + 4 * c, :], wB("down", KD)[:, k, :], HT[:, k, c * CH:(c + 1) * CH],
                                         start=k == 0, stop=k == KD - 1)
                    last.then_inc(S["narrow"], 1)
                pe.wait_ge(S["bias_gelu"], 1)
                for f in range(NF):
                    pe.matmul(PS[:, 6, 0:1], wB("w2")[:, f * P:(f + 1) * P], gb1[:, f:f + 1],
                              start=f == 0, stop=f == NF - 1)

            def gelus(act):
                act.activation(gb1[:], vv("b1"), ACT.Gelu).then_inc(S["bias_gelu"], 1)
                for c in range(NCH):
                    act.wait_ge(S["narrow"], c + 1)
                    act.activation(GH[:, c * CH:(c + 1) * CH], PS[:, 3 + 4 * c, :], ACT.Gelu, bias=vv("b_down1"))
                act.activation(GX, HT[:], ACT.Gelu)

            route(E1, 0, wB("router", KD), logits_of, gates_of, G, GT, beside=(biases, narrow, gelus))
            d = dict(done)
            n_all = NF + 1
            work = [(f, c) for f in range(n_all) for c in range(NCH)]
            with nc.Block() as block:
                @block.sync
                def _(sp):
                    sp.dma_start(gate_rows[0:E1, :], GT[0:E1, :]).then_inc(S["gates_sent"], 16)
                    sp.wait_ge(S["gates_sent"], d["gates_sent"] + 16)
                    for e in range(E1):
                        sp.dma_start(GB[:, e, :], gate_rows[e:e + 1, :].to_broadcast([P, B * T])
                                     ).then_inc(S[f"gates_back{e}"], 16)

                @block.tensor
                def _(pe):
                    def go_up(n):
                        f, c = work[n]
                        if n >= 2:
                            pe.wait_ge(S["act_out"], d["act_out"] + n - 1)
                        w = wB("w1")[:, f * P:(f + 1) * P] if f < NF else wB("sh1")
                        pe.matmul(PS[:, n % 2, :], w, GH[:, c * CH:(c + 1) * CH], start=True, stop=True).then_inc(S["up_ps"], 1)

                    def go_down(n):
                        f, c = work[n]
                        pe.wait_ge(S["mult_out"], d["mult_out"] + n + 1)
                        w = wB("w2")[:, f * P:(f + 1) * P] if f < NF else wB("sh2")
                        pe.matmul(PS[:, 4 + c, :], w, HB[:, n % 4, :], start=f == 0, stop=f == n_all - 1
                                  ).then_inc(S["down_ps"], 1)

                    go_up(0)
                    go_up(1)
                    for t in range(TT):
                        if t >= 2:
                            pe.wait_ge(S["x_added"], d["x_added"] + t - 1)
                        for k in range(KD):
                            last = pe.matmul(PS[:, 2 + t % 2, 0:D], GX[:, k, t * P:(t + 1) * P], wB("core", KD)[:, k, :],
                                             start=k == 0, stop=k == KD - 1)
                        last.then_inc(S["o_proj"], 1)
                    for n in range(len(work)):
                        if n + 2 < len(work):
                            go_up(n + 2)
                        go_down(n)
                    pe.wait_ge(S["dve_mark"], d["dve_mark"] + 1)
                    for t in range(TT):
                        if t >= 4:
                            pe.wait_ge(S["x_added"], d["x_added"] + TT + t - 3)
                        pe.matmul(PS[:, t % 4, 0:D], MT[:, t * P:(t + 1) * P], wB("up"), start=True, stop=True
                                  ).then_inc(S["o_proj"], 1)

                @block.scalar
                def _(act):
                    for n, (f, c) in enumerate(work):
                        act.wait_ge(S["up_ps"], d["up_ps"] + n + 1)
                        if n >= 4:
                            act.wait_ge(S["mult_out"], d["mult_out"] + n - 3)
                        b = vv("b1")[:, f:f + 1] if f < NF else vv("b_sh1")
                        act.activation(HA[:, n % 4, :], PS[:, n % 2, :], ACT.Gelu, bias=b).then_inc(S["act_out"], 1)

                @block.vector
                def _(dve):
                    L = lambda ins: link(dve, ins, "dve_chain")
                    for t in range(TT):
                        dve.wait_ge(S["o_proj"], d["o_proj"] + t + 1)
                        dve.tensor_tensor(X[:, t, :], X[:, t, :], PS[:, 2 + t % 2, 0:D], ALU.add).then_inc(S["x_added"], 1)
                    for n, (f, c) in enumerate(work):
                        if c == 0 and f < NF and (f == 0 or owner[f] != owner[f - 1]):
                            dve.wait_ge(S[f"gates_back{owner[f]}"], 16)
                        dve.wait_ge(S["act_out"], d["act_out"] + n + 1)
                        if n >= 4:
                            dve.wait_ge(S["down_ps"], d["down_ps"] + n - 3)
                        if f < NF:
                            ins = dve.scalar_tensor_tensor(HB[:, n % 4, :], HA[:, n % 4, :], gb1[:, f:f + 1],
                                                           GB[:, owner[f], c * CH:(c + 1) * CH], ALU.subtract, ALU.mult)
                        else:
                            ins = dve.tensor_scalar(HB[:, n % 4, :], HA[:, n % 4, :], 0.1, None, ALU.mult)
                        ins.then_inc(S["mult_out"], 1)
                    L(dve.tensor_reduce(cc[:, 0:1], vv("b2"), AX, ALU.add))
                    L(dve.scalar_tensor_tensor(cc[:, 1:2], vv("b_sh2"), 0.1, cc[:, 0:1], ALU.mult, ALU.add))
                    L(dve.tensor_tensor(cc[:, 2:3], PS[:, 6, 0:1], cc[:, 1:2], ALU.add))
                    dve.wait_ge(S["down_ps"], d["down_ps"] + len(work))
                    dve.tensor_scalar(MT[:].rearrange("p (a n) -> p a n", a=2), PS[:, 4:6, :], cc[:, 2:3], None,
                                      ALU.add).then_inc(S["dve_mark"], 1)
                    for t in range(TT):
                        dve.wait_ge(S["o_proj"], d["o_proj"] + TT + t + 1)
                        dve.tensor_tensor(X[:, t, :], X[:, t, :], PS[:, t % 4, 0:D], ALU.add).then_inc(S["x_added"], 1)
            for name, k in (("gates_sent", 16), ("up_ps", len(work)),
                            ("act_out", len(work)), ("mult_out", len(work)), ("down_ps", len(work)), ("dve_mark", 1), ("o_proj", 2 * TT), ("x_added", 2 * TT)):
                done[name] += k

    def experts2(replace):
        tag = str(nc.next_id())
        with ExitStack() as st:
            def tmp(name, shape, dt=F32):
                return st.enter_context(nc.sbuf_tensor(name + tag, shape, dt))
            G = tmp("G", [P, TT, E2 + 1])
            GT = tmp("GT", [P, B * T])
            W2 = tmp("W2", [P, RING2, 3 * D])
            GR = tmp("GR", [P, RINGG, B * T])
            scratch = tmp("scratch", [P, CH])

            def logits_of(dve, L, LG, ps):
                L(dve.tensor_copy(LG[:], ps))

            def gates_of(dve, L, PRB, RK, LG, r1, r2, wide, d):
                L(dve.scalar_tensor_tensor(LG[:], RK[:], 4.0, PRB[:], ALU.is_lt, ALU.mult))
                L(dve.tensor_reduce(r2[:], LG[:], AX, ALU.add))
                L(dve.tensor_scalar(r2[:], r2[:], 1e-9, None, ALU.max))
                L(dve.reciprocal(r2[:], r2[:]))
                dve.wait_ge(S["act_mark"], d["act_mark"] + 2)
                dve.tensor_tensor(G[:, :, 0:E2], LG[:], wide(r2), ALU.mult).then_inc(S["gates"], 1)

            route(E2, 1, wL("router2", KD), logits_of, gates_of, G, GT)

            def load(sp, d):
                sp.dma_start(gate_rows[:, :], GT[0:E2 + 1, :]).then_inc(S["gates_sent"], 16)

                def weights(i):
                    if i >= RING2:
                        sp.wait_ge(S["down_ps"], d["down_ps"] + NCH * (i - RING2 + 1))
                    sp.dma_start(W2[:, i % RING2, :], w2f[i]).then_inc(S[f"w_slot{i % RING2}"], 16)

                def gates(i):
                    if i >= RINGG:
                        sp.wait_ge(S["pool_mark"], d["pool_mark"] + NCH * (i - RINGG + 1))
                    owner = [min((i * P + r) // I2, E2) for r in range(P)]
                    cut = next((r for r in range(P) if owner[r] != owner[0]), P // 2)
                    for lo, hi in ((0, cut), (cut, P)):
                        e = owner[lo]
                        sp.dma_start(GR[lo:hi, i % RINGG, :], gate_rows[e:e + 1, :].to_broadcast([hi - lo, B * T])
                                     ).then_inc(S[f"g_slot{i % RINGG}"], 16)

                for i in range(NI2):
                    weights(i)
                    if i == 0:
                        sp.wait_ge(S["gates_sent"], d["gates_sent"] + 16)
                    gates(i)

            chunk = lambda i, j: W2[:, i % RING2, j * D:(j + 1) * D]
            mlp(NI2, up=lambda i, k: chunk(i, 0)[:, k * P:(k + 1) * P], gate=lambda i, k: chunk(i, 1)[:, k * P:(k + 1) * P],
                down=lambda i: chunk(i, 2), mode="silu", load=load, gates=lambda i: GR[:, i % RINGG, :],
                beside=lambda dve, n: replace(dve, scratch[:], n))
            done["gates_sent"] += 16

    def wkv_scan():
        NS = KD * B
        d = dict(done)
        tag = str(nc.next_id())
        with ExitStack() as st:
            def tmp(name, shape, dt=F32):
                return st.enter_context(nc.sbuf_tensor(name + tag, shape, dt))
            O, PN, QN = (tmp(x, [P, NS, T + 1]) for x in ("O", "PN", "QN"))
            KEEP, EK, EV = (tmp(x, [P, NS, T]) for x in ("KEEP", "EK", "EV"))
            TOP, OLD, NEW, NV = (tmp(x, [P, NS, T]) for x in ("TOP", "OLD", "NEW", "NV"))
            K = HT[:].rearrange("p k (b t) -> p (k b) t", t=T)
            V = CXT[:].rearrange("p k (b t) -> p (k b) t", t=T)
            w, u = vv("w3"), vv("u3")
            half = lambda a, k: a[:, k * B:(k + 1) * B]
            old, new = (lambda a: a[:, :, 0:T]), (lambda a: a[:, :, 1:T + 1])
            with nc.Block() as block:
                @block.vector
                def _(dve):
                    L = lambda ins: link(dve, ins, "dve_chain")
                    dve.memset(O[:, :, 0:1], -1e38)
                    dve.memset(PN[:, :, 0:1], 0.0)
                    L(dve.memset(QN[:, :, 0:1], 0.0))
                    for s in range(NS):
                        k = s // B
                        ins = dve.tensor_tensor_scan(O[:, s, 1:T + 1], w[:, k:k + 1].to_broadcast([P, T]), K[:, s, :], -1e38,
                                                     ALU.add, ALU.max)
                    ins.then_inc(S["maxima"], 1)
                    dve.wait_ge(S["maxima"], 1)
                    for k in range(KD):
                        ins = dve.scalar_tensor_tensor(half(KEEP, k), half(old(O), k), w[:, k:k + 1], half(new(O), k),
                                                       ALU.add, ALU.subtract)
                    ins.then_inc(S["keep"], 1)
                    for k in range(KD):
                        ins = dve.scalar_tensor_tensor(half(TOP, k), half(K, k), u[:, k:k + 1], half(old(O), k), ALU.add, ALU.max)
                    ins.then_inc(S["top"], 1)
                    dve.wait_ge(S["top"], 1)
                    for k in range(KD):
                        ins = dve.scalar_tensor_tensor(half(NEW, k), half(K, k), u[:, k:k + 1], half(TOP, k), ALU.add, ALU.subtract)
                    ins.then_inc(S["new"], 1)
                    dve.wait_ge(S["keep_exp"], 1)
                    dve.wait_ge(S["key_exp"], 1)
                    for s in range(NS):
                        ins = dve.tensor_tensor_scan(QN[:, s, 1:T + 1], KEEP[:, s, :], EK[:, s, :], 0.0, ALU.mult, ALU.add)
                    L(ins)
                    dve.wait_ge(S["key_values"], 1)
                    for s in range(NS):
                        ins = dve.tensor_tensor_scan(PN[:, s, 1:T + 1], KEEP[:, s, :], EV[:, s, :], 0.0, ALU.mult, ALU.add)
                    ins.then_inc(S["numerators"], 1)
                    dve.wait_ge(S["new_exp"], 1)
                    dve.wait_ge(S["old_exp"], 1)
                    dve.wait_ge(S["numerators"], 1)
                    L(dve.tensor_tensor(KEEP[:], OLD[:], old(QN), ALU.mult))
                    L(dve.tensor_tensor(KEEP[:], KEEP[:], NEW[:], ALU.add))
                    for k in range(KD):
                        dve.reciprocal(half(KEEP, k), half(KEEP, k)).then_inc(S["inverse"], 1)
                    for k in range(KD):
                        dve.wait_ge(S["inverse"], k + 1)
                        dve.wait_ge(S["outputs"], k + 1)
                        dve.tensor_tensor(half(TOP, k), half(EV, k), half(KEEP, k), ALU.mult).then_inc(S["quotients"], 1)
                    for g in range(TT // 2):
                        dve.wait_ge(S["turned"], d["turned"] + g + 1)
                        v = X[:, 2 * g:2 * g + 2, :].rearrange("p t d -> p (t d)")
                        dve.tensor_tensor(v, v, PS[:, g, :], ALU.add)

                @block.gpsimd
                def _(pool):
                    pool.wait_ge(S["maxima"], 1)
                    pool.tensor_tensor(EK[:], K, new(O), ALU.subtract).then_inc(S["keys"], 1)
                    pool.wait_ge(S["top"], 1)
                    pool.tensor_tensor(OLD[:], old(O), TOP[:], ALU.subtract).then_inc(S["old"], 1)
                    pool.wait_ge(S["key_exp"], 1)
                    pool.tensor_tensor(EV[:], EK[:], V, ALU.mult).then_inc(S["key_values"], 1)
                    pool.wait_ge(S["new_exp"], 1)
                    pool.tensor_tensor(NV[:], NEW[:], V, ALU.mult).then_inc(S["new_values"], 1)
                    pool.wait_ge(S["old_exp"], 1)
                    pool.wait_ge(S["numerators"], 1)
                    pool.tensor_tensor(EV[:], OLD[:], old(PN), ALU.mult).then_inc(S["old_values"], 1)
                    pool.wait_ge(S["old_values"], 1)
                    for k in range(KD):
                        pool.tensor_tensor(half(EV, k), half(EV, k), half(NV, k), ALU.add).then_inc(S["outputs"], 1)

                @block.scalar
                def _(act):
                    for ready, a, out_ in (("keep", KEEP, "keep_exp"), ("keys", EK, "key_exp"), ("new", NEW, "new_exp"),
                                           ("old", OLD, "old_exp")):
                        act.wait_ge(S[ready], 1)
                        act.activation(a[:], a[:], ACT.Exp).then_inc(S[out_], 1)

                @block.tensor
                def _(pe):
                    pe.wait_ge(S["quotients"], KD)
                    for g in range(TT // 2):
                        for j in range(2):
                            for k in range(KD):
                                last = pe.transpose(PS[:, g, j * D + k * P:j * D + (k + 1) * P],
                                                    TOP[:, k * B + g, j * P:(j + 1) * P], ident)
                        last.then_inc(S["turned"], 1)
            done["turned"] += TT // 2

    def ternary():
        mats = [wL(x) for x in ("up3", "gate3", "dn3")]
        NPC = 2048 // CH
        pieces = [(j, slice(m * CH, (m + 1) * CH)) for j in range(3) for m in range(NPC)]
        rs = sb("rs", [P, 3 * NPC])
        total = sb("total", [P, 4])
        SC = sb("SC", [P, 4])
        th = sb("th", [P, 2, 4])

        def sums(act):
            act.wait_ge(S["late_in"], 16)
            for n, (j, c) in enumerate(pieces):
                if n:
                    act.wait_ge(S["abs_sums"], n)
                act.activation(PS[:, 7, :], mats[j][:, c], ACT.Abs, accum_out=rs[:, n:n + 1]).then_inc(S["abs_sums"], 1)

        def over_partitions(pe):
            pe.wait_ge(S["abs_sums"], len(pieces))
            pe.matmul(PS[:, 6, 0:len(pieces)], cst("ones"), rs[:], start=True, stop=True).then_inc(S["abs_total"], 1)

        def scales(dve):
            L = lambda ins: link(dve, ins, "dve_chain")
            dve.wait_ge(S["abs_total"], 1)
            L(dve.tensor_reduce(total[:, 0:3], PS[:, 6, 0:len(pieces)].rearrange("p (j m) -> p j m", j=3), AX, ALU.add))
            L(dve.tensor_scalar(SC[:, 0:3], total[:, 0:3], 1.0 / (F3 * D), 1e-8, ALU.mult, ALU.add))
            L(dve.tensor_scalar(th[:, 0, 0:3], SC[:, 0:3], 0.5, None, ALU.mult))
            L(dve.tensor_scalar(th[:, 1, 0:3], SC[:, 0:3], -0.5, None, ALU.mult))

        def replace(dve, scratch, n):
            if n < len(pieces):
                j, c = pieces[n]
                w = mats[j][:, c]
                link(dve, dve.tensor_scalar(scratch, w, th[:, 1, j:j + 1], None, ALU.is_lt), "dve_chain")
                link(dve, dve.scalar_tensor_tensor(w, w, th[:, 0, j:j + 1], scratch, ALU.is_gt, ALU.subtract), "dve_chain")

        return SC, (sums, over_partitions, scales), replace

    load_all()

    def finish(st, pre, rows, **norm):
        layernorm(X, H, pre=pre, rows=rows, **norm)
        st.close()

    def cross16(left):
        hd = 16
        NR = 16 * NSTACK[hd]
        with ExitStack() as cs:
            SQ, SK = (cs.enter_context(nc.sbuf_tensor(x, [P, TT * P // hd, D], BF16)) for x in ("SQX", "SKX"))
            at0 = dict(done)

            def fetch(sp, g, dst, src, order):
                blk = slice(g * 2 * P // hd, (g + 1) * 2 * P // hd)
                fetch_parts(sp, hd, lambda _: dst[:, blk],
                            lambda which, _: src[which, g * 2 * P:(g + 1) * 2 * P, :].rearrange("(a d) c -> d a c", d=hd),
                            order, f"stacked{g}")

            with ExitStack() as ss:
                SPL = ss.enter_context(nc.sbuf_tensor("SPLX", [P, TT // 2, 3, 2, D], BF16))
                REST = CX[:].rearrange("p (g t) d -> p g t d", t=2)

                def send(sp, g, d):
                    if g == 0:
                        fetch(sp, 0, SK, xk_parts, PARTS_K)
                    sp.wait_ge(S["part_l"], d["part_l"] + g + 1)
                    for t in range(2):
                        sp.dma_start(xq_parts[:, (2 * g + t) * P:(2 * g + t + 1) * P, :].rearrange("a p c -> p a c"),
                                     SPL[:, g, :, t]).then_inc(S[f"chunk_out{g}"], 16)
                    if g == 1:
                        sp.wait_ge(S["chunk_out0"], d["chunk_out0"] + 32)
                        fetch(sp, 0, SQ, xq_parts, PARTS_Q)
                    if g == TT // 2 - 1:
                        for n in range(1, TT // 2):
                            sp.wait_ge(S[f"chunk_out{n}"], d[f"chunk_out{n}"] + 32)

                st, pre, rows = left
                layernorm(X, H, pre=pre, rows=rows, split=(SPL, REST, send))
                for g in range(TT // 2):
                    done[f"chunk_out{g}"] += 32
            st.close()

            def rest(sp):
                for g in range(1, TT // 2):
                    fetch(sp, g, SK, xk_parts, PARTS_K)
                    fetch(sp, g, SQ, xq_parts, PARTS_Q)

            def arrivals(bb):
                batches = [bb] if isinstance(bb, int) else range(2, B)
                return [(f"stacked{g}", at0[f"stacked{g}"] + 2 * NR) for g in batches]

            stacked_cross(hd, SQ, SK, (arrivals, rest))
            for g in range(TT // 2):
                done[f"stacked{g}"] += 2 * NR

    def context_parts():
        st = ExitStack()
        SPL = st.enter_context(nc.sbuf_tensor("SPLC", [P, 3, TT, D], BF16))
        REST = st.enter_context(nc.sbuf_tensor("RESTC", [P, TT, D], F32))

        def vector(dve):
            L = lambda ins: link(dve, ins, "dve_chain")
            L(dve.tensor_copy(SPL[:, 0], CX[:]))
            L(dve.tensor_tensor(REST[:], CX[:], SPL[:, 0], ALU.subtract))
            L(dve.tensor_copy(SPL[:, 1], REST[:]))
            dve.tensor_tensor(SPL[:, 2], REST[:], SPL[:, 1], ALU.subtract).then_inc(S["part_l"], 1)

        def sync(sp, d):
            sp.wait_ge(S["part_l"], d["part_l"] + 1)
            for k in range(3):
                sp.dma_start(xk_parts[k].rearrange("(t p) c -> p t c", p=P), SPL[:, k]).then_inc(S["parts_out"], 16)
            sp.wait_ge(S["parts_out"], d["parts_out"] + 48)

        return st, vector, sync

    def layers():
        layernorm(X, H, to_HT, first=True)
        left = self_attention(0, {"q": wA("q0", KD), "qp": wA("qp0", KD), "k": wA("k0", KD), "kp": wA("kp0", KD),
                                  "v": wA("v0", KD), "o": wA("o0", 4)}, 4, 32, D ** -0.5, softcap=50.0,
                              arrived=(S["a_in"], 16), beside=quantise_fp4())
        finish(*left)
        turn_context_and_weights()
        cross_attention(32)
        layernorm(X, H, to_HT)
        up0 = wA("up0", KD)
        dn0 = wA("dn0", 8)
        st, vector, sync = context_parts()
        mlp(F0 // P, up=lambda i, k: up0[:, k, i * P:(i + 1) * P], gate=None, down=lambda i: dn0[:, i, :], mode="gelu",
            bias=vv("b_up0"), load=sync, beside=vector)
        st.close()
        done["part_l"] += 1
        done["parts_out"] += 48
        layernorm(X, H, pre=add_sums())
        finish(*mixing())
        with nc.Block() as block:
            @block.sync
            def _(sp):
                sp.dma_start(WA[:, 0:L_N], wl).then_inc(S["late_in"], 16)
        cross_attention(32, gamma=rv("gamma"))
        layernorm(X, H, to_HT)
        experts1()
        wb_store.close()
        SC, scale_work, replace = ternary()
        layernorm(X, H, to_HT)
        left = stacked_attention(2, {"q": wL("q2", KD), "qp": wL("qp2", KD), "k": wL("k2", KD), "kp": wL("kp2", KD),
                                  "v": wL("v2", KD), "o": wL("o2", KD)}, 2, 8, 8 ** -0.5, arrived=(S["late_in"], 16), extra=scale_work)
        cross16(left)
        layernorm(X, H, to_HT)
        experts2(replace)
        layernorm(X, H, to_HT, pre=add_sums())
        left = stacked_attention(3, {"q": wL("q3", KD), "qp": wL("qp3", KD), "k": wL("k3", KD), "kp": wL("kp3", KD),
                                  "v": wL("v3", KD), "o": wL("o3", KD)}, 2, 16, 0.25)
        finish(*left, dstT=to_HT)
        wkv_scan()
        layernorm(X, H, to_HT)
        up3, gate3, dn3 = wL("up3", KD), wL("gate3", KD), wL("dn3", 8)
        mlp(F3 // P, up=lambda i, k: up3[:, k, i * P:(i + 1) * P], gate=lambda i, k: gate3[:, k, i * P:(i + 1) * P],
            down=lambda i: dn3[:, i, :], mode="silu", scales=SC)
        with nc.Block() as block:
            @block.vector
            def _(dve):
                for g in range(TT // 2):
                    v = X[:, 2 * g:2 * g + 2, :]
                    ps = PS[:, 4 + g, :].rearrange("p (t n) -> p t n", t=2)
                    dve.scalar_tensor_tensor(v, ps, SC[:, 2:3], v, ALU.mult, ALU.add).then_inc(S["x_added"], 1)

            @block.sync
            def _(sp):
                half = TT // 2
                for h in range(2):
                    sp.wait_ge(S["x_added"], done["x_added"] + 2 * (h + 1))
                    sp.dma_start(tok(out)[:, h * half:(h + 1) * half, :], X[:, h * half:(h + 1) * half, :]
                                 ).then_inc(S["out_done"], 16)
                sp.wait_ge(S["out_done"], 32)

    layers()
    es.close()


def blocks(w):
    k = w.shape[0] // P
    return w.reshape(k, P, -1).transpose(1, 0, 2).reshape(P, -1)


def column_of(v):
    return v.reshape(-1, P).T


def swapped(w, hd, paired):
    i = np.arange(w.shape[1])
    h, dd = i // hd, i % hd
    other = dd ^ 1 if paired else (dd + hd // 2) % hd
    return w[:, h * hd + other]


def gqa(wq, wk, wv, wo, hd, group, paired):
    if hd == 32:
        order = [2 * (4 * kb + s) + r for kb in range(2) for r in range(2) for s in range(4)]
        cols = np.concatenate([np.arange(h * hd, (h + 1) * hd) for h in order])
        wq, wo = wq[:, cols], wo[cols]
    else:
        cols = np.concatenate([np.arange(h // group * hd, (h // group + 1) * hd) for h in range(D // hd)])
        wk, wv = wk[:, cols], wv[:, cols]
    return [blocks(a) for a in (wq, swapped(wq, hd, paired), wk, swapped(wk, hd, paired), wv, wo)]


def layout(i):
    n = {k: np.asarray(v) for k, v in i.items()}
    cat = lambda xs: np.ascontiguousarray(np.concatenate(xs, axis=1))
    g0 = gqa(n["L0_attn_Wq"], n["L0_attn_Wk"], n["L0_attn_Wv"], n["L0_attn_Wo"], 32, 2, False)
    wa = cat(g0 + [blocks(n["L0_ffn_up_kernel"].T), blocks(n["L0_ffn_down_kernel"].T)]
             + [blocks(n["L1_attn_" + k].T) for k in ("tm_Wr", "tm_Wk", "tm_Wv", "tm_Wout", "cm_Wr", "cm_Wk", "cm_Wv")])
    f = lambda k: n["L1_ffn_" + k]
    wb = cat([blocks(f("down_w")), blocks(f("up_w")), blocks(f("router_w")), f("shared_w1"), f("shared_w2"),
              blocks(f("core_w"))] + [f(f"e{e}_w1") for e in range(E1)] + [blocks(f(f"e{e}_w2")) for e in range(E1)])
    g2 = gqa(n["L2_attn_wq"], n["L2_attn_wk"], n["L2_attn_wv"], n["L2_attn_wo"], 8, 4, True)
    g3 = gqa(n["L3_attn_wq"], n["L3_attn_wk"], n["L3_attn_wv"], n["L3_attn_wo"], 16, 4, False)
    router2 = np.concatenate([n["L2_ffn_router_w"].T, n["L2_ffn_sh_gate_w"]], axis=1)
    wl = cat(g2 + g3 + [blocks(n["L3_ffn_W_up"].T), blocks(n["L3_ffn_W_gate"].T), blocks(n["L3_ffn_W_down"].T),
                        blocks(router2)])
    pad = NI2 * P - E2 * I2 - ISH
    wide = lambda w, s: np.concatenate([w.transpose(1, 0, 2).reshape(D, -1), s, np.zeros((D, pad), np.float32)], axis=1)
    gate, up = wide(n["L2_ffn_w_gate"], n["L2_ffn_sh_gate"]), wide(n["L2_ffn_w_up"], n["L2_ffn_sh_up"])
    down = np.concatenate([n["L2_ffn_w_down"].reshape(-1, D), n["L2_ffn_sh_down"], np.zeros((pad, D), np.float32)])
    halves = lambda w: w.reshape(KD, P, NI2, P).transpose(2, 1, 0, 3).reshape(NI2, P, KD * P)
    w2f = np.ascontiguousarray(np.concatenate([halves(gate), halves(up), down.reshape(NI2, P, D)], axis=2))
    a = lambda k: column_of(n["L1_attn_" + k])
    vec = cat([column_of(n["L0_ffn_up_bias"])] + [a(k) for k in ("ln1_g", "ln1_b", "ln2_g", "ln2_b", "tm_u", "tm_mu_r",
              "tm_mu_k", "tm_mu_v", "cm_mu_r", "cm_mu_k")]
              + [column_of(f(k)) for k in ("down_b", "shared_b1", "shared_b2")] + [column_of(f(f"e{e}_b1")) for e in range(E1)]
              + [column_of(f(f"e{e}_b2")) for e in range(E1)] + [column_of(n["L3_xattn_w"]), column_of(n["L3_xattn_u"])])
    rowv = cat([n["L0_ffn_down_bias"][None], f("up_b")[None], f("core_b")[None], f("router_b")[None],
                n["L1_xattn_gamma"].reshape(1, 1)])
    return {"x": n["x"], "ctx": n["ctx_2048"], "wa": wa, "wb": wb, "wl": wl, "w2f": w2f, "vec": vec, "rowv": rowv,
            "const": shape_constants()}


def kernel(**inputs):
    import concourse.bacc as bacc
    from concourse.bass_utils import run_bass_kernel_spmd

    nc = bacc.Bacc("TRN2", target_bir_lowering=False, num_devices=1)
    arrays = layout(inputs)
    aps = {k: nc.dram_tensor(k + "_in", a.shape, mybir.dt.from_np(a.dtype), kind="ExternalInput").ap()
           for k, a in arrays.items()}
    out = nc.dram_tensor("out", (B, T, D), F32, kind="ExternalOutput").ap()
    build_decoder(nc, out=out, **aps)
    r = run_bass_kernel_spmd(nc, [{k + "_in": a for k, a in arrays.items()}], core_ids=[0])
    return r.results[0]["out"]
```
